# Optimizing a Trainium2 kernel written in Bass

```python
import numpy as np
import jax
import jax.numpy as jnp

def _softmax(x, axis=-1):
    return jax.nn.softmax(x, axis=axis)

def _gelu(x):
    return jax.nn.gelu(x, approximate=True)

def _silu(x):
    return jax.nn.silu(x)

def _sigmoid(x):
    return jax.nn.sigmoid(x)

def _layernorm(x, axis=-1, eps=1e-05):
    m = jnp.mean(x, axis=axis, keepdims=True)
    v = jnp.var(x, axis=axis, keepdims=True)
    return (x - m) / jnp.sqrt(v + eps)

def _scatter_add(tgt, idx, src, axis=0):
    return tgt.at[idx].add(src)

def _segment_sum(src, seg, n):
    return jax.ops.segment_sum(src, seg, n)
kernel_name = 'mk_decoder_postln_d2_seqx_r4_cba973'

def setup_inputs(seed: int=0):
    np.random.seed(seed)
    _w = jnp.asarray

    def _rec_inputs():
        import jax
        import jax.numpy as jnp
        _rk = jax.random.key(seed)
        x = 7.22e-05 + 1 * jax.random.normal(jax.random.fold_in(_rk, 1), (8, 512, 256), jnp.float32)
        _lenS = 512 - jax.random.randint(jax.random.fold_in(_rk, 7), (8,), 0, max(1, 512 // 4) + 1, jnp.int32)
        _lenS2 = 512 - jax.random.randint(jax.random.fold_in(_rk, 8), (8,), 0, max(1, 512 // 4) + 1, jnp.int32)
        _ctx_768P = jax.random.normal(jax.random.fold_in(_rk, 11), (8, 16, 192), jnp.float32)
        _ctx_768c = jax.random.dirichlet(jax.random.fold_in(_rk, 511), 0.3 * jnp.ones((16,), jnp.float32), (8, 512))
        _ctx_768t = jnp.einsum('bsk,bkd->bsd', _ctx_768c, _ctx_768P)
        _ctx_768t = _ctx_768t * jax.lax.rsqrt(jnp.mean(jnp.square(_ctx_768t)) + 1e-12) * 0.953939
        ctx_768 = 2.09791e-05 + 1.00001 * (_ctx_768t + 0.3 * jax.random.normal(jax.random.fold_in(_rk, 611), (8, 512, 192), jnp.float32))
        return (x, ctx_768)
    x, ctx_768 = _rec_inputs()

    def _L0_attn_setup():
        import jax, jax.numpy as jnp
        import numpy as np
        D_MODEL = 256
        N_HEADS = 16
        D_HEAD = 64
        GROUP_SIZE = 2
        N_GROUPS = N_HEADS // GROUP_SIZE
        key = jax.random.key(seed)
        k1, k2, k3, k4, k5 = jax.random.split(key, 5)

        def xavier(k, shape):
            fan_in, fan_out = (shape[0], int(np.prod(shape[1:])))
            bound = float(np.sqrt(6.0 / (fan_in + fan_out)))
            return jax.random.uniform(k, shape, jnp.float32, -bound, bound)
        return {'resid': jax.random.normal(k1, (2, 512, D_MODEL), jnp.float32), 'W_Q': xavier(k2, (D_MODEL, N_HEADS, D_HEAD)), 'W_K': xavier(k3, (D_MODEL, N_GROUPS, D_HEAD)), 'W_V': xavier(k4, (D_MODEL, N_GROUPS, D_HEAD)), 'W_out': xavier(k5, (D_HEAD, N_HEADS, D_MODEL)), 'b_out': jnp.zeros((D_MODEL,), jnp.float32)}
    _L0_attn_all = _L0_attn_setup()
    _L0_attn_in = {k: v for k, v in _L0_attn_all.items() if k in ('W_Q', 'W_K', 'W_V', 'W_out', 'b_out')}
    del _L0_attn_all

    def _L0_xattn_setup():
        import jax, jax.numpy as jnp
        import numpy as np
        HEADS = 8
        DIM_HEAD = 64
        SCALE = DIM_HEAD ** (-0.5)
        key = jax.random.key(seed)
        ks = jax.random.split(key, 7)
        b, n, m = (4, 512, 256)
        qd, cd, inner = (256, 192, HEADS * DIM_HEAD)
        s = lambda fan_in: 1.0 / np.sqrt(fan_in)
        return {'x': jax.random.normal(ks[0], (b, n, qd), jnp.float32), 'context': jax.random.normal(ks[1], (b, m, cd), jnp.float32), 'Wq': jax.random.normal(ks[2], (qd, inner), jnp.float32) * s(qd), 'Wk': jax.random.normal(ks[3], (cd, inner), jnp.float32) * s(cd), 'Wv': jax.random.normal(ks[4], (cd, inner), jnp.float32) * s(cd), 'Wout': jax.random.normal(ks[5], (inner, qd), jnp.float32) * s(inner), 'bout': jax.random.normal(ks[6], (qd,), jnp.float32) * 0.01}
    _L0_xattn_all = _L0_xattn_setup()
    _L0_xattn_in = {k: v for k, v in _L0_xattn_all.items() if k in ('Wq', 'Wk', 'Wv', 'Wout', 'bout')}
    del _L0_xattn_all

    def _L0_ffn_setup():
        import jax, jax.numpy as jnp
        import numpy as np
        HIDDEN = 256
        HEAD_DIM = 64
        N_EXPERTS = 16
        MIN_EXPERTS = 2
        B, T = (4, 512)

        def _normalize(x, axis):
            n = jnp.sqrt(jnp.sum(x * x, axis=axis, keepdims=True))
            return x / jnp.maximum(n, 1e-12)

        def _ste(x):
            hard = jax.lax.stop_gradient((x > 0).astype(x.dtype))
            return hard + x - jax.lax.stop_gradient(x)

        def _gating(hidden_states, sim_matrix, gates):
            b, t, c = hidden_states.shape
            flat = hidden_states.reshape(b * t, c)
            logits = _normalize(flat, -1) @ _normalize(sim_matrix, 0) - jax.nn.sigmoid(gates)
            gated = jax.nn.relu(logits)
            mask = _ste(gated)
            inactive = jnp.sum(mask, axis=1) == 0
            _, fb_idx = jax.lax.top_k(logits, MIN_EXPERTS)
            fb = jnp.zeros_like(mask).at[jnp.arange(b * t)[:, None], fb_idx].set(1.0)
            fb_applied = inactive[:, None] & (fb > 0)
            mask = jnp.where(fb_applied, 1.0, mask)
            masked_logits = jnp.where(mask > 0, gated, -jnp.inf)
            return jax.nn.softmax(masked_logits, axis=-1).reshape(b, t, -1)
        key = jax.random.key(seed)
        ks = jax.random.split(key, 6)
        xav_qkv = float(np.sqrt(6.0 / (HIDDEN + HEAD_DIM)))
        return {'hidden_states': jax.random.normal(ks[0], (B, T, HIDDEN), dtype=jnp.float32), 'sim_matrix': jax.random.normal(ks[1], (HIDDEN, N_EXPERTS), dtype=jnp.float32), 'gates': jnp.zeros((N_EXPERTS,), dtype=jnp.float32), 'q_proj': jax.random.uniform(ks[2], (N_EXPERTS, HIDDEN, HEAD_DIM), jnp.float32, -xav_qkv, xav_qkv), 'k_proj': jax.random.uniform(ks[3], (N_EXPERTS, HIDDEN, HEAD_DIM), jnp.float32, -xav_qkv, xav_qkv), 'v_proj': jax.random.uniform(ks[4], (N_EXPERTS, HIDDEN, HEAD_DIM), jnp.float32, -xav_qkv, xav_qkv), 'o_proj': jax.random.uniform(ks[5], (N_EXPERTS, HEAD_DIM, HIDDEN), jnp.float32, -xav_qkv, xav_qkv)}
    _L0_ffn_all = _L0_ffn_setup()
    _L0_ffn_in = {k: v for k, v in _L0_ffn_all.items() if k in ('sim_matrix', 'gates', 'q_proj', 'k_proj', 'v_proj', 'o_proj')}
    del _L0_ffn_all

    def _L1_attn_setup():
        import jax, jax.numpy as jnp
        import numpy as np
        B, T, D = (1, 512, 256)
        H = 16
        HD = D // H
        WINDOW = 128
        NEG = -10000000000.0

        def _mask(t):
            i = jnp.arange(t)[:, None]
            j = jnp.arange(t)[None, :]
            return ((j <= i) & (j >= i - WINDOW)).astype(jnp.float32)

        def _genetic_fitness(g):
            t = g.shape[2]
            dot = jnp.einsum('bhid,bhjd->bhij', g, g)
            nrm = jnp.linalg.norm(g, axis=-1)
            corr = dot / (nrm[..., :, None] * nrm[..., None, :] + 1e-08)
            corr = jnp.nan_to_num(corr, nan=0.0, posinf=1.0, neginf=-1.0)
            m = _mask(t)[None, None]
            corr = corr * m
            corr = (corr + 1.0) / 2.0
            gene_means = jnp.mean(corr, axis=3)
            denom = gene_means + 0.5
            sum_inv = jnp.sum(1.0 / denom, axis=2, keepdims=True)
            gene_fitness = 1.0 / (denom * sum_inv)
            weighted = corr * gene_fitness[..., None]
            masked = weighted * m + (1.0 - m) * NEG
            return jax.nn.softmax(masked, axis=-1)
        key = jax.random.key(seed)
        ks = jax.random.split(key, 7)
        s = 1.0 / np.sqrt(D)
        return {'x': jax.random.normal(ks[0], (B, T, D), jnp.float32), 'Wg': jax.random.normal(ks[1], (D, D), jnp.float32) * s, 'bg': jax.random.normal(ks[2], (D,), jnp.float32) * 0.01, 'Wv': jax.random.normal(ks[3], (D, D), jnp.float32) * s, 'bv': jax.random.normal(ks[4], (D,), jnp.float32) * 0.01, 'Wo': jax.random.normal(ks[5], (D, D), jnp.float32) * s, 'bo': jax.random.normal(ks[6], (D,), jnp.float32) * 0.01}
    _L1_attn_all = _L1_attn_setup()
    _L1_attn_in = {k: v for k, v in _L1_attn_all.items() if k in ('Wg', 'bg', 'Wv', 'bv', 'Wo', 'bo')}
    del _L1_attn_all

    def _L1_xattn_setup():
        import jax, jax.numpy as jnp
        import numpy as np
        IMAGE_DIM = 256
        TEXT_DIM = 192
        NUM_HEADS = 16
        HEAD_DIM = IMAGE_DIM // NUM_HEADS
        key = jax.random.key(seed)
        ks = jax.random.split(key, 14)
        B, N, M = (4, 1024, 128)
        s_img = 1.0 / np.sqrt(IMAGE_DIM)
        s_txt = 1.0 / np.sqrt(TEXT_DIM)
        s_ff = 1.0 / np.sqrt(2 * IMAGE_DIM)
        return {'x': jax.random.normal(ks[0], (B, N, IMAGE_DIM), jnp.float32), 'y': jax.random.normal(ks[1], (B, M, TEXT_DIM), jnp.float32), 'Wq': jax.random.normal(ks[2], (IMAGE_DIM, IMAGE_DIM), jnp.float32) * s_img, 'bq': jax.random.normal(ks[3], (IMAGE_DIM,), jnp.float32) * s_img, 'Wk': jax.random.normal(ks[4], (TEXT_DIM, IMAGE_DIM), jnp.float32) * s_txt, 'bk': jax.random.normal(ks[5], (IMAGE_DIM,), jnp.float32) * s_txt, 'Wv': jax.random.normal(ks[6], (TEXT_DIM, IMAGE_DIM), jnp.float32) * s_txt, 'bv': jax.random.normal(ks[7], (IMAGE_DIM,), jnp.float32) * s_txt, 'W1': jax.random.normal(ks[8], (IMAGE_DIM, 2 * IMAGE_DIM), jnp.float32) * s_img, 'b1': jax.random.normal(ks[9], (2 * IMAGE_DIM,), jnp.float32) * s_img, 'W2': jax.random.normal(ks[10], (2 * IMAGE_DIM, IMAGE_DIM), jnp.float32) * s_ff, 'b2': jax.random.normal(ks[11], (IMAGE_DIM,), jnp.float32) * s_ff}
    _L1_xattn_all = _L1_xattn_setup()
    _L1_xattn_in = {k: v for k, v in _L1_xattn_all.items() if k in ('Wq', 'bq', 'Wk', 'bk', 'Wv', 'bv', 'W1', 'b1', 'W2', 'b2')}
    del _L1_xattn_all

    def _L1_ffn_setup():
        import jax, jax.numpy as jnp
        import numpy as np
        D = 256
        H = 192
        E = 8
        K = 2
        NS = 2
        ROUTE_SCALE = 1.0

        def _gated_mlp(x, w1, w2):
            h = x @ w1.T
            y, g = jnp.split(h, 2, axis=-1)
            return y * jax.nn.silu(g) @ w2.T
        key = jax.random.key(seed)
        ks = jax.random.split(key, 6)
        s = 0.02
        return {'x': jax.random.normal(ks[0], (2, 256, D), jnp.float32), 'gate_w': jax.random.normal(ks[1], (E, D), jnp.float32) * s, 'W1': jax.random.normal(ks[2], (E, 2 * H, D), jnp.float32) * s, 'W2': jax.random.normal(ks[3], (E, D, H), jnp.float32) * s, 'Ws1': jax.random.normal(ks[4], (2 * NS * H, D), jnp.float32) * s, 'Ws2': jax.random.normal(ks[5], (D, NS * H), jnp.float32) * s}
    _L1_ffn_all = _L1_ffn_setup()
    _L1_ffn_in = {k: v for k, v in _L1_ffn_all.items() if k in ('gate_w', 'W1', 'W2', 'Ws1', 'Ws2')}
    del _L1_ffn_all
    return {'x': x, 'ctx_768': ctx_768, 'L0_attn_W_Q': _L0_attn_in['W_Q'], 'L0_attn_W_K': _L0_attn_in['W_K'], 'L0_attn_W_V': _L0_attn_in['W_V'], 'L0_attn_W_out': _L0_attn_in['W_out'], 'L0_attn_b_out': _L0_attn_in['b_out'], 'L0_xattn_Wq': _L0_xattn_in['Wq'], 'L0_xattn_Wk': _L0_xattn_in['Wk'], 'L0_xattn_Wv': _L0_xattn_in['Wv'], 'L0_xattn_Wout': _L0_xattn_in['Wout'], 'L0_xattn_bout': _L0_xattn_in['bout'], 'L0_ffn_sim_matrix': _L0_ffn_in['sim_matrix'], 'L0_ffn_gates': _L0_ffn_in['gates'], 'L0_ffn_q_proj': _L0_ffn_in['q_proj'], 'L0_ffn_k_proj': _L0_ffn_in['k_proj'], 'L0_ffn_v_proj': _L0_ffn_in['v_proj'], 'L0_ffn_o_proj': _L0_ffn_in['o_proj'], 'L1_attn_Wg': _L1_attn_in['Wg'], 'L1_attn_bg': _L1_attn_in['bg'], 'L1_attn_Wv': _L1_attn_in['Wv'], 'L1_attn_bv': _L1_attn_in['bv'], 'L1_attn_Wo': _L1_attn_in['Wo'], 'L1_attn_bo': _L1_attn_in['bo'], 'L1_xattn_Wq': _L1_xattn_in['Wq'], 'L1_xattn_bq': _L1_xattn_in['bq'], 'L1_xattn_Wk': _L1_xattn_in['Wk'], 'L1_xattn_bk': _L1_xattn_in['bk'], 'L1_xattn_Wv': _L1_xattn_in['Wv'], 'L1_xattn_bv': _L1_xattn_in['bv'], 'L1_xattn_W1': _L1_xattn_in['W1'], 'L1_xattn_b1': _L1_xattn_in['b1'], 'L1_xattn_W2': _L1_xattn_in['W2'], 'L1_xattn_b2': _L1_xattn_in['b2'], 'L1_ffn_gate_w': _L1_ffn_in['gate_w'], 'L1_ffn_W1': _L1_ffn_in['W1'], 'L1_ffn_W2': _L1_ffn_in['W2'], 'L1_ffn_Ws1': _L1_ffn_in['Ws1'], 'L1_ffn_Ws2': _L1_ffn_in['Ws2']}

def reference(x, ctx_768, L0_attn_W_Q, L0_attn_W_K, L0_attn_W_V, L0_attn_W_out, L0_attn_b_out, L0_xattn_Wq, L0_xattn_Wk, L0_xattn_Wv, L0_xattn_Wout, L0_xattn_bout, L0_ffn_sim_matrix, L0_ffn_gates, L0_ffn_q_proj, L0_ffn_k_proj, L0_ffn_v_proj, L0_ffn_o_proj, L1_attn_Wg, L1_attn_bg, L1_attn_Wv, L1_attn_bv, L1_attn_Wo, L1_attn_bo, L1_xattn_Wq, L1_xattn_bq, L1_xattn_Wk, L1_xattn_bk, L1_xattn_Wv, L1_xattn_bv, L1_xattn_W1, L1_xattn_b1, L1_xattn_W2, L1_xattn_b2, L1_ffn_gate_w, L1_ffn_W1, L1_ffn_W2, L1_ffn_Ws1, L1_ffn_Ws2):
    import jax
    import jax.numpy as jnp

    def _L0_attn_ref(resid, W_Q, W_K, W_V, W_out, b_out):
        import jax, jax.numpy as jnp
        import numpy as np
        D_MODEL = 256
        N_HEADS = 16
        D_HEAD = 64
        GROUP_SIZE = 2
        N_GROUPS = N_HEADS // GROUP_SIZE
        batch, seq, _ = resid.shape
        q = jnp.einsum('bsd,dhe->bshe', resid, W_Q)
        q = q.reshape(batch, seq, N_GROUPS, GROUP_SIZE, D_HEAD)
        k = jnp.einsum('bsd,dge->bsge', resid, W_K)
        v = jnp.einsum('bsd,dge->bsge', resid, W_V)
        scores = jnp.einsum('bqgre,bkge->bgrqk', q, k) / jnp.sqrt(jnp.float32(D_HEAD))
        causal_mask = jnp.triu(jnp.ones((seq, seq), bool), k=1)
        scores = jnp.where(causal_mask, jnp.float32(-1000000.0), scores)
        probs = jax.nn.softmax(scores, axis=-1)
        z = jnp.einsum('bgrqk,bkge->bqgre', probs, v)
        z = z.reshape(batch, seq, N_HEADS, D_HEAD)
        out = jnp.einsum('bshe,ehd->bsd', z, W_out) + b_out
        return out

    def _L0_xattn_ref(x, context, Wq, Wk, Wv, Wout, bout):
        import jax, jax.numpy as jnp
        import numpy as np
        HEADS = 8
        DIM_HEAD = 64
        SCALE = DIM_HEAD ** (-0.5)
        b, n, _ = x.shape
        m = context.shape[1]
        q = (x @ Wq).reshape(b, n, HEADS, DIM_HEAD)
        k = (context @ Wk).reshape(b, m, HEADS, DIM_HEAD)
        v = (context @ Wv).reshape(b, m, HEADS, DIM_HEAD)
        sim = jnp.einsum('bihd,bjhd->bhij', q, k) * SCALE
        attn = jax.nn.softmax(sim, axis=-1)
        out = jnp.einsum('bhij,bjhd->bihd', attn, v).reshape(b, n, HEADS * DIM_HEAD)
        return out @ Wout + bout

    def _L0_ffn_ref(hidden_states, sim_matrix, gates, q_proj, k_proj, v_proj, o_proj):
        import jax, jax.numpy as jnp
        import numpy as np
        HIDDEN = 256
        HEAD_DIM = 64
        N_EXPERTS = 16
        MIN_EXPERTS = 2
        B, T = (4, 512)

        def _normalize(x, axis):
            n = jnp.sqrt(jnp.sum(x * x, axis=axis, keepdims=True))
            return x / jnp.maximum(n, 1e-12)

        def _ste(x):
            hard = jax.lax.stop_gradient((x > 0).astype(x.dtype))
            return hard + x - jax.lax.stop_gradient(x)

        def _gating(hidden_states, sim_matrix, gates):
            b, t, c = hidden_states.shape
            flat = hidden_states.reshape(b * t, c)
            logits = _normalize(flat, -1) @ _normalize(sim_matrix, 0) - jax.nn.sigmoid(gates)
            gated = jax.nn.relu(logits)
            mask = _ste(gated)
            inactive = jnp.sum(mask, axis=1) == 0
            _, fb_idx = jax.lax.top_k(logits, MIN_EXPERTS)
            fb = jnp.zeros_like(mask).at[jnp.arange(b * t)[:, None], fb_idx].set(1.0)
            fb_applied = inactive[:, None] & (fb > 0)
            mask = jnp.where(fb_applied, 1.0, mask)
            masked_logits = jnp.where(mask > 0, gated, -jnp.inf)
            return jax.nn.softmax(masked_logits, axis=-1).reshape(b, t, -1)
        b, t, c = hidden_states.shape
        rw = _gating(hidden_states, sim_matrix, gates)
        q = jnp.einsum('bte,bted->btd', rw, jnp.einsum('btc,ecd->bted', hidden_states, q_proj))
        k = jnp.einsum('bte,bted->btd', rw, jnp.einsum('btc,ecd->bted', hidden_states, k_proj))
        v = jnp.einsum('bte,bted->btd', rw, jnp.einsum('btc,ecd->bted', hidden_states, v_proj))
        scale = 1.0 / jnp.sqrt(jnp.asarray(HEAD_DIM, dtype=q.dtype))
        scores = jnp.einsum('bqd,bkd->bqk', q, k) * scale
        causal = jnp.tril(jnp.ones((t, t), dtype=bool))
        scores = jnp.where(causal, scores, -jnp.inf)
        attn = jnp.einsum('bqk,bkd->bqd', jax.nn.softmax(scores, axis=-1), v)
        mixed = attn[:, :, None, :] * rw[..., None]
        return jnp.einsum('bted,edc->btc', mixed, o_proj)

    def _L1_attn_ref(x, Wg, bg, Wv, bv, Wo, bo):
        import jax, jax.numpy as jnp
        import numpy as np
        B, T, D = (1, 512, 256)
        H = 16
        HD = D // H
        WINDOW = 128
        NEG = -10000000000.0

        def _mask(t):
            i = jnp.arange(t)[:, None]
            j = jnp.arange(t)[None, :]
            return ((j <= i) & (j >= i - WINDOW)).astype(jnp.float32)

        def _genetic_fitness(g):
            t = g.shape[2]
            dot = jnp.einsum('bhid,bhjd->bhij', g, g)
            nrm = jnp.linalg.norm(g, axis=-1)
            corr = dot / (nrm[..., :, None] * nrm[..., None, :] + 1e-08)
            corr = jnp.nan_to_num(corr, nan=0.0, posinf=1.0, neginf=-1.0)
            m = _mask(t)[None, None]
            corr = corr * m
            corr = (corr + 1.0) / 2.0
            gene_means = jnp.mean(corr, axis=3)
            denom = gene_means + 0.5
            sum_inv = jnp.sum(1.0 / denom, axis=2, keepdims=True)
            gene_fitness = 1.0 / (denom * sum_inv)
            weighted = corr * gene_fitness[..., None]
            masked = weighted * m + (1.0 - m) * NEG
            return jax.nn.softmax(masked, axis=-1)
        b, t, d = x.shape
        g = x @ Wg.T + bg
        v = x @ Wv.T + bv
        g = g.reshape(b, t, H, HD).transpose(0, 2, 1, 3)
        v = v.reshape(b, t, H, HD).transpose(0, 2, 1, 3)
        attn = _genetic_fitness(g)
        out = jnp.einsum('bhij,bhjd->bhid', attn, v)
        out = out.transpose(0, 2, 1, 3).reshape(b, t, d)
        return out @ Wo.T + bo

    def _L1_xattn_ref(x, y, Wq, bq, Wk, bk, Wv, bv, W1, b1, W2, b2):
        import jax, jax.numpy as jnp
        import numpy as np
        IMAGE_DIM = 256
        TEXT_DIM = 192
        NUM_HEADS = 16
        HEAD_DIM = IMAGE_DIM // NUM_HEADS
        B, N, _ = x.shape
        M = y.shape[1]
        q = (x @ Wq + bq).reshape(B, N, NUM_HEADS, HEAD_DIM)
        k = (y @ Wk + bk).reshape(B, M, NUM_HEADS, HEAD_DIM)
        v = (y @ Wv + bv).reshape(B, M, NUM_HEADS, HEAD_DIM)
        scale = 1.0 / np.sqrt(HEAD_DIM)
        scores = jnp.einsum('bnhd,bmhd->bhnm', q, k) * scale
        attn = jax.nn.softmax(scores, axis=-1)
        out = jnp.einsum('bhnm,bmhd->bnhd', attn, v).reshape(B, N, IMAGE_DIM)
        h = jax.nn.relu(out @ W1 + b1)
        return h @ W2 + b2

    def _L1_ffn_ref(x, gate_w, W1, W2, Ws1, Ws2):
        import jax, jax.numpy as jnp
        import numpy as np
        D = 256
        H = 192
        E = 8
        K = 2
        NS = 2
        ROUTE_SCALE = 1.0

        def _gated_mlp(x, w1, w2):
            h = x @ w1.T
            y, g = jnp.split(h, 2, axis=-1)
            return y * jax.nn.silu(g) @ w2.T
        x_shape = x.shape
        xf = x.reshape(-1, D)
        T = xf.shape[0]
        scores = jax.nn.softmax((xf @ gate_w.T).astype(jnp.float32), axis=-1)
        top_vals, top_idx = jax.lax.top_k(scores, K)
        weights = (top_vals * ROUTE_SCALE).astype(x.dtype)
        w_dense = jnp.zeros((T, E), x.dtype).at[jnp.arange(T)[:, None], top_idx].set(weights)
        h = jnp.einsum('td,ehd->teh', xf, W1)
        y, g = jnp.split(h, 2, axis=-1)
        eo = jnp.einsum('teh,edh->ted', y * jax.nn.silu(g), W2)
        z = jnp.einsum('te,ted->td', w_dense, eo)
        z = z + _gated_mlp(xf, Ws1, Ws2)
        return z.reshape(x_shape)
    x = _layernorm(x + _L0_attn_ref(x, L0_attn_W_Q, L0_attn_W_K, L0_attn_W_V, L0_attn_W_out, L0_attn_b_out), axis=-1)
    x = _layernorm(x + _L0_xattn_ref(x, ctx_768, L0_xattn_Wq, L0_xattn_Wk, L0_xattn_Wv, L0_xattn_Wout, L0_xattn_bout), axis=-1)
    x = _layernorm(x + _L0_ffn_ref(x, L0_ffn_sim_matrix, L0_ffn_gates, L0_ffn_q_proj, L0_ffn_k_proj, L0_ffn_v_proj, L0_ffn_o_proj), axis=-1)
    x = _layernorm(x + _L1_attn_ref(x, L1_attn_Wg, L1_attn_bg, L1_attn_Wv, L1_attn_bv, L1_attn_Wo, L1_attn_bo), axis=-1)
    x = _layernorm(x + _L1_xattn_ref(x, ctx_768, L1_xattn_Wq, L1_xattn_bq, L1_xattn_Wk, L1_xattn_bk, L1_xattn_Wv, L1_xattn_bv, L1_xattn_W1, L1_xattn_b1, L1_xattn_W2, L1_xattn_b2), axis=-1)
    x = _layernorm(x + _L1_ffn_ref(x, L1_ffn_gate_w, L1_ffn_W1, L1_ffn_W2, L1_ffn_Ws1, L1_ffn_Ws2), axis=-1)
    return x

_drawn_inputs = setup_inputs


def setup_inputs(seed=0):
    import zlib

    import numpy as np

    out = dict(_drawn_inputs(seed))
    spreads = {'L0_attn_b_out': (0.0, 0.1), 'L0_ffn_gates': (0.0, 0.1)}
    factors = {'L0_xattn_bout': 3.51,
     'L1_attn_Wg': 8.0,
     'L1_attn_bg': 8.0,
     'L1_attn_bv': 6.734,
     'L1_attn_bo': 6.379,
     'L1_xattn_bq': 6.965,
     'L1_xattn_bk': 8.0,
     'L1_ffn_gate_w': 8.0,
     'L1_ffn_W1': 8.0,
     'L1_ffn_W2': 8.0,
     'L1_ffn_Ws1': 2.744,
     'L1_ffn_Ws2': 2.759}
    for name, (base, spread) in spreads.items():
        noise = np.random.default_rng([zlib.crc32(name.encode()), seed]).standard_normal(out[name].shape)
        drawn = base * np.exp(spread * noise) if base else spread * noise
        out[name] = jnp.asarray(drawn.astype(out[name].dtype))
    for name, factor in factors.items():
        out[name] = (out[name] * factor).astype(out[name].dtype)
    return out
```

```python
from contextlib import ExitStack

import concourse.bass as bass
from concourse import mybir

F32 = mybir.dt.float32
BF16 = mybir.dt.bfloat16
U32 = mybir.dt.uint32
ALU = mybir.AluOpType
ACT = mybir.ActivationFunctionType
AX = mybir.AxisListType.X

P = 128
T = 512
D = 256
QT = T // P
KT = D // P
LN_EPS = 1e-5
S_BANKS, P_SLOTS = 3, 4
T_LAG, PV_LAG = 2, 3


def at(b, per, k):
    return b * per + max(k, 0)


class Names:
    pass




def apart(eng, passed):
    eng.sem_inc(passed, 1)


def sp_stream(nc, sp, L, NB):

    def load_tokens(b, first=False):
        if not first:
            sp.wait_ge(L.item_ready[0], at(b, L.per[0], 0) - L.per[0] + 1)
            sp.wait_ge(L.item_ready[1], at(b, L.per[1], 0) - L.per[1] + 1)
            apart(sp, L.passed["sp"])
            if L.extra_tokens_reader is not None:
                sp.wait_ge(L.extra_tokens_reader, b * L.extra_tokens_per)
        nc.sync.dma_start(L.tokens, L.x_in(b)).then_inc(L.tokens_loaded, 16)

    def load_context(b, first=False):
        if not first:
            for e in range(2):
                sp.wait_ge(L.item_ready[e], b * L.per[e])
        nc.sync.dma_start(L.context, L.ctx_in(b)).then_inc(L.context_loaded, 16)

    def load_residual(b, first=False):
        if not first:
            sp.wait_ge(L.y_added, b * QT)
            apart(sp, L.passed["sp"])
        nc.sync.dma_start(L.residual, L.x_in(b)).then_inc(L.residual_loaded, 16)

    def store(b):
        sp.wait_ge(L.normed, (b + 1) * QT)
        apart(sp, L.passed["sp"])
        nc.sync.dma_start(L.x_out(b), L.result).then_inc(L.stored, 16)

    load_tokens(0, True)
    if L.ctx_in is not None:
        load_context(0, True)
    load_residual(0, True)
    L.load_next_weights(sp)
    with nc.Fori(0, NB - 1, engines=[mybir.EngineType.SP]) as b:
        load_tokens(b + 1)
        if L.ctx_in is not None:
            load_context(b + 1)
        store(b)
        load_residual(b + 1)
    store(NB - 1)
    sp.wait_ge(L.stored, 16 * NB)


def pe_transpose_tokens(nc, pe, L, b, first):
    pe.wait_ge(L.tokens_loaded, 16 * (b + 1))
    if not first:
        pe.wait_ge(L.y_added, QT * (b - 1))
    for k in range(KT):
        pe.wait_ge(L.item_copied[k % 2], at(b, L.per[k % 2], 0))
        for t in range(QT):
            last = nc.tensor.transpose(L.J[k % 2][:, t * P:(t + 1) * P], L.tokens[:, t, k * P:(k + 1) * P], L.ident)
        last.then_inc(L.item_ready[k % 2], 1)


def pe_item(nc, pe, L, b, n, out, parts):
    e = n % 2
    pe.wait_ge(L.item_copied[e], at(b, L.per[e], n // 2))
    for i, (w, x) in enumerate(parts):
        last = nc.tensor.matmul(out, w, x, start=(i == 0), stop=(i == len(parts) - 1))
    last.then_inc(L.item_ready[e], 1)


def wait_item(eng, L, b, n):
    eng.wait_ge(L.item_ready[n % 2], at(b, L.per[n % 2], n // 2 + 1))


def wait_items_copied(eng, L, b, n):
    for e in range(2):
        eng.wait_ge(L.item_copied[e], at(b, L.per[e], (n - e) // 2 + 1))


def wait_banks_free(eng, L, rows):
    for e in range(2):
        eng.wait_ge(L.item_copied[e], rows * L.per[e])


def affine_copy(nc, e, out, in_, scale, bias):
    if e == 0:
        return nc.scalar.activation(out, in_, ACT.Identity, bias=bias, scale=scale)
    return nc.vector.tensor_scalar(out, in_, scale, bias, ALU.mult, ALU.add)


def scale_copy(nc, e, out, in_, scale):
    if e == 0:
        return nc.scalar.activation(out, in_, ACT.Identity, scale=scale)
    return nc.vector.tensor_scalar(out, in_, scale, None, ALU.mult)


def copy_transposed(nc, eng, L, b, e):
    wait_item(eng, L, b, e)
    scale_copy(nc, e, L.xT[:, e, :], L.J[e], 1.0).then_inc(L.item_copied[e], 1)




def pe_output(nc, pe, L, b, z, wo):
    n = len(wo)
    for t in range(QT):
        if t >= 2:
            pe.wait_ge(L.y_added, at(b, QT, t - 1))
        for c in range(n):
            last = nc.tensor.matmul(L.J[t % 2][:, 0:D], z[:, c, t * P:(t + 1) * P], wo[c], start=(c == 0), stop=(c == n - 1))
        last.then_inc(L.y_ready, 1)


def pool_bias(nc, pool, L, b, first):
    pool.wait_ge(L.residual_loaded, 16 * (b + 1))
    nc.gpsimd.tensor_tensor(L.residual, L.residual, L.bias, ALU.add).then_inc(L.residual_biased, 1)


def dve_norm(nc, dve, L, b):
    if L.bias is not None:
        dve.wait_ge(L.residual_biased, b + 1)
    else:
        dve.wait_ge(L.residual_loaded, 16 * (b + 1))
    for t in range(QT):
        dve.wait_ge(L.y_ready, at(b, QT, t + 1))
        nc.vector.tensor_tensor(L.h[:, t, :], L.J[t % 2][:, 0:D], L.residual[:, t, :], ALU.add).then_inc(L.y_added, 1)
    for t in range(QT):
        dve.wait_ge(L.y_added, at(b, QT, t + 1))
        nc.vector.bn_stats(L.stats[:, t, :], L.h[:, t, :]).then_inc(L.stats_done, 1)
    for t in range(QT):
        dve.wait_ge(L.stats_done, at(b, QT, t + 1))
        apart(dve, L.passed["dve"])
        nc.vector.bn_aggr(L.moments[:, t, :], L.stats[:, t, :]).then_inc(L.aggr_done, 1)
    dve.wait_ge(L.aggr_done, at(b, QT, QT))
    nc.vector.tensor_scalar(L.var_eps, L.moments[:, :, 1], LN_EPS, None, ALU.add).then_inc(L.var_done, 1)
    dve.wait_ge(L.rstd_done, b + 1)
    dve.wait_ge(L.stored, 16 * b)
    for t in range(QT):
        nc.vector.tensor_scalar(L.result[:, t, :], L.h[:, t, :], L.moments[:, t, 0:1], L.rstd[:, t:t + 1],
                                ALU.subtract, ALU.mult).then_inc(L.normed, 1)


def pool_rstd(nc, pool, L, b):
    pool.wait_ge(L.var_done, b + 1)
    nc.gpsimd.tensor_tensor(L.rstd, L.var_eps, L.minus_half, ALU.pow).then_inc(L.rstd_done, 1)




def unit_keys(A, u):
    return u % QT + 1 if A.causal else QT


def pe_attention(nc, pe, A, b):
    U = QT * A.heads

    def scores(u):
        h, qt = divmod(u, QT)
        nk = unit_keys(A, u) * P
        S = A.S[u % S_BANKS]
        pe.wait_ge(A.exp_done, at(b, U, u - S_BANKS + 1))
        last = nc.tensor.matmul(S[:, 0:nk], A.query(h, qt), A.keys(h)[:, 0:nk], start=True, stop=not A.causal)
        if A.causal:
            last = nc.tensor.matmul(S[:, nk - P:nk], A.ident_bf, A.future, start=False, stop=True)
        last.then_inc(A.scores_ready, 1)

    def transposes(u):
        pe.wait_ge(A.probs_ready, at(b, U, u + 1))
        pe.wait_ge(A.probsT_copied, at(b, U, u - 1))
        for k in range(unit_keys(A, u)):
            last = nc.tensor.transpose(A.TB[u % 2][:, k * P:(k + 1) * P], A.probs[:, u % P_SLOTS, k * P:(k + 1) * P], A.ident)
        last.then_inc(A.probsT_ready, 1)

    def values(h):
        pe.wait_ge(A.probsT_copied, at(b, U, QT * h + QT))
        g, j = divmod(h, A.group)
        if j == 0:
            pe.wait_ge(A.z_copied, at(b, A.heads // A.group, g))
        for k in range(QT):
            c0 = k * P if A.causal else 0
            last = nc.tensor.matmul(A.Z[A.z_step * j:A.z_step * j + A.z_rows, c0:T], A.value(h, k), A.probsT[:, h % 2, k, c0:T],
                                    start=(k == 0), stop=(k == QT - 1))
        last.then_inc(A.values_done, 1)

    for i in range(U + PV_LAG):
        if i < U:
            scores(i)
        if T_LAG <= i < U + T_LAG:
            transposes(i - T_LAG)
        if i >= PV_LAG and (i - PV_LAG) % QT == QT - 1:
            values((i - PV_LAG) // QT)


def act_attention(nc, act, A, b):
    U = QT * A.heads

    def copy_probsT(u):
        h, qt = divmod(u, QT)
        n = unit_keys(A, u)
        act.wait_ge(A.probsT_ready, at(b, U, u + 1))
        act.wait_ge(A.values_done, at(b, A.heads, h - 1))
        nc.scalar.activation(A.probsT[:, h % 2, 0:n, qt * P:(qt + 1) * P],
                             A.TB[u % 2][:, 0:n * P].rearrange("p (k q) -> p k q", k=n), ACT.Copy).then_inc(A.probsT_copied, 1)

    def exps(u):
        nk = unit_keys(A, u) * P
        act.wait_ge(A.negmax_ready, at(b, U, u + 1))
        act.wait_ge(A.probsT_ready, at(b, U, u - P_SLOTS + 1))
        nc.scalar.activation(A.probs[:, u % P_SLOTS, 0:nk], A.S[u % S_BANKS][:, 0:nk], ACT.Exp,
                             bias=A.negmax[:, u:u + 1], accum_out=A.sums[:, u:u + 1]).then_inc(A.exp_done, 1)

    for i in range(U + PV_LAG):
        if i >= PV_LAG:
            copy_probsT(i - PV_LAG)
        if i < U:
            exps(i)


def dve_attention(nc, dve, A, b):
    U = QT * A.heads

    def negmax(u):
        nk = unit_keys(A, u) * P
        dve.wait_ge(A.scores_ready, at(b, U, u + 1))
        nc.vector.tensor_reduce(A.negmax[:, u:u + 1], A.S[u % S_BANKS][:, 0:nk], AX, ALU.max, negate=True).then_inc(A.negmax_ready, 1)

    def rinv(u):
        dve.wait_ge(A.exp_done, at(b, U, u + 1))
        nc.vector.reciprocal(A.rinv[:, u:u + 1], A.sums[:, u:u + 1]).then_inc(A.rinv_ready, 1)

    def copy_z(g):
        dve.wait_ge(A.values_done, at(b, A.heads, (g + 1) * A.group))
        if A.z_bias is None:
            nc.vector.tensor_copy(A.zT[0:A.z_part, g, :], A.Z[0:A.z_part]).then_inc(A.z_copied, 1)
        else:
            nc.vector.tensor_scalar(A.zT[:, g, :], A.Z, A.z_bias[:, g:g + 1], None, ALU.add).then_inc(A.z_copied, 1)

    for i in range(U + PV_LAG + 2):
        if i < U:
            negmax(i)
        if 1 <= i <= U:
            rinv(i - 1)
        j = i - PV_LAG - 1
        if j >= 0 and j % (QT * A.group) == QT * A.group - 1:
            copy_z(j // (QT * A.group))


def pool_attention(nc, pool, A, b):
    U = QT * A.heads
    for u in range(U):
        nk = unit_keys(A, u) * P
        pr = A.probs[:, u % P_SLOTS, 0:nk]
        pool.wait_ge(A.rinv_ready, at(b, U, u + 1))
        apart(pool, A.passed["pool"])
        nc.gpsimd.tensor_scalar(pr, pr, A.rinv[:, u:u + 1], 1.0, ALU.mult, ALU.mult).then_inc(A.probs_ready, 1)




def build(nc, a, out, layers=(0, 1, 2, 3, 4, 5)):
    NB = a["x"].shape[0]
    ET = mybir.EngineType
    with ExitStack() as root:
        def sbt(name, shape, dt=F32):
            return root.enter_context(nc.sbuf_tensor(name, shape, dt))

        def psum(name):
            return root.enter_context(nc.psum_tensor(name, [P, T], F32))

        weights = [sbt("weights_even", [P, 8400]), sbt("weights_odd", [P, 13100])]
        arena = sbt("arena", [P, 22800])
        consts = sbt("consts", [P, 160])
        consts_bf = sbt("consts_bf", [P, 256], BF16)
        tokens = sbt("tokens", [P, QT, D])
        residual = sbt("residual", [P, QT, D])
        hbuf = sbt("hbuf", [P, QT, D])
        result = sbt("result", [P, QT, D])
        xT = sbt("xT", [P, KT, T])
        small = sbt("small", [P, 64])
        banks = [psum(f"bank{i}") for i in range(8)]
        scratch = [nc.dram_tensor(f"tokens_after_{i}", [NB, T, D], F32).ap() for i in range(5)]

        ident = consts[:, 0:P]
        half_mask = consts[:, P:P + 2]
        head_mask = consts[:, P + 2:P + 10]
        minus_half = consts[:, P + 10:P + 10 + QT]
        iota = consts[:, P + 14:P + 30]
        ident_bf = consts_bf[:, 0:P]
        future = consts_bf[:, P:2 * P]
        consts_loaded = root.enter_context(nc.semaphore("consts_loaded"))
        weights_loaded = [root.enter_context(nc.semaphore(f"weights_loaded_{i}")) for i in range(6)]

        def carve(buf):
            off = [0]

            def take(*shape):
                n = 1
                for s in shape:
                    n *= s
                v = buf[:, off[0]:off[0] + n]
                off[0] += n
                assert off[0] <= buf.shape[1], off[0]
                if len(shape) == 2:
                    v = v.rearrange("p (a b) -> p a b", a=shape[0])
                if len(shape) == 3:
                    v = v.rearrange("p (a b c) -> p a b c", a=shape[0], b=shape[1])
                return v
            return take

        W = [{} for _ in range(6)]
        moves = [[] for _ in range(6)]

        def bring(l, name, take, *shape, rows=P):
            v = take(*shape)
            W[l][name] = v
            flat = v
            if len(shape) == 2:
                flat = v.rearrange("p a b -> p (a b)")
            moves[l].append((flat[0:rows], a[name]))

        t = carve(weights[0])
        bring(0, "l0a_wq", t, KT, 1024)
        bring(0, "l0a_wk", t, KT, 512)
        bring(0, "l0a_wv", t, KT, 512)
        bring(0, "l0a_wo", t, 8, D)
        bring(0, "l0a_bo", t, D)
        t = carve(weights[1])
        bring(1, "l0x_wq", t, KT, 512)
        bring(1, "l0x_wk", t, 2, 512, rows=96)
        bring(1, "l0x_wv", t, 2, 512, rows=96)
        bring(1, "l0x_wo", t, 4, D)
        bring(1, "l0x_bo", t, D)
        t = carve(weights[0])
        bring(2, "l0f_wqkv", t, 3 * KT, 1024)
        bring(2, "l0f_wo", t, 8, D)
        bring(2, "l0f_sim", t, KT, 16)
        bring(2, "l0f_gates", t, 16)
        t = carve(weights[1])
        bring(3, "l1a_wg", t, KT, D)
        bring(3, "l1a_wv", t, KT, D)
        bring(3, "l1a_wo", t, 4, D)
        bring(3, "l1a_head_rows", t, 16, P)
        bring(3, "l1a_bg", t, D)
        bring(3, "l1a_bv", t, 4)
        bring(3, "l1a_bo", t, D)
        take_rest_of_odd = t
        t = carve(weights[1])
        bring(5, "l1f_wy", t, KT, 1920)
        bring(5, "l1f_wg", t, KT, 1920)
        bring(5, "l1f_w2", t, 15, D)
        bring(5, "l1f_gate", t, KT, 8)
        bring(5, "l1f_expert_rows", t, 12, P)
        t = carve(weights[0])
        bring(4, "l1x_wq", t, KT, 256)
        bring(4, "l1x_wk", t, 2, 256, rows=96)
        bring(4, "l1x_wv", t, 2, 256, rows=96)
        bring(4, "l1x_w1", t, 4, 512)
        bring(4, "l1x_w2", t, 4, D)
        bring(4, "l1x_bq", t, 2)
        bring(4, "l1x_bk", t, 2)
        bring(4, "l1x_bv", t, 4)
        bring(4, "l1x_b1", t, 4)
        bring(4, "l1x_b2", t, D)

        def load_weights(sp, l):
            for dst, src in moves[l]:
                nc.sync.dma_start(dst, src).then_inc(weights_loaded[l], 16)

        def wait_weights(eng, l):
            eng.wait_ge(weights_loaded[l], 16 * len(moves[l]))

        def load_next_weights(l):
            def load(sp):
                later = [m for m in layers if m > l]
                if later:
                    load_weights(sp, later[0])
            return load

        def common(l, per, bias):
            def sem(name):
                return nc.alloc_semaphore(f"l{l}_{name}")
            src = a["x"] if l == layers[0] else scratch[l - 1]
            dst = out if l == layers[-1] else scratch[l]
            L = Names()
            L.x_in = lambda b: src[bass.ds(b, 1)].rearrange("o (t p) d -> p (o t) d", p=P)
            L.x_out = lambda b: dst[bass.ds(b, 1)].rearrange("o (t p) d -> p (o t) d", p=P)
            L.ctx_in, L.load_next_weights, L.extra_tokens_reader = None, load_next_weights(l), None
            L.bias, L.per = bias, per
            L.tokens, L.residual, L.h, L.result, L.xT, L.J = tokens[:], residual[:], hbuf[:], result[:], xT[:], [banks[6][:], banks[7][:]]
            L.ident, L.ident_bf, L.future, L.minus_half, L.consts_loaded = ident, ident_bf, future, minus_half, consts_loaded
            L.stats = small[:, 0:24].rearrange("p (t s) -> p t s", t=QT)
            L.moments = small[:, 24:32].rearrange("p (t s) -> p t s", t=QT)
            L.var_eps, L.rstd = small[:, 32:36], small[:, 36:40]
            L.tokens_loaded, L.context_loaded, L.residual_loaded = sem("tokens_loaded"), sem("context_loaded"), sem("residual_loaded")
            L.residual_biased, L.stored = sem("residual_biased"), sem("stored")
            L.item_ready = [sem("item_ready_act"), sem("item_ready_dve")]
            L.item_copied = [sem("item_copied_act"), sem("item_copied_dve")]
            L.y_ready, L.y_added, L.stats_done, L.aggr_done = sem("y_ready"), sem("y_added"), sem("stats_done"), sem("aggr_done")
            L.var_done, L.rstd_done, L.normed = sem("var_done"), sem("rstd_done"), sem("normed")
            L.sem = sem
            L.passed = {e: sem(f"{e}_passed") for e in ("sp", "pe", "dve", "pool")}
            return L

        def attention_of(L, take, heads, group, z_step, z_rows, causal, prefix=""):
            U = QT * heads
            L.scores_ready, L.negmax_ready, L.exp_done, L.rinv_ready = (
                L.sem(s) for s in ("scores_ready", "negmax_ready", "exp_done", "rinv_ready"))
            L.probs_ready, L.probsT_ready, L.probsT_copied, L.values_done, L.z_copied, L.pads_zeroed = (
                L.sem(s) for s in ("probs_ready", "probsT_ready", "probsT_copied", "values_done", "z_copied", "pads_zeroed"))
            L.z_bias, L.z_part, L.heads, L.group, L.z_step, L.z_rows, L.causal = None, z_step * group, heads, group, z_step, z_rows, causal
            L.S, L.TB, L.Z = [banks[i][:] for i in range(S_BANKS)], [banks[3][:], banks[4][:]], banks[5][:]
            L.probs, L.probsT = take(P_SLOTS, T), take(2, QT, T)
            L.negmax, L.sums, L.rinv = take(U), take(U), take(U)

        def wide_attention(l, heads, kv_heads, causal, context):
            w = W[l]
            with nc.cleanup_on_exit():
                qn, kn = heads // 2, kv_heads // 2
                Q0, K0 = KT, KT + qn
                V0 = K0 + kn
                n_items = V0 + QT
                L = common(l, [(n_items + 1) // 2, n_items // 2], None)
                take = carve(arena)
                L.qT, L.kz, L.v = take(qn, T), take(kv_heads, T), take(QT, 64 * kv_heads)
                L.zT = take(heads // 2, T)
                attention_of(L, take, heads, 2, 64, 64, causal)
                if context:
                    L.ctx_in = lambda b: a["ctxT"][bass.ds(b, 1)].rearrange("o (k p) t -> p (o k) t", p=96)
                    L.context = take(2, T)[0:96]
                    wq, wk, wv, wo, bo = w["l0x_wq"], w["l0x_wk"][0:96], w["l0x_wv"][0:96], w["l0x_wo"], w["l0x_bo"]
                    src = L.context
                else:
                    wq, wk, wv, wo, bo = w["l0a_wq"], w["l0a_wk"], w["l0a_wv"], w["l0a_wo"], w["l0a_bo"]
                    src = L.xT
                L.bias = bo.unsqueeze(1).broadcast_to([P, QT, D])

                def head_at(i):
                    c, j = divmod(i, 2)
                    kv = (c // 2) * 2 + j if not context else i
                    return c, kv

                L.query = lambda i, qt: L.qT[:, head_at(i)[0], qt * P:(qt + 1) * P]
                L.keys = lambda i: L.kz[:, head_at(i)[1], :]
                L.value = lambda i, k: L.v[:, k, 64 * head_at(i)[1]:64 * head_at(i)[1] + 64]

                with nc.Block() as block:
                    @block.sync
                    def _(sp):
                        sp_stream(nc, sp, L, NB)

                    @block.tensor
                    def _(pe):
                        wait_weights(pe, l)

                        def project(b, first):
                            pe_transpose_tokens(nc, pe, L, b, first)
                            wait_items_copied(pe, L, b, 1)
                            if context:
                                pe.wait_ge(L.context_loaded, 16 * (b + 1))
                            for c in range(qn):
                                pe_item(nc, pe, L, b, Q0 + c, L.J[(Q0 + c) % 2], [(wq[:, k, c * P:(c + 1) * P], L.xT[:, k, :]) for k in range(KT)])
                            for c in range(kn):
                                pe_item(nc, pe, L, b, K0 + c, L.J[(K0 + c) % 2], [(wk[:, k, c * P:(c + 1) * P], src[:, k, :]) for k in range(2)])
                            for t in range(QT):
                                pe_item(nc, pe, L, b, V0 + t, L.J[(V0 + t) % 2][:, 0:64 * kv_heads],
                                        [(src[:, k, t * P:(t + 1) * P], wv[:, k, :]) for k in range(2)])

                        def attend(b):
                            wait_items_copied(pe, L, b, n_items - 1)
                            pe_attention(nc, pe, L, b)

                        def output(b, rows):
                            pe.wait_ge(L.z_copied, at(b, heads // 2, heads // 2))
                            wait_banks_free(pe, L, rows)
                            pe_output(nc, pe, L, b, L.zT, [wo[:, c, :] for c in range(qn)])

                        project(0, True)
                        with nc.Fori(0, NB - 1, engines=[ET.PE]) as b:
                            attend(b)
                            project(b + 1, False)
                            output(b, b + 2)
                        attend(NB - 1)
                        output(NB - 1, NB)

                    def copy_items(eng, e, b):
                        copy_transposed(nc, eng, L, b, e)
                        for c in range(qn):
                            if (Q0 + c) % 2 == e:
                                wait_item(eng, L, b, Q0 + c)
                                scale_copy(nc, e, L.qT[:, c, :], L.J[e], 64 ** -0.5).then_inc(L.item_copied[e], 1)
                        for c in range(kn):
                            if (K0 + c) % 2 == e:
                                wait_item(eng, L, b, K0 + c)
                                scale_copy(nc, e, L.kz[:, 2 * c, :], L.J[e], half_mask[:, 0:1])
                                scale_copy(nc, e, L.kz[:, 2 * c + 1, :], L.J[e], half_mask[:, 1:2]).then_inc(L.item_copied[e], 1)
                        for t in range(QT):
                            if (V0 + t) % 2 == e:
                                wait_item(eng, L, b, V0 + t)
                                scale_copy(nc, e, L.v[:, t, :], L.J[e][:, 0:64 * kv_heads], 1.0).then_inc(L.item_copied[e], 1)

                    @block.scalar
                    def _(act):
                        act.wait_ge(consts_loaded, 32)
                        copy_items(act, 0, 0)
                        with nc.Fori(0, NB - 1, engines=[ET.Activation]) as b:
                            act_attention(nc, act, L, b)
                            copy_items(act, 0, b + 1)
                        act_attention(nc, act, L, NB - 1)

                    @block.vector
                    def _(dve):
                        dve.wait_ge(consts_loaded, 32)
                        copy_items(dve, 1, 0)
                        with nc.Fori(0, NB - 1, engines=[ET.DVE]) as b:
                            dve_attention(nc, dve, L, b)
                            copy_items(dve, 1, b + 1)
                            dve_norm(nc, dve, L, b)
                        dve_attention(nc, dve, L, NB - 1)
                        dve_norm(nc, dve, L, NB - 1)

                    @block.gpsimd
                    def _(pool):
                        wait_weights(pool, l)
                        pool.wait_ge(consts_loaded, 32)
                        with nc.Fori(0, NB, engines=[ET.Pool]) as b:
                            pool_bias(nc, pool, L, b, False)
                            pool_attention(nc, pool, L, b)
                            pool_rstd(nc, pool, L, b)

        def narrow_cross_attention(l):
            w = W[l]
            heads, d = 16, 16
            with nc.cleanup_on_exit():
                Q0, K0, V0 = 2, 4, 6
                n_items = 10
                L = common(l, [n_items // 2, n_items // 2], w["l1x_b2"].unsqueeze(1).broadcast_to([P, QT, D]))
                take = carve(arena)
                L.qT, L.kz, L.v = take(2, T), take(heads, T), take(QT, 32 * heads)
                L.zT, L.hT = take(4, T), take(4, T)
                attention_of(L, take, heads, 4, 32, 32, False)
                L.ctx_in = lambda b: a["ctxT"][bass.ds(b, 1)].rearrange("o (k p) t -> p (o k) t", p=96)
                L.context = take(2, T)[0:96]
                bq_scaled, bk_masked = take(2), take(heads)
                hidden_ready = [L.sem("hidden_ready_act"), L.sem("hidden_ready_dve")]
                hidden_copied = [L.sem("hidden_copied_act"), L.sem("hidden_copied_dve")]
                biases_made = L.sem("biases_made")
                L.query = lambda h, qt: L.qT[:, h // 8, qt * P:(qt + 1) * P]
                L.keys = lambda h: L.kz[:, h, :]
                L.value = lambda h, k: L.v[:, k, 32 * h:32 * h + 32]
                L.z_bias = w["l1x_bv"]

                with nc.Block() as block:
                    @block.sync
                    def _(sp):
                        sp_stream(nc, sp, L, NB)

                    @block.tensor
                    def _(pe):
                        wait_weights(pe, l)
                        pe.wait_ge(L.pads_zeroed, 1)

                        def project(b, first):
                            pe_transpose_tokens(nc, pe, L, b, first)
                            wait_items_copied(pe, L, b, 1)
                            pe.wait_ge(L.context_loaded, 16 * (b + 1))
                            for c in range(2):
                                pe_item(nc, pe, L, b, Q0 + c, L.J[(Q0 + c) % 2], [(w["l1x_wq"][:, k, c * P:(c + 1) * P], L.xT[:, k, :]) for k in range(2)])
                            for c in range(2):
                                pe_item(nc, pe, L, b, K0 + c, L.J[(K0 + c) % 2], [(w["l1x_wk"][0:96, k, c * P:(c + 1) * P], L.context[:, k, :]) for k in range(2)])
                            for t in range(QT):
                                pe_item(nc, pe, L, b, V0 + t, L.J[(V0 + t) % 2][:, 0:D],
                                        [(L.context[:, k, t * P:(t + 1) * P], w["l1x_wv"][0:96, k, :]) for k in range(2)])

                        def attend(b):
                            wait_items_copied(pe, L, b, n_items - 1)
                            pe_attention(nc, pe, L, b)

                        def hidden(b, rows):
                            pe.wait_ge(L.z_copied, at(b, 4, 4))
                            wait_banks_free(pe, L, rows)
                            for c in range(4):
                                if c >= 2:
                                    pe.wait_ge(hidden_copied[c % 2], at(b, 2, c // 2))
                                for k in range(4):
                                    last = nc.tensor.matmul(L.J[c % 2], w["l1x_w1"][:, k, c * P:(c + 1) * P], L.zT[:, k, :], start=(k == 0), stop=(k == 3))
                                last.then_inc(hidden_ready[c % 2], 1)
                            for e in range(2):
                                pe.wait_ge(hidden_copied[e], at(b, 2, 2))

                        def output(b, rows):
                            hidden(b, rows)
                            pe_output(nc, pe, L, b, L.hT, [w["l1x_w2"][:, c, :] for c in range(4)])

                        project(0, True)
                        with nc.Fori(0, NB - 1, engines=[ET.PE]) as b:
                            attend(b)
                            project(b + 1, False)
                            output(b, b + 2)
                        attend(NB - 1)
                        output(NB - 1, NB)

                    def copy_items(eng, e, b):
                        copy_transposed(nc, eng, L, b, e)
                        wait_item(eng, L, b, Q0 + e)
                        affine_copy(nc, e, L.qT[:, e, :], L.J[e], d ** -0.5, bq_scaled[:, e:e + 1]).then_inc(L.item_copied[e], 1)
                        wait_item(eng, L, b, K0 + e)
                        for j in range(8):
                            h = 8 * e + j
                            last = affine_copy(nc, e, L.kz[:, h, :], L.J[e], head_mask[:, j:j + 1], bk_masked[:, h:h + 1])
                        last.then_inc(L.item_copied[e], 1)
                        for t in range(e, QT, 2):
                            wait_item(eng, L, b, V0 + t)
                            scale_copy(nc, e, L.v[:, t, :].rearrange("p (h c) -> p h c", c=32)[:, :, 0:d],
                                       L.J[e][:, 0:D].rearrange("p (h c) -> p h c", c=d), 1.0).then_inc(L.item_copied[e], 1)

                    def copy_hidden(eng, e, b):
                        for c in range(e, 4, 2):
                            eng.wait_ge(hidden_ready[e], at(b, 2, c // 2 + 1))
                            if e == 0:
                                last = nc.scalar.activation(L.hT[:, c, :], L.J[e], ACT.Relu, bias=w["l1x_b1"][:, c:c + 1])
                            else:
                                last = nc.vector.tensor_scalar(L.hT[:, c, :], L.J[e], w["l1x_b1"][:, c:c + 1], 0.0, ALU.add, ALU.max)
                            last.then_inc(hidden_copied[e], 1)

                    @block.scalar
                    def _(act):
                        wait_weights(act, l)
                        act.wait_ge(consts_loaded, 32)
                        act.wait_ge(biases_made, 3)
                        act.wait_ge(L.pads_zeroed, 1)
                        copy_items(act, 0, 0)
                        with nc.Fori(0, NB - 1, engines=[ET.Activation]) as b:
                            act_attention(nc, act, L, b)
                            copy_items(act, 0, b + 1)
                            copy_hidden(act, 0, b)
                        act_attention(nc, act, L, NB - 1)
                        copy_hidden(act, 0, NB - 1)

                    @block.vector
                    def _(dve):
                        wait_weights(dve, l)
                        dve.wait_ge(consts_loaded, 32)
                        dve.wait_ge(biases_made, 3)
                        dve.wait_ge(L.pads_zeroed, 1)
                        copy_items(dve, 1, 0)
                        with nc.Fori(0, NB - 1, engines=[ET.DVE]) as b:
                            dve_attention(nc, dve, L, b)
                            copy_items(dve, 1, b + 1)
                            copy_hidden(dve, 1, b)
                            dve_norm(nc, dve, L, b)
                        dve_attention(nc, dve, L, NB - 1)
                        copy_hidden(dve, 1, NB - 1)
                        dve_norm(nc, dve, L, NB - 1)

                    @block.gpsimd
                    def _(pool):
                        nc.gpsimd.memset(L.v, 0.0).then_inc(L.pads_zeroed, 1)
                        wait_weights(pool, l)
                        pool.wait_ge(consts_loaded, 32)
                        nc.gpsimd.tensor_scalar(bq_scaled, w["l1x_bq"], d ** -0.5, 1.0, ALU.mult, ALU.mult).then_inc(biases_made, 1)
                        for c in range(2):
                            nc.gpsimd.tensor_scalar(bk_masked[:, 8 * c:8 * c + 8], head_mask, w["l1x_bk"][:, c:c + 1], 1.0, ALU.mult, ALU.mult).then_inc(biases_made, 1)
                        with nc.Fori(0, NB, engines=[ET.Pool]) as b:
                            pool_bias(nc, pool, L, b, False)
                            pool_attention(nc, pool, L, b)
                            pool_rstd(nc, pool, L, b)

        def gated_experts(l):
            w = W[l]
            E, NC, NX = 8, 15, 12
            with nc.cleanup_on_exit():
                L = common(l, [2, 2], None)
                sem = L.sem
                take = carve(arena)
                L.acts, silu, scaled = take(NC, T), take(2, T), take(2, T)
                wT, logits, shifted, exps, scores, gates = take(T), take(QT, E), take(QT, E), take(QT, E), take(QT, E), take(QT, E)
                top, picked, picked2, index_f, index = take(QT, 8), take(QT, E), take(QT, E), take(QT, 8), take(QT, 8).bitcast(U32)
                peak, total, inverse = take(QT), take(QT), take(QT)
                Y, G, WB = ([banks[3 * i + j][:] for i in range(2)] for j in range(3))
                route_step, shifted_ready, exps_ready, gates_ready = sem("route_step"), sem("shifted_ready"), sem("exps_ready"), sem("gates_ready")
                g_ready, yw_ready, silu_done, scaled_done, chunk_done, zeroed = (
                    sem("g_ready"), sem("yw_ready"), sem("silu_done"), sem("scaled_done"), sem("chunk_done"), sem("zeroed"))
                order = list(range(NX, NC)) + list(range(NX))
                STEPS = 15

                with nc.Block() as block:
                    @block.sync
                    def _(sp):
                        sp_stream(nc, sp, L, NB)

                    @block.tensor
                    def _(pe):
                        wait_weights(pe, l)
                        pe.wait_ge(zeroed, 1)

                        def head(b, first):
                            pe_transpose_tokens(nc, pe, L, b, first)
                            wait_items_copied(pe, L, b, 1)
                            for t in range(QT):
                                for k in range(KT):
                                    last = nc.tensor.matmul(L.J[0][:, E * t:E * t + E], L.xT[:, k, t * P:(t + 1) * P], w["l1f_gate"][:, k, :], start=(k == 0), stop=(k == KT - 1))
                            last.then_inc(L.item_ready[0], 1)

                        def chunks(b):
                            for i, c in enumerate(order):
                                if i == NC - NX:
                                    pe.wait_ge(gates_ready, b + 1)
                                    pe.wait_ge(L.y_added, QT * b)
                                    apart(pe, L.passed["pe"])
                                    for t in range(QT):
                                        last = nc.tensor.transpose(L.J[1][0:E, t * P:(t + 1) * P], gates[:, t, :], L.ident)
                                    last.then_inc(L.item_ready[1], 1)
                                    pe.wait_ge(L.item_copied[1], at(b, 2, 2))
                                s = i % 2
                                pe.wait_ge(chunk_done, at(b, NC, i - 1))
                                for k in range(KT):
                                    last = nc.tensor.matmul(G[s], w["l1f_wg"][:, k, c * P:(c + 1) * P], L.xT[:, k, :], start=(k == 0), stop=(k == KT - 1))
                                last.then_inc(g_ready, 1)
                                for k in range(KT):
                                    last = nc.tensor.matmul(Y[s], w["l1f_wy"][:, k, c * P:(c + 1) * P], L.xT[:, k, :], start=(k == 0), stop=(k == KT - 1))
                                if c < NX:
                                    last = nc.tensor.matmul(WB[s], w["l1f_expert_rows"][:, c, :], wT, start=True, stop=True)
                                last.then_inc(yw_ready, 1)

                        def output(b, more):
                            pe.wait_ge(chunk_done, NC * (b + 1))
                            pe.wait_ge(L.item_copied[0], 2 * (b + 1) + 2 * more)
                            pe.wait_ge(L.item_copied[1], 2 * (b + 1) + more)
                            pe_output(nc, pe, L, b, L.acts, [w["l1f_w2"][:, c, :] for c in range(NC)])

                        head(0, True)
                        with nc.Fori(0, NB - 1, engines=[ET.PE]) as b:
                            chunks(b)
                            head(b + 1, False)
                            output(b, 1)
                        chunks(NB - 1)
                        output(NB - 1, 0)

                    @block.scalar
                    def _(act):
                        def head(b):
                            copy_transposed(nc, act, L, b, 0)
                            wait_item(act, L, b, 2)
                            nc.scalar.activation(logits, L.J[0][:, 0:QT * E].rearrange("p (t e) -> p t e", t=QT), ACT.Copy).then_inc(L.item_copied[0], 1)
                            act.wait_ge(shifted_ready, b + 1)
                            nc.scalar.activation(exps, shifted, ACT.Exp).then_inc(exps_ready, 1)

                        def chunks(b):
                            for i in range(NC):
                                act.wait_ge(g_ready, at(b, NC, i + 1))
                                act.wait_ge(chunk_done, at(b, NC, i - 1))
                                nc.scalar.activation(silu[:, i % 2, :], G[i % 2], ACT.Silu).then_inc(silu_done, 1)

                        head(0)
                        with nc.Fori(0, NB - 1, engines=[ET.Activation]) as b:
                            chunks(b)
                            head(b + 1)
                        chunks(NB - 1)

                    @block.vector
                    def _(dve):
                        dve.wait_ge(consts_loaded, 32)

                        def head(b):
                            copy_transposed(nc, dve, L, b, 1)
                            steps = [0]

                            def step(ins):
                                steps[0] += 1
                                ins.then_inc(route_step, 1)
                                dve.wait_ge(route_step, at(b, STEPS, steps[0]))
                                apart(dve, L.passed["dve"])

                            dve.wait_ge(L.item_copied[0], at(b, 2, 2))
                            step(nc.vector.tensor_reduce(peak, logits, AX, ALU.max))
                            nc.vector.tensor_tensor(shifted, logits, peak.unsqueeze(2).broadcast_to([P, QT, E]), ALU.subtract).then_inc(shifted_ready, 1)
                            dve.wait_ge(exps_ready, b + 1)
                            step(nc.vector.tensor_reduce(total, exps, AX, ALU.add))
                            step(nc.vector.reciprocal(inverse, total))
                            step(nc.vector.tensor_tensor(scores, exps, inverse.unsqueeze(2).broadcast_to([P, QT, E]), ALU.mult))
                            for t in range(QT):
                                step(nc.vector.max(top[:, t, :], scores[:, t, :]))
                            for t in range(QT):
                                step(nc.vector.max_index(index[:, t, :], top[:, t, :], scores[:, t, :]))
                            step(nc.vector.tensor_copy(index_f, index))
                            ids = iota[:, 0:E].unsqueeze(1).broadcast_to([P, QT, E])
                            nc.vector.tensor_tensor(picked2, ids, index_f[:, :, 1:2].broadcast_to([P, QT, E]), ALU.is_equal)
                            step(nc.vector.tensor_tensor(picked, ids, index_f[:, :, 0:1].broadcast_to([P, QT, E]), ALU.is_equal))
                            step(nc.vector.tensor_tensor(picked, picked, picked2, ALU.add))
                            dve.wait_ge(L.item_ready[1], at(b, 2, 0))
                            nc.vector.tensor_tensor(gates, scores, picked, ALU.mult).then_inc(gates_ready, 1)
                            assert steps[0] == STEPS

                        def chunks(b):
                            for i, c in enumerate(order):
                                s = i % 2
                                if i == NC - NX:
                                    wait_item(dve, L, b, 3)
                                    nc.vector.tensor_copy(wT[0:E], L.J[1][0:E]).then_inc(L.item_copied[1], 1)
                                dve.wait_ge(silu_done, at(b, NC, i + 1))
                                dve.wait_ge(yw_ready, at(b, NC, i + 1))
                                if c >= NX:
                                    nc.vector.tensor_tensor(L.acts[:, c, :], Y[s], silu[:, s, :], ALU.mult).then_inc(chunk_done, 1)
                                    continue
                                nc.vector.tensor_tensor(scaled[:, s, :], Y[s], silu[:, s, :], ALU.mult).then_inc(scaled_done, 1)
                                dve.wait_ge(scaled_done, at(b, NX, i - (NC - NX) + 1))
                                nc.vector.tensor_tensor(L.acts[:, c, :], WB[s], scaled[:, s, :], ALU.mult).then_inc(chunk_done, 1)

                        head(0)
                        with nc.Fori(0, NB - 1, engines=[ET.DVE]) as b:
                            chunks(b)
                            head(b + 1)
                            dve_norm(nc, dve, L, b)
                        chunks(NB - 1)
                        dve_norm(nc, dve, L, NB - 1)

                    @block.gpsimd
                    def _(pool):
                        nc.gpsimd.memset(wT, 0.0).then_inc(zeroed, 1)
                        with nc.Fori(0, NB, engines=[ET.Pool]) as b:
                            pool_rstd(nc, pool, L, b)

        def mixture_attention(l):
            w = W[l]
            E, d = 16, 64
            with nc.cleanup_on_exit():
                L = common(l, [3, 2], None)
                sem = L.sem
                take = carve(arena)
                L.qT, L.kT, qkv = take(T), take(T), take(3 * QT, d)
                product = [take(E, d), take(E, d)]
                mixed, L.mixT, L.zT = take(QT, E * d), take(8, T), take(1, T)
                attention_of(L, take, 1, 1, d, d, True)
                ones, sim_square, sim_unit, sim_norm, sim_inverse, sigmoid = take(P), take(KT, E), take(KT, E), take(E), take(E), take(E)
                halves, square = take(E), take(D)
                raw, logits, active, gated, shifted, exps, masked, weights_ = (take(QT, E) for _ in range(8))
                fallback, fallback2 = take(QT, E), take(QT, E)
                top, index_f, index = take(QT, 8), take(QT, 8), take(QT, 8).bitcast(U32)
                length2, length, inv_length, peak, idle, total, inverse = (take(QT) for _ in range(7))
                L.query = lambda h, qt: L.qT[:, qt * P:(qt + 1) * P]
                L.keys = lambda h: L.kT
                L.value = lambda h, k: qkv[:, 2 * QT + k, :]
                setup_step, squared, norm2_ready, norm_done, sim_ready = sem("setup_step"), sem("squared"), sem("norm2_ready"), sem("norm_done"), sem("sim_ready")
                exp_gates_done = sem("exp_gates_done")
                lengths_done, length_ready, route_step, shifted_ready, exps_ready = (
                    sem("lengths_done"), sem("length_ready"), sem("route_step"), sem("shifted_ready"), sem("exps_ready"))
                moe_ready, moe_copied, reduced = sem("moe_ready"), sem("moe_copied"), sem("reduced")
                zt_ready, mixed_done = sem("zt_ready"), sem("mixed_done")
                mix_ready = [sem("mix_ready_act"), sem("mix_ready_dve")]
                mix_copied = [sem("mix_copied_act"), sem("mix_copied_dve")]
                L.extra_tokens_reader, L.extra_tokens_per = lengths_done, QT
                STEPS, NM, RING = 28, 24, 6

                with nc.Block() as block:
                    @block.sync
                    def _(sp):
                        sp_stream(nc, sp, L, NB)

                    @block.tensor
                    def _(pe):
                        wait_weights(pe, l)
                        pe.wait_ge(L.pads_zeroed, 3)
                        pe.wait_ge(squared, 1)
                        for k in range(KT):
                            last = nc.tensor.matmul(L.Z[:, 0:E], ones, sim_square[:, k, :], start=(k == 0), stop=(k == KT - 1))
                        last.then_inc(norm2_ready, 1)
                        pe.wait_ge(sim_ready, 1)

                        def project(b, first):
                            pe_transpose_tokens(nc, pe, L, b, first)
                            wait_items_copied(pe, L, b, 1)
                            for t in range(QT):
                                for k in range(KT):
                                    last = nc.tensor.matmul(L.J[0][:, E * t:E * t + E], L.xT[:, k, t * P:(t + 1) * P], sim_unit[:, k, :], start=(k == 0), stop=(k == KT - 1))
                            last.then_inc(L.item_ready[0], 1)
                            for m in range(NM):
                                t, kind, half = m // 6, m // 2 % 3, m % 2
                                pe.wait_ge(moe_copied, at(b, NM, m - RING + 1))
                                if m == RING - 1 and not first:
                                    pe.wait_ge(mixed_done, QT * b)
                                for k in range(KT):
                                    last = nc.tensor.matmul(banks[m % RING][:], L.xT[:, k, t * P:(t + 1) * P],
                                                            w["l0f_wqkv"][:, kind * KT + k, 512 * half:512 * half + 512], start=(k == 0), stop=(k == KT - 1))
                                last.then_inc(moe_ready, 1)

                        def attend(b):
                            pe.wait_ge(reduced, at(b, 12, 12))
                            pe.wait_ge(L.y_added, QT * b)
                            for kind, item in ((1, 3), (0, 4)):
                                e = item % 2
                                pe.wait_ge(L.item_copied[e], at(b, L.per[e], item // 2))
                                apart(pe, L.passed["pe"])
                                for t in range(QT):
                                    last = nc.tensor.transpose(L.J[e][0:d, t * P:(t + 1) * P], qkv[:, kind * QT + t, :], L.ident)
                                last.then_inc(L.item_ready[e], 1)
                            wait_items_copied(pe, L, b, 4)
                            pe.wait_ge(L.item_copied[1], at(b, 2, 2))
                            pe_attention(nc, pe, L, b)
                            pe.wait_ge(L.z_copied, b + 1)
                            apart(pe, L.passed["pe"])
                            for t in range(QT):
                                last = nc.tensor.transpose(L.Z[:, d * t:d * t + d], L.zT[0:d, 0, t * P:(t + 1) * P], L.ident[0:d, 0:d])
                            last.then_inc(zt_ready, 1)

                        def output(b, more):
                            pe.wait_ge(mixed_done, QT * (b + 1))
                            pe.wait_ge(L.item_copied[0], 3 * (b + 1) + 2 * more)
                            pe.wait_ge(L.item_copied[1], 2 * (b + 1) + more)
                            for c in range(8):
                                pe.wait_ge(mix_copied[c % 2], at(b, 4, c // 2))
                                for t in range(QT):
                                    last = nc.tensor.transpose(L.J[c % 2][:, t * P:(t + 1) * P], mixed[:, t, c * P:(c + 1) * P], L.ident)
                                last.then_inc(mix_ready[c % 2], 1)
                            for e in range(2):
                                pe.wait_ge(mix_copied[e], at(b, 4, 4))
                            pe_output(nc, pe, L, b, L.mixT, [w["l0f_wo"][:, c, :] for c in range(8)])

                        project(0, True)
                        with nc.Fori(0, NB - 1, engines=[ET.PE]) as b:
                            attend(b)
                            project(b + 1, False)
                            output(b, 1)
                        attend(NB - 1)
                        output(NB - 1, 0)

                    def copy_mixed(eng, e, b):
                        for c in range(e, 8, 2):
                            eng.wait_ge(mix_ready[e], at(b, 4, c // 2 + 1))
                            scale_copy(nc, e, L.mixT[:, c, :], L.J[e], 1.0).then_inc(mix_copied[e], 1)

                    @block.scalar
                    def _(act):
                        wait_weights(act, l)
                        nc.scalar.activation(sigmoid, w["l0f_gates"], ACT.Exp, scale=-1.0).then_inc(exp_gates_done, 1)

                        def project(b):
                            act.wait_ge(L.tokens_loaded, 16 * (b + 1))
                            act.wait_ge(length_ready, b)
                            for t in range(QT):
                                act.wait_ge(lengths_done, at(b, QT, t))
                                nc.scalar.activation(square, L.tokens[:, t, :], ACT.Square, accum_out=length2[:, t:t + 1]).then_inc(lengths_done, 1)
                            copy_transposed(nc, act, L, b, 0)
                            wait_item(act, L, b, 2)
                            nc.scalar.activation(raw, L.J[0][:, 0:QT * E].rearrange("p (t e) -> p t e", t=QT), ACT.Copy).then_inc(L.item_copied[0], 1)
                            act.wait_ge(shifted_ready, b + 1)
                            nc.scalar.activation(exps, shifted, ACT.Exp).then_inc(exps_ready, 1)

                        def attend(b):
                            wait_item(act, L, b, 4)
                            scale_copy(nc, 0, L.qT[0:d], L.J[0][0:d], d ** -0.5).then_inc(L.item_copied[0], 1)
                            act_attention(nc, act, L, b)

                        project(0)
                        with nc.Fori(0, NB - 1, engines=[ET.Activation]) as b:
                            attend(b)
                            project(b + 1)
                            copy_mixed(act, 0, b)
                        attend(NB - 1)
                        copy_mixed(act, 0, NB - 1)

                    @block.vector
                    def _(dve):
                        dve.wait_ge(consts_loaded, 32)
                        wait_weights(dve, l)
                        setup = [0]

                        def setup_do(ins):
                            setup[0] += 1
                            ins.then_inc(setup_step, 1)
                            dve.wait_ge(setup_step, setup[0])

                        dve.wait_ge(exp_gates_done, 1)
                        setup_do(nc.vector.tensor_scalar(sigmoid, sigmoid, 1.0, None, ALU.add))
                        setup_do(nc.vector.reciprocal(sigmoid, sigmoid))
                        dve.wait_ge(norm2_ready, 1)
                        nc.vector.tensor_copy(sim_norm, L.Z[:, 0:E]).then_inc(norm2_ready, 1)
                        dve.wait_ge(norm_done, 1)
                        setup_do(nc.vector.tensor_scalar(sim_norm, sim_norm, 1e-12, None, ALU.max))
                        setup_do(nc.vector.reciprocal(sim_inverse, sim_norm))
                        nc.vector.tensor_tensor(sim_unit, w["l0f_sim"], sim_inverse.unsqueeze(1).broadcast_to([P, KT, E]), ALU.mult).then_inc(sim_ready, 1)

                        def project(b):
                            copy_transposed(nc, dve, L, b, 1)
                            steps = [0]

                            def step(ins):
                                steps[0] += 1
                                ins.then_inc(route_step, 1)
                                dve.wait_ge(route_step, at(b, STEPS, steps[0]))
                                apart(dve, L.passed["dve"])

                            dve.wait_ge(length_ready, b + 1)
                            step(nc.vector.tensor_scalar(length, length, 1e-12, None, ALU.max))
                            step(nc.vector.reciprocal(inv_length, length))
                            dve.wait_ge(L.item_copied[0], at(b, 3, 2))
                            for t in range(QT):
                                step(nc.vector.scalar_tensor_tensor(logits[:, t, :], raw[:, t, :], inv_length[:, t:t + 1], sigmoid, ALU.mult, ALU.subtract))
                            for t in range(QT):
                                step(nc.vector.max(top[:, t, :], logits[:, t, :]))
                            for t in range(QT):
                                step(nc.vector.max_index(index[:, t, :], top[:, t, :], logits[:, t, :]))
                            step(nc.vector.tensor_scalar(active, logits, 0.0, None, ALU.is_gt))
                            step(nc.vector.tensor_scalar(gated, logits, 0.0, None, ALU.max))
                            step(nc.vector.tensor_scalar(peak, top[:, :, 0], 0.0, None, ALU.max))
                            nc.vector.tensor_tensor(shifted, gated, peak.unsqueeze(2).broadcast_to([P, QT, E]), ALU.subtract).then_inc(shifted_ready, 1)
                            step(nc.vector.tensor_scalar(idle, top[:, :, 0], 0.0, None, ALU.is_le))
                            step(nc.vector.tensor_copy(index_f, index))
                            ids = iota[:, 0:E].unsqueeze(1).broadcast_to([P, QT, E])
                            step(nc.vector.tensor_tensor(fallback, ids, index_f[:, :, 0:1].broadcast_to([P, QT, E]), ALU.is_equal))
                            step(nc.vector.tensor_tensor(fallback2, ids, index_f[:, :, 1:2].broadcast_to([P, QT, E]), ALU.is_equal))
                            step(nc.vector.tensor_tensor(fallback, fallback, fallback2, ALU.add))
                            step(nc.vector.tensor_tensor(fallback, fallback, idle.unsqueeze(2).broadcast_to([P, QT, E]), ALU.mult))
                            step(nc.vector.tensor_tensor(active, active, fallback, ALU.add))
                            dve.wait_ge(exps_ready, b + 1)
                            step(nc.vector.tensor_tensor(masked, exps, active, ALU.mult))
                            step(nc.vector.tensor_reduce(total, masked, AX, ALU.add))
                            step(nc.vector.reciprocal(inverse, total))
                            step(nc.vector.tensor_tensor(weights_, masked, inverse.unsqueeze(2).broadcast_to([P, QT, E]), ALU.mult))
                            assert steps[0] == STEPS, steps[0]
                            for m in range(NM):
                                t, kind, half = m // 6, m // 2 % 3, m % 2
                                dve.wait_ge(moe_ready, at(b, NM, m + 1))
                                part = product[m // 2 % 2][:, 8 * half:8 * half + 8, :]
                                nc.vector.tensor_tensor(part, banks[m % RING][:].rearrange("p (e d) -> p e d", e=8),
                                                        weights_[:, t, 8 * half:8 * half + 8].unsqueeze(2).broadcast_to([P, 8, d]), ALU.mult).then_inc(moe_copied, 1)
                                if half == 1:
                                    dve.wait_ge(moe_copied, at(b, NM, m + 1))
                                    nc.vector.tensor_reduce(qkv[:, kind * QT + t, :], product[m // 2 % 2].rearrange("p e d -> p d e"), AX, ALU.add).then_inc(reduced, 1)

                        def attend(b):
                            wait_item(dve, L, b, 3)
                            scale_copy(nc, 1, L.kT[0:d], L.J[1][0:d], 1.0).then_inc(L.item_copied[1], 1)
                            dve_attention(nc, dve, L, b)
                            dve.wait_ge(zt_ready, b + 1)
                            for t in range(QT):
                                nc.vector.tensor_tensor(mixed[:, t, :].rearrange("p (e d) -> p e d", e=E),
                                                        L.Z[:, d * t:d * t + d].unsqueeze(1).broadcast_to([P, E, d]),
                                                        weights_[:, t, :].unsqueeze(2).broadcast_to([P, E, d]), ALU.mult).then_inc(mixed_done, 1)

                        project(0)
                        with nc.Fori(0, NB - 1, engines=[ET.DVE]) as b:
                            attend(b)
                            project(b + 1)
                            copy_mixed(dve, 1, b)
                            dve_norm(nc, dve, L, b)
                        attend(NB - 1)
                        copy_mixed(dve, 1, NB - 1)
                        dve_norm(nc, dve, L, NB - 1)

                    @block.gpsimd
                    def _(pool):
                        nc.gpsimd.memset(ones, 1.0).then_inc(L.pads_zeroed, 1)
                        nc.gpsimd.memset(L.qT, 0.0).then_inc(L.pads_zeroed, 1)
                        nc.gpsimd.memset(L.kT, 0.0).then_inc(L.pads_zeroed, 1)
                        nc.gpsimd.memset(halves, 0.5).then_inc(L.pads_zeroed, 1)
                        wait_weights(pool, l)
                        nc.gpsimd.tensor_tensor(sim_square, w["l0f_sim"], w["l0f_sim"], ALU.mult).then_inc(squared, 1)
                        pool.wait_ge(L.pads_zeroed, 4)
                        pool.wait_ge(norm2_ready, 2)
                        nc.gpsimd.tensor_tensor(sim_norm, sim_norm, halves, ALU.pow).then_inc(norm_done, 1)

                        def lengths(b):
                            pool.wait_ge(lengths_done, QT * (b + 1))
                            nc.gpsimd.tensor_tensor(length, length2, halves[:, 0:QT], ALU.pow).then_inc(length_ready, 1)

                        lengths(0)
                        with nc.Fori(0, NB - 1, engines=[ET.Pool]) as b:
                            pool_attention(nc, pool, L, b)
                            lengths(b + 1)
                            pool_rstd(nc, pool, L, b)
                        pool_attention(nc, pool, L, NB - 1)
                        pool_rstd(nc, pool, L, NB - 1)

        def windowed_attention(l):
            w = W[l]
            H, d, NA, NT, LAG = 16, 16, 28, 4, 20
            U = QT * H
            with nc.cleanup_on_exit():
                L = common(l, [7, 6], w["l1a_bo"].unsqueeze(1).broadcast_to([P, QT, D]))
                sem = L.sem
                take = carve(arena)
                L.eT, L.ez, L.v, L.zT = take(2, T), take(H, T), take(QT, 32 * H), take(4, T)
                probs, probsT, tanhs, LT = take(P_SLOTS, 2 * P), take(2, QT * 2 * P), take(NT, 2 * P), take(T)
                g, unit, ones = take(QT, D), take(QT, D), take(P)
                halves, norm2, norm, floor, inv_norm, ln_norm, half_ln = (take(U) for _ in range(7))
                rowsum, inv_denom, fit, sums, rinv = (take(U) for _ in range(5))
                denom_sum, denom_inv = take(QT), take(QT)
                corr = take_rest_of_odd(NA, 2 * P)
                S, LB, TB, Z, stat = [banks[0][:], banks[1][:]], banks[2][:], [banks[3][:], banks[4][:]], banks[5][:], banks[7][:, 0:16]
                zeroed, squared, norm2_ready, norm_ready, floor_ready, ln_ready, half_ready, unit_ready, chain = (
                    sem(n) for n in ("zeroed", "squared", "norm2_ready", "norm_ready", "floor_ready", "ln_ready", "half_ready", "unit_ready", "chain"))
                lb_ready, dot_ready, tanh_done, tanh_masked, corr_done, corr_masked, inv_ready, stat_ready, fit_ready, stat_step = (
                    sem(n) for n in ("lb_ready", "dot_ready", "tanh_done", "tanh_masked", "corr_done", "corr_masked", "inv_ready", "stat_ready", "fit_ready", "stat_step"))
                exp_done, rinv_ready, probs_ready, probsT_ready, probsT_copied, values_done, z_copied = (
                    sem(n) for n in ("exp_done", "rinv_ready", "probs_ready", "probsT_ready", "probsT_copied", "values_done", "z_copied"))

                def first_col(u):
                    return P if u % QT == 0 else 0

                with nc.Block() as block:
                    @block.sync
                    def _(sp):
                        sp_stream(nc, sp, L, NB)

                    @block.tensor
                    def _(pe):
                        wait_weights(pe, l)
                        pe.wait_ge(zeroed, 3)

                        def project(b, first):
                            pe_transpose_tokens(nc, pe, L, b, first)
                            wait_items_copied(pe, L, b, 1)
                            for t in range(QT):
                                for j, wt in enumerate((w["l1a_wv"], w["l1a_wg"])):
                                    pe_item(nc, pe, L, b, 2 + 2 * t + j, L.J[j][:, 0:D], [(L.xT[:, k, t * P:(t + 1) * P], wt[:, k, :]) for k in range(KT)])

                        def turn(b):
                            pe.wait_ge(unit_ready, b + 1)
                            pe.wait_ge(L.y_added, QT * b)
                            for c in range(2):
                                pe.wait_ge(L.item_copied[c], at(b, L.per[c], 5))
                                for t in range(QT):
                                    last = nc.tensor.transpose(L.J[c][:, t * P:(t + 1) * P], unit[:, t, c * P:(c + 1) * P], L.ident)
                                last.then_inc(L.item_ready[c], 1)
                            pe.wait_ge(L.item_copied[0], at(b, 7, 6))
                            pe.wait_ge(half_ready, b + 1)
                            apart(pe, L.passed["pe"])
                            for t in range(QT):
                                last = nc.tensor.transpose(L.J[0][0:H, t * P:(t + 1) * P], half_ln[:, H * t:H * t + H], L.ident)
                            last.then_inc(L.item_ready[0], 1)

                        def attend(b):
                            wait_items_copied(pe, L, b, 12)

                            def dots(u):
                                h, qt = divmod(u, QT)
                                if qt == 0:
                                    pe.wait_ge(tanh_done, at(b, U, u))
                                    nc.tensor.matmul(LB, w["l1a_head_rows"][:, h, :], LT, start=True, stop=True).then_inc(lb_ready, 1)
                                c0 = first_col(u)
                                pe.wait_ge(corr_done, at(b, U, u - 1))
                                nc.tensor.matmul(S[u % 2][:, c0:2 * P], L.eT[:, h // 8, qt * P:(qt + 1) * P],
                                                 L.ez[:, h, (qt - 1) * P + c0:(qt + 1) * P], start=True, stop=True).then_inc(dot_ready, 1)

                            def transposes(u):
                                pe.wait_ge(probs_ready, at(b, U, u + 1))
                                pe.wait_ge(probsT_copied, at(b, U, u - 1))
                                for c in range(first_col(u), 2 * P, P):
                                    last = nc.tensor.transpose(TB[u % 2][:, c:c + P], probs[:, u % P_SLOTS, c:c + P], L.ident)
                                last.then_inc(probsT_ready, 1)

                            def values(h):
                                pe.wait_ge(probsT_copied, at(b, U, QT * h + QT))
                                j = h % 4
                                if j == 0:
                                    pe.wait_ge(z_copied, at(b, 4, h // 4))
                                for k in range(QT):
                                    n = min(2 * P, T - k * P)
                                    last = nc.tensor.matmul(Z[32 * j:32 * j + 32, k * P:k * P + n], L.v[:, k, 32 * h:32 * h + 32],
                                                            probsT[:, h % 2, 2 * P * k:2 * P * k + n], start=(k == 0), stop=(k == QT - 1), skip_group_check=True)
                                last.then_inc(values_done, 1)

                            for s in range(U + LAG + PV_LAG + 1):
                                if s < U:
                                    dots(s)
                                if s % 16 == 2 and 16 < s <= U + 2:
                                    n = s // 16 - 1
                                    pe.wait_ge(inv_ready, at(b, 4, n + 1))
                                    nc.tensor.matmul(stat, ones, inv_denom[:, 16 * n:16 * n + 16], start=True, stop=True).then_inc(stat_ready, 1)
                                if LAG <= s < U + LAG:
                                    transposes(s - LAG)
                                if s > LAG and (s - LAG - 1) % QT == QT - 1 and s - LAG - 1 < U:
                                    values((s - LAG - 1) // QT)

                        def output(b, more):
                            pe.wait_ge(z_copied, at(b, 4, 4))
                            pe.wait_ge(L.item_copied[0], 7 * (b + 1) + 5 * more)
                            pe.wait_ge(L.item_copied[1], 6 * (b + 1) + 5 * more)
                            pe_output(nc, pe, L, b, L.zT, [w["l1a_wo"][:, c, :] for c in range(4)])

                        project(0, True)
                        turn(0)
                        with nc.Fori(0, NB - 1, engines=[ET.PE]) as b:
                            attend(b)
                            project(b + 1, False)
                            output(b, 1)
                            turn(b + 1)
                        attend(NB - 1)
                        output(NB - 1, 0)

                    def copy_units(eng, e, b):
                        wait_item(eng, L, b, 10 + e)
                        scale_copy(nc, e, L.eT[:, e, :], L.J[e], 1.0)
                        for j in range(8):
                            last = scale_copy(nc, e, L.ez[:, 8 * e + j, :], L.J[e], head_mask[:, j:j + 1])
                        last.then_inc(L.item_copied[e], 1)

                    @block.scalar
                    def _(act):
                        act.wait_ge(consts_loaded, 32)
                        act.wait_ge(zeroed, 3)

                        def project(b):
                            copy_transposed(nc, act, L, b, 0)
                            for t in range(QT):
                                wait_item(act, L, b, 2 + 2 * t)
                                scale_copy(nc, 0, L.v[:, t, :].rearrange("p (h c) -> p h c", c=32)[:, :, 0:d],
                                           L.J[0][:, 0:D].rearrange("p (h c) -> p h c", c=d), 1.0).then_inc(L.item_copied[0], 1)
                            act.wait_ge(floor_ready, b + 1)
                            nc.scalar.activation(ln_norm, floor, ACT.Ln, scale=1e4).then_inc(ln_ready, 1)

                        def turn(b):
                            copy_units(act, 0, b)
                            wait_item(act, L, b, 12)
                            nc.scalar.activation(LT[0:H], L.J[0][0:H], ACT.Copy).then_inc(L.item_copied[0], 1)

                        def attend(b):
                            for s in range(U + LAG + PV_LAG):
                                if s < U:
                                    h, qt = divmod(s, QT)
                                    c0 = first_col(s)
                                    act.wait_ge(lb_ready, at(b, H, h + 1))
                                    act.wait_ge(corr_done, at(b, U, s - NT + 1))
                                    nc.scalar.activation(tanhs[:, s % NT, c0:2 * P], LB[:, (qt - 1) * P + c0:(qt + 1) * P], ACT.Tanh,
                                                         bias=half_ln[:, H * qt + h:H * qt + h + 1]).then_inc(tanh_done, 1)
                                v = s - LAG
                                if 0 <= v < U:
                                    c0 = first_col(v)
                                    act.wait_ge(fit_ready, at(b, 4, v // 16 + 1))
                                    act.wait_ge(corr_masked, at(b, U, v + 1))
                                    act.wait_ge(probsT_ready, at(b, U, v - P_SLOTS + 1))
                                    nc.scalar.activation(probs[:, v % P_SLOTS, c0:2 * P], corr[:, v % NA, c0:2 * P], ACT.Exp,
                                                         scale=fit[:, v:v + 1], accum_out=sums[:, v:v + 1]).then_inc(exp_done, 1)
                                v = s - LAG - PV_LAG + 1
                                if 0 <= v < U:
                                    h, qt = divmod(v, QT)
                                    c0 = first_col(v)
                                    x0 = 2 * P * qt - P + c0
                                    act.wait_ge(probsT_ready, at(b, U, v + 1))
                                    act.wait_ge(values_done, at(b, H, h - 1))
                                    nc.scalar.activation(probsT[:, h % 2, x0:x0 + 2 * P - c0], TB[v % 2][:, c0:2 * P], ACT.Copy).then_inc(probsT_copied, 1)

                        project(0)
                        turn(0)
                        with nc.Fori(0, NB - 1, engines=[ET.Activation]) as b:
                            attend(b)
                            project(b + 1)
                            turn(b + 1)
                        attend(NB - 1)

                    @block.vector
                    def _(dve):
                        wait_weights(dve, l)
                        dve.wait_ge(consts_loaded, 32)

                        def project(b):
                            copy_transposed(nc, dve, L, b, 1)
                            for t in range(QT):
                                wait_item(dve, L, b, 3 + 2 * t)
                                nc.vector.tensor_tensor(g[:, t, :], L.J[1][:, 0:D], w["l1a_bg"], ALU.add).then_inc(L.item_copied[1], 1)
                            dve.wait_ge(squared, b + 1)
                            nc.vector.tensor_reduce(norm2, unit.rearrange("p t (h c) -> p (t h) c", c=d), AX, ALU.add).then_inc(norm2_ready, 1)
                            dve.wait_ge(norm_ready, b + 1)
                            nc.vector.tensor_scalar(floor, norm, 1e-19, None, ALU.max).then_inc(floor_ready, 1)
                            dve.wait_ge(floor_ready, b + 1)
                            nc.vector.reciprocal(inv_norm, floor).then_inc(chain, 1)
                            dve.wait_ge(chain, b + 1)
                            nc.vector.tensor_tensor(unit.rearrange("p t (h c) -> p (t h) c", c=d), g.rearrange("p t (h c) -> p (t h) c", c=d),
                                                    inv_norm.unsqueeze(2).broadcast_to([P, U, d]), ALU.mult).then_inc(unit_ready, 1)
                            dve.wait_ge(ln_ready, b + 1)
                            nc.vector.tensor_scalar(half_ln, ln_norm, 0.5, None, ALU.mult).then_inc(half_ready, 1)

                        def attend(b):
                            def stats(n):
                                part = inv_denom[:, 16 * n:16 * n + 16]
                                dve.wait_ge(corr_done, at(b, U, 16 * n + 16))
                                nc.vector.tensor_scalar(part, rowsum[:, 16 * n:16 * n + 16], 1.0 / (4 * T), 1.0, ALU.mult, ALU.add).then_inc(stat_step, 1)
                                dve.wait_ge(stat_step, at(b, 12, 3 * n + 1))
                                nc.vector.reciprocal(part, part).then_inc(inv_ready, 1)

                            def fitness(n):
                                dve.wait_ge(stat_ready, at(b, 4, n + 1))
                                nc.vector.tensor_reduce(denom_sum, stat.rearrange("p (h q) -> p h q", h=4), AX, ALU.add).then_inc(stat_step, 1)
                                dve.wait_ge(stat_step, at(b, 12, 3 * n + 2))
                                nc.vector.reciprocal(denom_inv, denom_sum).then_inc(stat_step, 1)
                                dve.wait_ge(stat_step, at(b, 12, 3 * n + 3))
                                nc.vector.scalar_tensor_tensor(fit[:, 16 * n:16 * n + 16].rearrange("p (h q) -> p h q", h=4),
                                                               inv_denom[:, 16 * n:16 * n + 16].rearrange("p (h q) -> p h q", h=4), 0.25,
                                                               denom_inv.unsqueeze(2).broadcast_to([P, 4, QT]), ALU.mult, ALU.mult).then_inc(fit_ready, 1)

                            for s in range(U + LAG + PV_LAG + 3):
                                u = s - 1
                                if 0 <= u < U:
                                    c0 = first_col(u)
                                    dve.wait_ge(dot_ready, at(b, U, u + 1))
                                    dve.wait_ge(tanh_masked, at(b, U, u + 1))
                                    dve.wait_ge(exp_done, at(b, U, u - NA + 1))
                                    nc.vector.scalar_tensor_tensor(corr[:, u % NA, c0:2 * P], tanhs[:, u % NT, c0:2 * P], 1.0, S[u % 2][:, c0:2 * P],
                                                                   ALU.add, ALU.mult, accum_out=rowsum[:, u:u + 1]).then_inc(corr_done, 1)
                                    if u % 16 == 15:
                                        stats(u // 16)
                                if s % 16 == 3 and 16 < s <= U + 3:
                                    fitness(s // 16 - 1)
                                v = s - LAG - 1
                                if 0 <= v < U:
                                    c0 = first_col(v)
                                    dve.wait_ge(exp_done, at(b, U, v + 1))
                                    nc.vector.reciprocal(rinv[:, v:v + 1], sums[:, v:v + 1]).then_inc(rinv_ready, 1)
                                    dve.wait_ge(rinv_ready, at(b, U, v + 1))
                                    pr = probs[:, v % P_SLOTS, c0:2 * P]
                                    nc.vector.tensor_scalar(pr, pr, rinv[:, v:v + 1], None, ALU.mult).then_inc(probs_ready, 1)
                                v = s - LAG - 3
                                if 0 <= v < U and v % 16 == 15:
                                    n = v // 16
                                    dve.wait_ge(values_done, at(b, H, 4 * n + 4))
                                    nc.vector.tensor_scalar(L.zT[:, n, :], Z, w["l1a_bv"][:, n:n + 1], None, ALU.add).then_inc(z_copied, 1)

                        project(0)
                        copy_units(dve, 1, 0)
                        with nc.Fori(0, NB - 1, engines=[ET.DVE]) as b:
                            attend(b)
                            project(b + 1)
                            dve_norm(nc, dve, L, b)
                            copy_units(dve, 1, b + 1)
                        attend(NB - 1)
                        dve_norm(nc, dve, L, NB - 1)

                    @block.gpsimd
                    def _(pool):
                        nc.gpsimd.memset(L.v, 0.0).then_inc(zeroed, 1)
                        nc.gpsimd.memset(LT, 0.0).then_inc(zeroed, 1)
                        nc.gpsimd.memset(ones, 1.0).then_inc(zeroed, 1)
                        nc.gpsimd.memset(halves, 0.5).then_inc(zeroed, 1)
                        pool.wait_ge(zeroed, 4)
                        wait_weights(pool, l)

                        def norms(b):
                            pool.wait_ge(L.item_copied[1], at(b, 6, 5))
                            nc.gpsimd.tensor_tensor(unit, g, g, ALU.mult).then_inc(squared, 1)
                            pool.wait_ge(norm2_ready, b + 1)
                            nc.gpsimd.tensor_tensor(norm, norm2, halves, ALU.pow).then_inc(norm_ready, 1)

                        def mask(tile, u, fill):
                            ins = nc.gpsimd.affine_select(out=tile[:, P:2 * P], in_=tile[:, P:2 * P], compare_op=ALU.is_ge, fill=fill,
                                                          base=0, pattern=[[-1, P]], channel_multiplier=1)
                            if u % QT:
                                ins = nc.gpsimd.affine_select(out=tile[:, 0:P], in_=tile[:, 0:P], compare_op=ALU.is_ge, fill=fill,
                                                              base=0, pattern=[[1, P]], channel_multiplier=-1)
                            return ins

                        def attend(b):
                            for s in range(U + 2):
                                if s < U:
                                    pool.wait_ge(tanh_done, at(b, U, s + 1))
                                    apart(pool, L.passed["pool"])
                                    mask(tanhs[:, s % NT, :], s, no_tanh).then_inc(tanh_masked, 1)
                                if s >= 2:
                                    pool.wait_ge(corr_done, at(b, U, s - 1))
                                    apart(pool, L.passed["pool"])
                                    mask(corr[:, (s - 2) % NA, :], s - 2, no_prob).then_inc(corr_masked, 1)

                        no_tanh, no_prob = nc.gpsimd.to_reg(-1.0), nc.gpsimd.to_reg(-1e30)
                        norms(0)
                        with nc.Fori(0, NB - 1, engines=[ET.Pool]) as b:
                            pool_bias(nc, pool, L, b, False)
                            attend(b)
                            norms(b + 1)
                            pool_rstd(nc, pool, L, b)
                        pool_bias(nc, pool, L, NB - 1, False)
                        attend(NB - 1)
                        pool_rstd(nc, pool, L, NB - 1)

        with nc.Block() as block:
            @block.sync
            def _(sp):
                nc.sync.dma_start(consts[:, 0:a["consts"].shape[1]], a["consts"]).then_inc(consts_loaded, 16)
                nc.sync.dma_start(arena[:, 0:P], a["future"]).then_inc(consts_loaded, 16)
                load_weights(sp, layers[0])

            @block.vector
            def _(dve):
                dve.wait_ge(consts_loaded, 32)
                nc.vector.tensor_copy(ident_bf, ident)
                nc.vector.tensor_copy(future, arena[:, 0:P])

        for l in layers:
            if l == 0:
                wide_attention(0, 16, 8, True, False)
            if l == 1:
                wide_attention(1, 8, 8, False, True)
            if l == 2:
                mixture_attention(2)
            if l == 3:
                windowed_attention(3)
            if l == 4:
                narrow_cross_attention(4)
            if l == 5:
                gated_experts(5)




def lay_out(inputs):
    import numpy as np
    i = {k: np.ascontiguousarray(v) for k, v in inputs.items()}

    def tiles(w, p=128):
        k, n = w.shape
        return np.ascontiguousarray(w.reshape(k // p, p, n).transpose(1, 0, 2).reshape(p, -1))

    def rows(v):
        return np.ascontiguousarray(np.broadcast_to(v[None, :], (128, v.shape[0])))

    order = [4 * p + r + 2 * j for p in range(4) for r in range(2) for j in range(2)]
    a = {"x": i["x"], "ctxT": np.ascontiguousarray(i["ctx_768"].transpose(0, 2, 1))}
    a["l0a_wq"] = tiles(i["L0_attn_W_Q"][:, order].reshape(256, -1))
    a["l0a_wk"] = tiles(i["L0_attn_W_K"].reshape(256, -1))
    a["l0a_wv"] = tiles(i["L0_attn_W_V"].reshape(256, -1))
    a["l0a_wo"] = tiles(np.ascontiguousarray(i["L0_attn_W_out"].transpose(1, 0, 2)[order]).reshape(1024, 256))
    a["l0a_bo"] = rows(i["L0_attn_b_out"])
    a["l0x_wq"] = tiles(i["L0_xattn_Wq"])
    a["l0x_wk"] = tiles(i["L0_xattn_Wk"], 96)
    a["l0x_wv"] = tiles(i["L0_xattn_Wv"], 96)
    a["l0x_wo"] = tiles(i["L0_xattn_Wout"])
    a["l0x_bo"] = rows(i["L0_xattn_bout"])
    pad = lambda w: np.concatenate([w.reshape(16, 16, -1), np.zeros((16, 16, w.shape[1]), w.dtype)], 1).reshape(512, -1)
    a["l1x_wq"] = tiles(i["L1_xattn_Wq"])
    a["l1x_wk"] = tiles(i["L1_xattn_Wk"], 96)
    a["l1x_wv"] = tiles(i["L1_xattn_Wv"], 96)
    a["l1x_w1"] = tiles(pad(i["L1_xattn_W1"]))
    a["l1x_w2"] = tiles(i["L1_xattn_W2"])
    a["l1x_bq"] = np.ascontiguousarray(i["L1_xattn_bq"].reshape(2, 128).T)
    a["l1x_bk"] = np.ascontiguousarray(i["L1_xattn_bk"].reshape(2, 128).T)
    padcol = lambda v: np.ascontiguousarray(np.concatenate([v.reshape(16, 16), np.zeros((16, 16), v.dtype)], 1).reshape(4, 128).T)
    a["l1x_bv"] = padcol(i["L1_xattn_bv"])
    a["l1x_b1"] = np.ascontiguousarray(i["L1_xattn_b1"].reshape(4, 128).T)
    a["l1x_b2"] = rows(i["L1_xattn_b2"])
    qkv = [i["L0_ffn_" + n].transpose(1, 0, 2).reshape(256, 1024) for n in ("q_proj", "k_proj", "v_proj")]
    a["l0f_wqkv"] = np.ascontiguousarray(np.concatenate([tiles(m) for m in qkv], 1))
    a["l0f_wo"] = tiles(i["L0_ffn_o_proj"].reshape(1024, 256))
    a["l0f_sim"] = tiles(i["L0_ffn_sim_matrix"])
    a["l0f_gates"] = rows(i["L0_ffn_gates"])
    a["l1a_wg"] = tiles(np.ascontiguousarray(i["L1_attn_Wg"].T))
    a["l1a_wv"] = tiles(np.ascontiguousarray(i["L1_attn_Wv"].T))
    a["l1a_wo"] = tiles(pad(np.ascontiguousarray(i["L1_attn_Wo"].T)))
    a["l1a_bg"] = rows(i["L1_attn_bg"])
    a["l1a_bv"] = padcol(i["L1_attn_bv"])
    a["l1a_bo"] = rows(i["L1_attn_bo"])
    sel = np.zeros((128, 16, 128), np.float32)
    for h in range(16):
        sel[h, h, :] = 1
    a["l1a_head_rows"] = sel.reshape(128, -1)
    W1, Ws1 = i["L1_ffn_W1"], i["L1_ffn_Ws1"]
    down = np.concatenate([i["L1_ffn_W2"].transpose(0, 2, 1).reshape(-1, 256), i["L1_ffn_Ws2"].T], 0)
    a["l1f_wy"] = tiles(np.ascontiguousarray(np.concatenate([W1[:, :192].reshape(-1, 256), Ws1[:384]], 0).T))
    a["l1f_wg"] = tiles(np.ascontiguousarray(np.concatenate([W1[:, 192:].reshape(-1, 256), Ws1[384:]], 0).T))
    a["l1f_w2"] = tiles(np.ascontiguousarray(down))
    a["l1f_gate"] = tiles(np.ascontiguousarray(i["L1_ffn_gate_w"].T))
    sel = np.zeros((128, 12 * 128), np.float32)
    m = np.arange(12 * 128)
    sel[m // 192, m] = 1
    a["l1f_expert_rows"] = sel
    c = np.zeros((128, 158), np.float32)
    r = np.arange(128)
    c[r, r] = 1
    for j in range(2):
        c[64 * j:64 * j + 64, 128 + j] = 1
    for j in range(8):
        c[16 * j:16 * j + 16, 130 + j] = 1
    c[:, 138:142] = -0.5
    c[:, 142:158] = np.arange(16)
    a["consts"] = c
    a["future"] = np.where(r[None, :] > r[:, None], -1e30, 0).astype(np.float32)
    return a




def kernel(**inputs):
    import numpy as _np
    import concourse.bacc as _bacc
    from concourse import mybir as _mybir
    from concourse.bass_utils import run_bass_kernel_spmd as _run

    nc = _bacc.Bacc("TRN2", target_bir_lowering=False, num_devices=1)
    arrays, aps = {}, {}
    for name, a in lay_out(inputs).items():
        arrays[f"in_{name}_dram"] = a
        aps[name] = nc.dram_tensor(f"in_{name}_dram", a.shape, _mybir.dt.from_np(a.dtype), kind="ExternalInput").ap()
    shape = inputs["x"].shape
    out = nc.dram_tensor("out_0_dram", shape, _mybir.dt.float32, kind="ExternalOutput").ap()
    build(nc, aps, out)
    r = _run(nc, [arrays], core_ids=[0])
    return _np.asarray(r.results[0]["out_0_dram"])
```

```python
import math
from contextlib import ExitStack

import concourse.bass as bass
from concourse import mybir

F32 = mybir.dt.float32
BF16 = mybir.dt.bfloat16
FP32R = mybir.dt.float32r
U32 = mybir.dt.uint32
ALU = mybir.AluOpType
ACT = mybir.ActivationFunctionType
AX = mybir.AxisListType.X

P = 128
T = 512
D = 256
QT = T // P
KT = D // P
LN_EPS = 1e-5
S_BANKS, P_SLOTS = 3, 5
T_LAG, PV_LAG = 3, 4
ARENA = 25600


def at(b, per, k):
    return b * per + max(k, 0)


class Names:
    pass




def apart(eng, passed):
    eng.sem_inc(passed, 1)


def sp_stream(nc, sp, L, NB):


    def load_tokens(b, first=False):
        if not first:
            sp.wait_ge(L.item_ready[0], at(b, L.per[0], 0) - L.per[0] + 1)
            sp.wait_ge(L.item_ready[1], at(b, L.per[1], 0) - L.per[1] + 1)
            apart(sp, L.passed["sp"])
            if L.extra_tokens_reader is not None:
                sp.wait_ge(L.extra_tokens_reader, b * L.extra_tokens_per)
        nc.sync.dma_start(L.tokens, L.x_in(b)).then_inc(L.tokens_loaded, 16)

    def load_context(b, first=False):
        if not first:
            for e in range(2):
                sp.wait_ge(L.item_ready[e], b * L.per[e])
        nc.sync.dma_start(L.context, L.ctx_in(b)).then_inc(L.context_loaded, 16)

    def load_residual(b, first=False):
        if not first:
            sp.wait_ge(L.y_added, b * QT)
            apart(sp, L.passed["sp"])
        nc.sync.dma_start(L.residual, L.x_in(b)).then_inc(L.residual_loaded, 16)

    def store(b):
        sp.wait_ge(L.normed, (b + 1) * QT)
        apart(sp, L.passed["sp"])
        nc.sync.dma_start(L.x_out(b), L.result).then_inc(L.stored, 16)

    load_tokens(0, True)
    if L.ctx_in is not None:
        load_context(0, True)
    load_residual(0, True)
    L.load_next_weights(sp)
    with nc.Fori(0, NB - 1, engines=[mybir.EngineType.SP]) as b:
        load_tokens(b + 1)
        if L.ctx_in is not None:
            load_context(b + 1)
        load_residual(b + 1)
        store(b)
    store(NB - 1)
    sp.wait_ge(L.stored, 16 * NB)


def pe_transpose_tokens(nc, pe, L, b, first):
    pe.wait_ge(L.tokens_loaded, 16 * (b + 1))
    if not first:
        pe.wait_ge(L.y_added, QT * (b - 1))
    for k in range(KT):
        pe.wait_ge(L.item_copied[k % 2], at(b, L.per[k % 2], 0))
        for t in range(QT):
            last = nc.tensor.transpose(L.J[k % 2][:, t * P:(t + 1) * P], L.tokens[:, t, k * P:(k + 1) * P], L.ident)
        last.then_inc(L.item_ready[k % 2], 1)


def pe_item(nc, pe, L, b, n, out, parts):
    e = n % 2
    pe.wait_ge(L.item_copied[e], at(b, L.per[e], n // 2))
    for i, (w, x) in enumerate(parts):
        last = nc.tensor.matmul(out, w, x, start=(i == 0), stop=(i == len(parts) - 1))
    last.then_inc(L.item_ready[e], 1)


def wait_item(eng, L, b, n):
    eng.wait_ge(L.item_ready[n % 2], at(b, L.per[n % 2], n // 2 + 1))


def wait_items_copied(eng, L, b, n):
    for e in range(2):
        eng.wait_ge(L.item_copied[e], at(b, L.per[e], (n - e) // 2 + 1))


def wait_banks_free(eng, L, rows):
    for e in range(2):
        eng.wait_ge(L.item_copied[e], rows * L.per[e])


def affine_copy(nc, e, out, in_, scale, bias):
    if e == 0:
        return nc.scalar.activation(out, in_, ACT.Identity, bias=bias, scale=scale)
    return nc.vector.tensor_scalar(out, in_, scale, bias, ALU.mult, ALU.add)


def scale_copy(nc, e, out, in_, scale):
    if e == 0:
        return nc.scalar.activation(out, in_, ACT.Identity, scale=scale)
    return nc.vector.tensor_scalar(out, in_, scale, None, ALU.mult)


def copy_transposed(nc, eng, L, b, e):
    wait_item(eng, L, b, e)
    scale_copy(nc, e, L.xT[:, e, :], L.J[e], 1.0).then_inc(L.item_copied[e], 1)




def pe_output(nc, pe, L, b, z, wo):
    n = len(wo)
    for t in range(QT):
        if t >= 2:
            pe.wait_ge(L.y_added, at(b, QT, t - 1))
        for c in range(n):
            last = nc.tensor.matmul(L.J[t % 2][:, 0:D], z[:, c, t * P:(t + 1) * P], wo[c], start=(c == 0), stop=(c == n - 1))
        last.then_inc(L.y_ready, 1)


def pool_bias(nc, pool, L, b):
    pool.wait_ge(L.residual_loaded, 16 * (b + 1))
    nc.gpsimd.tensor_tensor(L.residual, L.residual, L.bias, ALU.add).then_inc(L.residual_biased, 1)


def dve_add(nc, dve, L, b):
    if L.bias is not None:
        dve.wait_ge(L.residual_biased, b + 1)
    else:
        dve.wait_ge(L.residual_loaded, 16 * (b + 1))
    for t in range(QT):
        dve.wait_ge(L.y_ready, at(b, QT, t + 1))
        nc.vector.tensor_tensor(L.h[:, t, :], L.J[t % 2][:, 0:D], L.residual[:, t, :], ALU.add).then_inc(L.y_added, 1)


def dve_moments(nc, dve, L, b):
    for t in range(QT):
        dve.wait_ge(L.y_added, at(b, QT, t + 1))
        nc.vector.bn_stats(L.stats[:, t, :], L.h[:, t, :]).then_inc(L.stats_done, 1)
    for t in range(QT):
        dve.wait_ge(L.stats_done, at(b, QT, t + 1))
        apart(dve, L.passed["dve"])
        nc.vector.bn_aggr(L.moments[:, t, :], L.stats[:, t, :]).then_inc(L.aggr_done, 1)
    dve.wait_ge(L.aggr_done, at(b, QT, QT))
    nc.vector.tensor_scalar(L.var_eps, L.moments[:, :, 1], LN_EPS, None, ALU.add).then_inc(L.var_done, 1)


def dve_result(nc, dve, L, b):
    dve.wait_ge(L.rstd_done, b + 1)
    dve.wait_ge(L.stored, 16 * b)
    for t in range(QT):
        nc.vector.tensor_scalar(L.result[:, t, :], L.h[:, t, :], L.moments[:, t, 0:1], L.rstd[:, t:t + 1],
                                ALU.subtract, ALU.mult).then_inc(L.normed, 1)


def dve_norm(nc, dve, L, b):
    dve_moments(nc, dve, L, b)
    dve_result(nc, dve, L, b)


def pool_rstd(nc, pool, L, b):
    pool.wait_ge(L.var_done, b + 1)
    nc.gpsimd.tensor_tensor(L.rstd, L.var_eps, L.minus_half, ALU.pow).then_inc(L.rstd_done, 1)




def unit_keys(A, u):
    return u % QT + 1 if A.causal else QT


def pe_attention(nc, pe, A, b):
    U = QT * A.heads

    def scores(u):
        h, qt = divmod(u, QT)
        nk = unit_keys(A, u) * P
        S = A.S[u % S_BANKS]
        pe.wait_ge(A.exp_done, at(b, U, u - S_BANKS + 1))
        last = nc.tensor.matmul(S[:, 0:nk], A.query(h, qt), A.keys(h)[:, 0:nk], start=True, stop=not A.causal)
        if A.causal:
            last = nc.tensor.matmul(S[:, nk - P:nk], A.ident_bf, A.future, start=False, stop=True)
        last.then_inc(A.scores_ready, 1)

    def transposes(u):
        pe.wait_ge(A.probs_ready, at(b, U, u + 1))
        pe.wait_ge(A.probsT_copied, at(b, U, u - 1))
        for k in range(unit_keys(A, u)):
            last = nc.tensor.transpose(A.TB[u % 2][:, k * P:(k + 1) * P], A.probs[:, u % P_SLOTS, k * P:(k + 1) * P], A.ident)
        last.then_inc(A.probsT_ready, 1)

    def values(h):
        pe.wait_ge(A.probsT_copied, at(b, U, QT * h + QT))
        g, j = divmod(h, A.group)
        if j == 0:
            pe.wait_ge(A.z_copied, at(b, A.heads // A.group, g))
        for k in range(QT):
            c0 = k * P if A.causal else 0
            last = nc.tensor.matmul(A.Z[A.z_step * j:A.z_step * j + A.z_rows, c0:T], A.value(h, k), A.probsT[:, h % 2, k, c0:T],
                                    start=(k == 0), stop=(k == QT - 1))
        last.then_inc(A.values_done, 1)

    for i in range(U + PV_LAG):
        if i < U:
            scores(i)
        if T_LAG <= i < U + T_LAG:
            transposes(i - T_LAG)
        if i >= PV_LAG and (i - PV_LAG) % QT == QT - 1:
            values((i - PV_LAG) // QT)


def act_attention(nc, act, A, b):
    U = QT * A.heads

    def copy_probsT(u):
        h, qt = divmod(u, QT)
        n = unit_keys(A, u)
        act.wait_ge(A.probsT_ready, at(b, U, u + 1))
        act.wait_ge(A.values_done, at(b, A.heads, h - 1))
        nc.scalar.activation(A.probsT[:, h % 2, 0:n, qt * P:(qt + 1) * P],
                             A.TB[u % 2][:, 0:n * P].rearrange("p (k q) -> p k q", k=n), ACT.Copy).then_inc(A.probsT_copied, 1)

    def exps(u):
        nk = unit_keys(A, u) * P
        act.wait_ge(A.negmax_ready, at(b, U, u + 1))
        act.wait_ge(A.probsT_ready, at(b, U, u - P_SLOTS + 1))
        nc.scalar.activation(A.probs[:, u % P_SLOTS, 0:nk], A.S[u % S_BANKS][:, 0:nk], ACT.Exp,
                             bias=A.negmax[:, u:u + 1], accum_out=A.sums[:, u:u + 1]).then_inc(A.exp_done, 1)

    for i in range(U + T_LAG):
        if i >= T_LAG:
            copy_probsT(i - T_LAG)
        if i < U:
            exps(i)


def dve_attention(nc, dve, A, b, norm_row=None):
    U = QT * A.heads

    def negmax(u):
        nk = unit_keys(A, u) * P
        dve.wait_ge(A.scores_ready, at(b, U, u + 1))
        nc.vector.tensor_reduce(A.negmax[:, u:u + 1], A.S[u % S_BANKS][:, 0:nk], AX, ALU.max, negate=True).then_inc(A.negmax_ready, 1)

    def rinv(u):
        dve.wait_ge(A.exp_done, at(b, U, u + 1))
        nc.vector.reciprocal(A.rinv[:, u:u + 1], A.sums[:, u:u + 1]).then_inc(A.rinv_ready, 1)

    def copy_z(g):
        dve.wait_ge(A.values_done, at(b, A.heads, (g + 1) * A.group))
        if A.z_bias is None:
            nc.vector.tensor_copy(A.zT[0:A.z_part, g, :], A.Z[0:A.z_part]).then_inc(A.z_copied, 1)
        else:
            nc.vector.tensor_scalar(A.zT[:, g, :], A.Z, A.z_bias[:, g:g + 1], None, ALU.add).then_inc(A.z_copied, 1)

    for i in range(U + PV_LAG + 2):
        if norm_row is not None and i == 4:
            dve_moments(nc, dve, A, norm_row)
        if norm_row is not None and i == 10:
            dve_result(nc, dve, A, norm_row)
        if i < U:
            negmax(i)
        if 1 <= i <= U:
            rinv(i - 1)
        j = i - PV_LAG - 1
        if j >= 0 and j % (QT * A.group) == QT * A.group - 1:
            copy_z(j // (QT * A.group))


def pool_attention(nc, pool, A, b, norm_row=None):
    U = QT * A.heads
    for u in range(U):
        nk = unit_keys(A, u) * P
        pr = A.probs[:, u % P_SLOTS, 0:nk]
        pool.wait_ge(A.rinv_ready, at(b, U, u + 1))
        apart(pool, A.passed["pool"])
        nc.gpsimd.tensor_scalar(pr, pr, A.rinv[:, u:u + 1], 1.0, ALU.mult, ALU.mult).then_inc(A.probs_ready, 1)
        if norm_row is not None and u == 5:
            pool_rstd(nc, pool, A, norm_row)
        if A.bias is not None and u == U // 2:
            pool_bias(nc, pool, A, b)




def build(nc, a, out, layers=(0, 1, 2, 3, 4, 5)):
    NB = a["x"].shape[0]
    ET = mybir.EngineType
    with ExitStack() as root:
        def sbt(name, shape, dt=F32):
            return root.enter_context(nc.sbuf_tensor(name, shape, dt))

        def psum(name):
            return root.enter_context(nc.psum_tensor(name, [P, T], F32))

        weights_odd = sbt("weights_odd", [P, 13100])
        consts = sbt("consts", [P, 160])
        consts_bf = sbt("consts_bf", [P, 256], BF16)
        tokens = sbt("tokens", [P, QT, D])
        residual = sbt("residual", [P, QT, D])
        hbuf = sbt("hbuf", [P, QT, D])
        result = sbt("result", [P, QT, D])
        xT = sbt("xT", [P, KT, T])
        small = sbt("small", [P, 64])
        banks = [psum(f"bank{i}") for i in range(8)]
        scratch = [nc.dram_tensor(f"tokens_after_{i}", [NB, T, D], F32).ap() for i in range(5)]

        ident = consts[:, 0:P]
        half_mask = consts[:, P:P + 2]
        head_mask = consts[:, P + 2:P + 10]
        minus_half = consts[:, P + 10:P + 10 + QT]
        iota = consts[:, P + 14:P + 30]
        ident_bf = consts_bf[:, 0:P]
        future = consts_bf[:, P:2 * P]
        consts_loaded = root.enter_context(nc.semaphore("consts_loaded"))
        weights_loaded = [root.enter_context(nc.semaphore(f"weights_loaded_{i}")) for i in range(6)]
        before_last = ExitStack()
        before_last.enter_context(nc.cleanup_on_exit())
        weights = [nc.alloc_sbuf_tensor("weights_even", [P, 8240], F32), weights_odd]

        def carve(buf):
            off = [0]

            def take(*shape):
                n = 1
                for s in shape:
                    n *= s
                v = buf[:, off[0]:off[0] + n]
                off[0] += n
                assert off[0] <= buf.shape[1], off[0]
                if len(shape) == 2:
                    v = v.rearrange("p (a b) -> p a b", a=shape[0])
                if len(shape) == 3:
                    v = v.rearrange("p (a b c) -> p a b c", a=shape[0], b=shape[1])
                return v
            return take

        W = [{} for _ in range(6)]
        moves = [[] for _ in range(6)]

        def bring(l, name, take, *shape, rows=P):
            v = take(*shape)
            W[l][name] = v
            flat = v
            if len(shape) == 2:
                flat = v.rearrange("p a b -> p (a b)")
            moves[l].append((flat[0:rows], a[name]))

        t = carve(weights[0])
        bring(0, "l0a_wq", t, KT, 1024)
        bring(0, "l0a_wk", t, KT, 512)
        bring(0, "l0a_wv", t, KT, 512)
        bring(0, "l0a_wo", t, 8, D)
        bring(0, "l0a_bo", t, D)
        t = carve(weights[1])
        bring(1, "l0x_wq", t, KT, 512)
        bring(1, "l0x_wk", t, 2, 512, rows=96)
        bring(1, "l0x_wv", t, 2, 512, rows=96)
        bring(1, "l0x_wo", t, 4, D)
        bring(1, "l0x_bo", t, D)
        t = carve(weights[0])
        bring(2, "l0f_wqkv", t, 3 * KT, 1024)
        bring(2, "l0f_wo", t, 8, D)
        bring(2, "l0f_sim", t, KT, 16)
        bring(2, "l0f_gates", t, 16)
        t = carve(weights[1])
        bring(3, "l1a_wg", t, KT, D)
        bring(3, "l1a_wv", t, KT, D)
        bring(3, "l1a_wo", t, 4, D)
        bring(3, "l1a_head_rows", t, 16, P)
        bring(3, "l1a_bg", t, D)
        bring(3, "l1a_bv", t, 4)
        bring(3, "l1a_bo", t, D)
        take_rest_of_odd = t
        t = carve(weights[1])
        bring(5, "l1f_wy", t, KT, 1920)
        bring(5, "l1f_wg", t, KT, 1920)
        bring(5, "l1f_w2", t, 15, D)
        bring(5, "l1f_gate", t, KT, 8)
        bring(5, "l1f_expert_rows", t, 12, P)
        t = carve(weights[0])
        bring(4, "l1x_wq", t, KT, 256)
        bring(4, "l1x_wk", t, 2, 256, rows=96)
        bring(4, "l1x_wv", t, 2, 256, rows=96)
        bring(4, "l1x_w1", t, 4, 512)
        bring(4, "l1x_w2", t, 4, D)
        bring(4, "l1x_bq", t, 2)
        bring(4, "l1x_bk", t, 2)
        bring(4, "l1x_bv", t, 4)
        bring(4, "l1x_b1", t, 4)
        bring(4, "l1x_b2", t, D)
        bring(4, "l1x_places", t, 4, T)
        take_rest_of_even_4 = t

        def load_weights(sp, l):
            for dst, src in moves[l]:
                nc.sync.dma_start(dst, src).then_inc(weights_loaded[l], 16)

        def wait_weights(eng, l):
            eng.wait_ge(weights_loaded[l], 16 * len(moves[l]))

        def load_next_weights(l):
            def load(sp):
                later = [m for m in layers if m > l]
                if later:
                    load_weights(sp, later[0])
            return load

        def common(l, per, bias):
            def sem(name):
                return nc.alloc_semaphore(f"l{l}_{name}")
            src = a["x"] if l == layers[0] else scratch[l - 1]
            dst = out if l == layers[-1] else scratch[l]
            L = Names()
            L.x_in = lambda b: src[bass.ds(b, 1)].rearrange("o (t p) d -> p (o t) d", p=P)
            L.x_out = lambda b: dst[bass.ds(b, 1)].rearrange("o (t p) d -> p (o t) d", p=P)
            L.ctx_in, L.load_next_weights, L.extra_tokens_reader = None, load_next_weights(l), None
            L.bias, L.per = bias, per
            L.tokens, L.residual, L.h, L.result, L.xT, L.J = tokens[:], residual[:], hbuf[:], result[:], xT[:], [banks[6][:], banks[7][:]]
            L.ident, L.ident_bf, L.future, L.minus_half, L.consts_loaded = ident, ident_bf, future, minus_half, consts_loaded
            L.stats = small[:, 0:24].rearrange("p (t s) -> p t s", t=QT)
            L.moments = small[:, 24:32].rearrange("p (t s) -> p t s", t=QT)
            L.var_eps, L.rstd = small[:, 32:36], small[:, 36:40]
            L.tokens_loaded, L.context_loaded, L.residual_loaded = sem("tokens_loaded"), sem("context_loaded"), sem("residual_loaded")
            L.residual_biased, L.stored = sem("residual_biased"), sem("stored")
            L.item_ready = [sem("item_ready_act"), sem("item_ready_dve")]
            L.item_copied = [sem("item_copied_act"), sem("item_copied_dve")]
            L.y_ready, L.y_added, L.stats_done, L.aggr_done = sem("y_ready"), sem("y_added"), sem("stats_done"), sem("aggr_done")
            L.var_done, L.rstd_done, L.normed = sem("var_done"), sem("rstd_done"), sem("normed")
            L.sem = sem
            L.passed = {e: sem(f"{e}_passed") for e in ("sp", "pe", "dve", "pool")}
            return L

        def attention_of(L, take, heads, group, z_step, z_rows, causal, prefix=""):
            U = QT * heads
            L.scores_ready, L.negmax_ready, L.exp_done, L.rinv_ready = (
                L.sem(s) for s in ("scores_ready", "negmax_ready", "exp_done", "rinv_ready"))
            L.probs_ready, L.probsT_ready, L.probsT_copied, L.values_done, L.z_copied, L.pads_zeroed = (
                L.sem(s) for s in ("probs_ready", "probsT_ready", "probsT_copied", "values_done", "z_copied", "pads_zeroed"))
            L.z_bias, L.z_part, L.heads, L.group, L.z_step, L.z_rows, L.causal = None, z_step * group, heads, group, z_step, z_rows, causal
            L.S, L.TB, L.Z = [banks[i][:] for i in range(S_BANKS)], [banks[3][:], banks[4][:]], banks[5][:]
            L.probs, L.probsT = take(P_SLOTS, T), take(2, QT, T)
            L.negmax, L.sums, L.rinv = take(U), take(U), take(U)

        def wide_attention(l, heads, kv_heads, causal, context):
            w = W[l]
            with nc.cleanup_on_exit():
                qn, kn = heads // 2, kv_heads // 2
                Q0, K0 = KT, KT + qn
                V0 = K0 + kn
                n_items = V0 + QT
                L = common(l, [(n_items + 1) // 2, n_items // 2], None)
                take = carve(nc.alloc_sbuf_tensor(f"arena_{l}", [P, ARENA], F32))
                L.qT, L.kz, L.v = take(qn, T), take(kv_heads, T), take(QT, 64 * kv_heads)
                L.zT = take(heads // 2, T)
                attention_of(L, take, heads, 2, 64, 64, causal)
                if context:
                    L.ctx_in = lambda b: a["ctxT"][bass.ds(b, 1)].rearrange("o (k p) t -> p (o k) t", p=96)
                    L.context = take(2, T)[0:96]
                    wq, wk, wv, wo, bo = w["l0x_wq"], w["l0x_wk"][0:96], w["l0x_wv"][0:96], w["l0x_wo"], w["l0x_bo"]
                    src = L.context
                else:
                    wq, wk, wv, wo, bo = w["l0a_wq"], w["l0a_wk"], w["l0a_wv"], w["l0a_wo"], w["l0a_bo"]
                    src = L.xT
                L.bias = bo.unsqueeze(1).broadcast_to([P, QT, D])

                def head_at(i):
                    c, j = divmod(i, 2)
                    kv = (c // 2) * 2 + j if not context else i
                    return c, kv

                L.query = lambda i, qt: L.qT[:, head_at(i)[0], qt * P:(qt + 1) * P]
                L.keys = lambda i: L.kz[:, head_at(i)[1], :]
                L.value = lambda i, k: L.v[:, k, 64 * head_at(i)[1]:64 * head_at(i)[1] + 64]

                with nc.Block() as block:
                    @block.sync
                    def _(sp):
                        sp_stream(nc, sp, L, NB)

                    @block.tensor
                    def _(pe):
                        wait_weights(pe, l)

                        def project(b, first):
                            pe_transpose_tokens(nc, pe, L, b, first)
                            wait_items_copied(pe, L, b, 1)
                            if context:
                                pe.wait_ge(L.context_loaded, 16 * (b + 1))
                            for c in range(qn):
                                pe_item(nc, pe, L, b, Q0 + c, L.J[(Q0 + c) % 2], [(wq[:, k, c * P:(c + 1) * P], L.xT[:, k, :]) for k in range(KT)])
                            for c in range(kn):
                                pe_item(nc, pe, L, b, K0 + c, L.J[(K0 + c) % 2], [(wk[:, k, c * P:(c + 1) * P], src[:, k, :]) for k in range(2)])
                            for t in range(QT):
                                pe_item(nc, pe, L, b, V0 + t, L.J[(V0 + t) % 2][:, 0:64 * kv_heads],
                                        [(src[:, k, t * P:(t + 1) * P], wv[:, k, :]) for k in range(2)])

                        def attend(b):
                            wait_items_copied(pe, L, b, n_items - 1)
                            pe_attention(nc, pe, L, b)

                        def output(b, rows):
                            pe.wait_ge(L.z_copied, at(b, heads // 2, heads // 2))
                            wait_banks_free(pe, L, rows)
                            pe_output(nc, pe, L, b, L.zT, [wo[:, c, :] for c in range(qn)])

                        project(0, True)
                        with nc.Fori(0, NB - 1, engines=[ET.PE]) as b:
                            attend(b)
                            project(b + 1, False)
                            output(b, b + 2)
                        attend(NB - 1)
                        output(NB - 1, NB)

                    def copy_items(eng, e, b):
                        copy_transposed(nc, eng, L, b, e)
                        for c in range(qn):
                            if (Q0 + c) % 2 == e:
                                wait_item(eng, L, b, Q0 + c)
                                scale_copy(nc, e, L.qT[:, c, :], L.J[e], 64 ** -0.5).then_inc(L.item_copied[e], 1)
                        for c in range(kn):
                            if (K0 + c) % 2 == e:
                                wait_item(eng, L, b, K0 + c)
                                scale_copy(nc, e, L.kz[:, 2 * c, :], L.J[e], half_mask[:, 0:1])
                                scale_copy(nc, e, L.kz[:, 2 * c + 1, :], L.J[e], half_mask[:, 1:2]).then_inc(L.item_copied[e], 1)
                        for t in range(QT):
                            if (V0 + t) % 2 == e:
                                wait_item(eng, L, b, V0 + t)
                                scale_copy(nc, e, L.v[:, t, :], L.J[e][:, 0:64 * kv_heads], 1.0).then_inc(L.item_copied[e], 1)

                    @block.scalar
                    def _(act):
                        act.wait_ge(consts_loaded, 32)
                        copy_items(act, 0, 0)
                        with nc.Fori(0, NB - 1, engines=[ET.Activation]) as b:
                            act_attention(nc, act, L, b)
                            copy_items(act, 0, b + 1)
                        act_attention(nc, act, L, NB - 1)

                    @block.vector
                    def _(dve):
                        dve.wait_ge(consts_loaded, 32)
                        copy_items(dve, 1, 0)
                        dve_attention(nc, dve, L, 0)
                        with nc.Fori(0, NB - 1, engines=[ET.DVE]) as b:
                            copy_items(dve, 1, b + 1)
                            dve_add(nc, dve, L, b)
                            dve_attention(nc, dve, L, b + 1, norm_row=b)
                        dve_add(nc, dve, L, NB - 1)
                        dve_norm(nc, dve, L, NB - 1)

                    @block.gpsimd
                    def _(pool):
                        wait_weights(pool, l)
                        pool.wait_ge(consts_loaded, 32)
                        pool_attention(nc, pool, L, 0)
                        with nc.Fori(0, NB - 1, engines=[ET.Pool]) as b:
                            pool_attention(nc, pool, L, b + 1, norm_row=b)
                        pool_rstd(nc, pool, L, NB - 1)

        def narrow_cross_attention(l):
            w = W[l]
            heads, d = 16, 16
            with nc.cleanup_on_exit():
                Q0, K0, n_items = 2, 6, 10
                V = [4, 5, 8, 9]
                STACKS = heads
                L = common(l, [n_items // 2, n_items // 2], w["l1x_b2"].unsqueeze(1).broadcast_to([P, QT, D]))
                take = carve(nc.alloc_sbuf_tensor(f"arena_{l}", [P, 9930], F32))
                take_part = carve(nc.alloc_sbuf_tensor("arena_4_parts", [P, 16384], FP32R))
                q_stacked, k_stacked, high, low, places = take_part(heads // 2, T), take_part(heads, T), take_part(2, T), take_part(2, T), take_part(4, T)
                L.v, whole = take(QT, 32 * heads), take(2, T)
                L.zT = w["l1x_places"]
                attention_of(L, take, heads, 4, 32, 32, False)
                L.hT = L.probsT[:, 0]
                high_ready, low_ready, places_ready = L.sem("high_ready"), L.sem("low_ready"), L.sem("places_ready")
                stack_ready = [L.sem("stack_ready_act"), L.sem("stack_ready_dve")]
                stack_copied = [L.sem("stack_copied_act"), L.sem("stack_copied_dve")]
                L.ctx_in = lambda b: a["ctxT"][bass.ds(b, 1)].rearrange("o (k p) t -> p (o k) t", p=96)
                L.context = take_rest_of_even_4(2, T)[0:96]
                bq_scaled = take(2)
                hidden_ready = [L.sem("hidden_ready_act"), L.sem("hidden_ready_dve")]
                hidden_copied = [L.sem("hidden_copied_act"), L.sem("hidden_copied_dve")]
                biases_made = L.sem("biases_made")
                L.query = lambda h, qt: q_stacked[:, h // 2, qt * P:(qt + 1) * P]
                L.keys = lambda h: k_stacked[:, h, :]
                L.value = lambda h, k: L.v[:, k, 32 * h:32 * h + 32]
                L.z_bias = w["l1x_bv"]

                with nc.Block() as block:
                    @block.sync
                    def _(sp):
                        sp_stream(nc, sp, L, NB)

                    @block.tensor
                    def _(pe):
                        wait_weights(pe, l)
                        pe.wait_ge(L.pads_zeroed, 1)
                        pe.wait_ge(places_ready, 1)

                        def project(b, first):
                            pe_transpose_tokens(nc, pe, L, b, first)
                            wait_items_copied(pe, L, b, 1)
                            pe.wait_ge(L.context_loaded, 16 * (b + 1))
                            def values(ts):
                                for t in ts:
                                    pe_item(nc, pe, L, b, V[t], L.J[V[t] % 2][:, 0:D],
                                            [(L.context[:, k, t * P:(t + 1) * P], w["l1x_wv"][0:96, k, :]) for k in range(2)])

                            def stack(first_stack, kind):
                                pe.wait_ge(low_ready, at(b, 4, 2 + kind))
                                for p in range(heads // 2):
                                    c, i = divmod(p, 4)
                                    n = first_stack + p
                                    pe.wait_ge(stack_copied[n % 2], at(b, STACKS // 2, n // 2 - 1))
                                    bank, cols = banks[n % 4][:], slice(i * P, (i + 1) * P)
                                    nc.tensor.matmul(bank, places[:, kind, cols], high[:, c, :], start=True, stop=False)
                                    nc.tensor.matmul(bank, places[:, kind + 1, cols], low[:, c, :], start=False, stop=True).then_inc(stack_ready[n % 2], 1)

                            for c in range(2):
                                pe_item(nc, pe, L, b, Q0 + c, L.J[c], [(w["l1x_wq"][:, k, c * P:(c + 1) * P], L.xT[:, k, :]) for k in range(2)])
                            values((0, 1))
                            stack(0, 0)
                            for c in range(2):
                                pe_item(nc, pe, L, b, K0 + c, L.J[c], [(w["l1x_wk"][0:96, k, c * P:(c + 1) * P], L.context[:, k, :]) for k in range(2)])
                            values((2, 3))
                            stack(heads // 2, 2)

                        def attend(b):
                            wait_items_copied(pe, L, b, n_items - 1)
                            for e in range(2):
                                pe.wait_ge(stack_copied[e], at(b, STACKS // 2, STACKS // 2))
                            pe_attention(nc, pe, L, b)

                        def hidden(b, rows):
                            pe.wait_ge(L.z_copied, at(b, 4, 4))
                            wait_banks_free(pe, L, rows)
                            for c in range(4):
                                if c >= 2:
                                    pe.wait_ge(hidden_copied[c % 2], at(b, 2, c // 2))
                                for k in range(4):
                                    last = nc.tensor.matmul(L.J[c % 2], w["l1x_w1"][:, k, c * P:(c + 1) * P], L.zT[:, k, :], start=(k == 0), stop=(k == 3))
                                last.then_inc(hidden_ready[c % 2], 1)
                            for e in range(2):
                                pe.wait_ge(hidden_copied[e], at(b, 2, 2))

                        def output(b, rows):
                            hidden(b, rows)
                            pe_output(nc, pe, L, b, L.hT, [w["l1x_w2"][:, c, :] for c in range(4)])

                        project(0, True)
                        with nc.Fori(0, NB - 1, engines=[ET.PE]) as b:
                            attend(b)
                            project(b + 1, False)
                            output(b, b + 2)
                        attend(NB - 1)
                        output(NB - 1, NB)

                    def copy_items(eng, e, b):
                        copy_transposed(nc, eng, L, b, e)
                        split(eng, e, b, Q0, 0, d ** -0.5, bq_scaled)
                        value(eng, e, b, e)
                        for n in range(e, heads // 2, 2):
                            eng.wait_ge(stack_ready[e], at(b, STACKS // 2, n // 2 + 1))
                            scale_copy(nc, e, q_stacked[:, n, :], banks[n % 4][:], 1.0).then_inc(stack_copied[e], 1)
                        if e == 0:
                            eng.wait_ge(stack_ready[1], at(b, STACKS // 2, heads // 4))
                        split(eng, e, b, K0, 2, 1.0, w["l1x_bk"])
                        value(eng, e, b, 2 + e)
                        for n in range(heads // 2 + e, STACKS, 2):
                            h, bank = 2 * n - heads, banks[n % 4][:]
                            eng.wait_ge(stack_ready[e], at(b, STACKS // 2, n // 2 + 1))
                            scale_copy(nc, e, k_stacked[:, h, :], bank, half_mask[:, 0:1])
                            scale_copy(nc, e, k_stacked[:, h + 1, :], bank, half_mask[:, 1:2]).then_inc(stack_copied[e], 1)

                    def split(eng, e, b, n0, done, scale, bias):
                        if e == 0:
                            wait_item(eng, L, b, 1)
                            for c in range(2):
                                wait_items_copied(eng, L, b, n0 + c)
                                nc.scalar.activation(high[:, c, :], whole[:, c, :], ACT.Copy).then_inc(high_ready, 1)
                        else:
                            for c in range(2):
                                wait_item(eng, L, b, n0 + c)
                                affine_copy(nc, 1, whole[:, c, :], L.J[c], scale, bias[:, c:c + 1]).then_inc(L.item_copied[c], 1)
                            for c in range(2):
                                eng.wait_ge(high_ready, at(b, 4, done + c + 1))
                                nc.vector.tensor_tensor(low[:, c, :], whole[:, c, :], high[:, c, :].bitcast(F32), ALU.subtract).then_inc(low_ready, 1)

                    def value(eng, e, b, t):
                        wait_item(eng, L, b, V[t])
                        scale_copy(nc, e, L.v[:, t, :].rearrange("p (h c) -> p h c", c=32)[:, :, 0:d],
                                   L.J[e][:, 0:D].rearrange("p (h c) -> p h c", c=d), 1.0).then_inc(L.item_copied[e], 1)

                    def copy_hidden(eng, e, b):
                        for c in range(e, 4, 2):
                            eng.wait_ge(hidden_ready[e], at(b, 2, c // 2 + 1))
                            if e == 0:
                                last = nc.scalar.activation(L.hT[:, c, :], L.J[e], ACT.Relu, bias=w["l1x_b1"][:, c:c + 1])
                            else:
                                last = nc.vector.tensor_scalar(L.hT[:, c, :], L.J[e], w["l1x_b1"][:, c:c + 1], 0.0, ALU.add, ALU.max)
                            last.then_inc(hidden_copied[e], 1)

                    @block.scalar
                    def _(act):
                        wait_weights(act, l)
                        act.wait_ge(consts_loaded, 32)
                        act.wait_ge(L.pads_zeroed, 1)
                        nc.scalar.activation(places, w["l1x_places"], ACT.Copy).then_inc(places_ready, 1)
                        copy_items(act, 0, 0)
                        with nc.Fori(0, NB - 1, engines=[ET.Activation]) as b:
                            act_attention(nc, act, L, b)
                            copy_items(act, 0, b + 1)
                            copy_hidden(act, 0, b)
                        act_attention(nc, act, L, NB - 1)
                        copy_hidden(act, 0, NB - 1)

                    @block.vector
                    def _(dve):
                        wait_weights(dve, l)
                        dve.wait_ge(consts_loaded, 32)
                        dve.wait_ge(biases_made, 1)
                        dve.wait_ge(L.pads_zeroed, 1)
                        copy_items(dve, 1, 0)
                        dve_attention(nc, dve, L, 0)
                        with nc.Fori(0, NB - 1, engines=[ET.DVE]) as b:
                            copy_items(dve, 1, b + 1)
                            copy_hidden(dve, 1, b)
                            dve_add(nc, dve, L, b)
                            dve_attention(nc, dve, L, b + 1, norm_row=b)
                        copy_hidden(dve, 1, NB - 1)
                        dve_add(nc, dve, L, NB - 1)
                        dve_norm(nc, dve, L, NB - 1)

                    @block.gpsimd
                    def _(pool):
                        nc.gpsimd.memset(L.v, 0.0).then_inc(L.pads_zeroed, 1)
                        wait_weights(pool, l)
                        pool.wait_ge(consts_loaded, 32)
                        nc.gpsimd.tensor_scalar(bq_scaled, w["l1x_bq"], d ** -0.5, 1.0, ALU.mult, ALU.mult).then_inc(biases_made, 1)
                        pool_attention(nc, pool, L, 0)
                        with nc.Fori(0, NB - 1, engines=[ET.Pool]) as b:
                            pool_attention(nc, pool, L, b + 1, norm_row=b)
                        pool_rstd(nc, pool, L, NB - 1)

        def gated_experts(l):
            w = W[l]
            E, NC, NX = 8, 15, 12
            LO = 32
            with nc.cleanup_on_exit():
                L = common(l, [2, 2], None)
                sem = L.sem
                take = carve(nc.alloc_sbuf_tensor("experts_whole", [P, 10300], F32))
                take_part = carve(nc.alloc_sbuf_tensor("experts_parts", [P, 19460], FP32R))
                L.acts, silu, scaled = take(NC, T), take(2, T), take(2, T)
                wT, logits, shifted, exps, scores, gates = take_part(T), take(QT, E), take(QT, E), take(QT, E), take(QT, E), take(QT, LO + E)
                wh, wl = take_part(2 * KT, 1920), take_part(2 * KT, 1920)
                whole = [w[name][:, k, :] for name in ("l1f_wy", "l1f_wg") for k in range(KT)]
                xh, xl = take_part(KT, T), take_part(KT, T)
                expert_rows = take_part(NX, P)
                weights_high, weights_low, xh_ready, xl_ready, wT_step = (
                    sem("weights_high"), sem("weights_low"), sem("xh_ready"), sem("xl_ready"), sem("wT_step"))
                top, picked, picked2, index_f, index = take(QT, 8), take(QT, E), take(QT, E), take(QT, 8), take(QT, 8).bitcast(U32)
                peak, total, inverse = take(QT), take(QT), take(QT)
                Y, G, WB = ([banks[3 * i + j][:] for i in range(2)] for j in range(3))
                route_step, shifted_ready, exps_ready, gates_ready = sem("route_step"), sem("shifted_ready"), sem("exps_ready"), sem("gates_ready")
                g_ready, yw_ready, silu_done, scaled_done, chunk_done, zeroed = (
                    sem("g_ready"), sem("yw_ready"), sem("silu_done"), sem("scaled_done"), sem("chunk_done"), sem("zeroed"))
                order = list(range(NX, NC)) + list(range(NX))
                STEPS = 15

                with nc.Block() as block:
                    @block.sync
                    def _(sp):
                        sp_stream(nc, sp, L, NB)

                    @block.tensor
                    def _(pe):
                        wait_weights(pe, l)
                        pe.wait_ge(weights_high, 6)
                        pe.wait_ge(weights_low, 4)

                        def head(b, first):
                            pe_transpose_tokens(nc, pe, L, b, first)
                            wait_items_copied(pe, L, b, 1)
                            for t in range(QT):
                                for k in range(KT):
                                    last = nc.tensor.matmul(L.J[0][:, E * t:E * t + E], L.xT[:, k, t * P:(t + 1) * P], w["l1f_gate"][:, k, :], start=(k == 0), stop=(k == KT - 1))
                            last.then_inc(L.item_ready[0], 1)

                        def up(bank, what, c):
                            cols = slice(c * P, (c + 1) * P)
                            parts = [(wa, xa) for k in range(KT) for wa, xa in (
                                (wh[:, what * KT + k, cols], xh[:, k, :]), (wl[:, what * KT + k, cols], xh[:, k, :]), (wh[:, what * KT + k, cols], xl[:, k, :]))]
                            for n, (wa, xa) in enumerate(parts):
                                last = nc.tensor.matmul(bank, wa, xa, start=(n == 0), stop=(n == len(parts) - 1))
                            return last

                        def chunks(b):
                            pe.wait_ge(xh_ready, 2 * (b + 1))
                            pe.wait_ge(xl_ready, 2 * (b + 1))
                            for i, c in enumerate(order):
                                if i == NC - NX:
                                    pe.wait_ge(gates_ready, 2 * (b + 1))
                                    pe.wait_ge(L.y_added, QT * b)
                                    apart(pe, L.passed["pe"])
                                    for t in range(QT):
                                        last = nc.tensor.transpose(L.J[1][0:LO + E, t * P:(t + 1) * P], gates[:, t, :], L.ident)
                                    last.then_inc(L.item_ready[1], 1)
                                    pe.wait_ge(L.item_copied[1], at(b, 2, 2))
                                s = i % 2
                                pe.wait_ge(chunk_done, at(b, NC, i - 1))
                                up(G[s], 1, c).then_inc(g_ready, 1)
                                last = up(Y[s], 0, c)
                                if c < NX:
                                    last = nc.tensor.matmul(WB[s], expert_rows[:, c, :], wT, start=True, stop=True)
                                last.then_inc(yw_ready, 1)

                        def output(b, more):
                            pe.wait_ge(chunk_done, NC * (b + 1))
                            pe.wait_ge(L.item_copied[0], 2 * (b + 1) + 2 * more)
                            pe.wait_ge(L.item_copied[1], 2 * (b + 1) + more)
                            pe_output(nc, pe, L, b, L.acts, [w["l1f_w2"][:, c, :] for c in range(NC)])

                        head(0, True)
                        with nc.Fori(0, NB - 1, engines=[ET.PE]) as b:
                            chunks(b)
                            head(b + 1, False)
                            output(b, 1)
                        chunks(NB - 1)
                        output(NB - 1, 0)

                    @block.scalar
                    def _(act):
                        wait_weights(act, l)
                        for i in range(4):
                            nc.scalar.activation(wh[:, i, :], whole[i], ACT.Copy).then_inc(weights_high, 1)
                        nc.scalar.activation(expert_rows, w["l1f_expert_rows"], ACT.Copy).then_inc(weights_high, 1)
                        act.wait_ge(zeroed, 2)
                        nc.scalar.activation(wT, scaled[:, 0, :], ACT.Copy).then_inc(weights_high, 1)

                        def head(b):
                            copy_transposed(nc, act, L, b, 0)
                            act.wait_ge(L.item_copied[0], at(b, 2, 1))
                            nc.scalar.activation(xh[:, 0, :], L.xT[:, 0, :], ACT.Copy).then_inc(xh_ready, 1)
                            act.wait_ge(L.item_copied[1], at(b, 2, 1))
                            nc.scalar.activation(xh[:, 1, :], L.xT[:, 1, :], ACT.Copy).then_inc(xh_ready, 1)
                            wait_item(act, L, b, 2)
                            nc.scalar.activation(logits, L.J[0][:, 0:QT * E].rearrange("p (t e) -> p t e", t=QT), ACT.Copy).then_inc(L.item_copied[0], 1)
                            act.wait_ge(shifted_ready, b + 1)
                            nc.scalar.activation(exps, shifted, ACT.Exp).then_inc(exps_ready, 1)

                        def chunks(b):
                            for i in range(NC):
                                act.wait_ge(g_ready, at(b, NC, i + 1))
                                act.wait_ge(chunk_done, at(b, NC, i - 1))
                                nc.scalar.activation(silu[:, i % 2, :], G[i % 2], ACT.Silu).then_inc(silu_done, 1)

                        head(0)
                        with nc.Fori(0, NB - 1, engines=[ET.Activation]) as b:
                            chunks(b)
                            head(b + 1)
                        chunks(NB - 1)

                    @block.vector
                    def _(dve):
                        dve.wait_ge(consts_loaded, 32)
                        dve.wait_ge(zeroed, 2)

                        def split_weights():
                            for i in range(4):
                                dve.wait_ge(weights_high, i + 1)
                                nc.vector.tensor_tensor(wl[:, i, :], whole[i], wh[:, i, :].bitcast(F32), ALU.subtract).then_inc(weights_low, 1)

                        def head(b):
                            copy_transposed(nc, dve, L, b, 1)
                            for k in range(KT):
                                dve.wait_ge(xh_ready, at(b, 2, k + 1))
                                nc.vector.tensor_tensor(xl[:, k, :], L.xT[:, k, :], xh[:, k, :].bitcast(F32), ALU.subtract).then_inc(xl_ready, 1)
                            steps = [0]

                            def step(ins):
                                steps[0] += 1
                                ins.then_inc(route_step, 1)
                                dve.wait_ge(route_step, at(b, STEPS, steps[0]))
                                apart(dve, L.passed["dve"])

                            dve.wait_ge(L.item_copied[0], at(b, 2, 2))
                            step(nc.vector.tensor_reduce(peak, logits, AX, ALU.max))
                            nc.vector.tensor_tensor(shifted, logits, peak.unsqueeze(2).broadcast_to([P, QT, E]), ALU.subtract).then_inc(shifted_ready, 1)
                            dve.wait_ge(exps_ready, b + 1)
                            step(nc.vector.tensor_reduce(total, exps, AX, ALU.add))
                            step(nc.vector.reciprocal(inverse, total))
                            step(nc.vector.tensor_tensor(scores, exps, inverse.unsqueeze(2).broadcast_to([P, QT, E]), ALU.mult))
                            for t in range(QT):
                                step(nc.vector.max(top[:, t, :], scores[:, t, :]))
                            for t in range(QT):
                                step(nc.vector.max_index(index[:, t, :], top[:, t, :], scores[:, t, :]))
                            step(nc.vector.tensor_copy(index_f, index))
                            ids = iota[:, 0:E].unsqueeze(1).broadcast_to([P, QT, E])
                            nc.vector.tensor_tensor(picked2, ids, index_f[:, :, 1:2].broadcast_to([P, QT, E]), ALU.is_equal)
                            step(nc.vector.tensor_tensor(picked, ids, index_f[:, :, 0:1].broadcast_to([P, QT, E]), ALU.is_equal))
                            step(nc.vector.tensor_tensor(picked, picked, picked2, ALU.add))
                            dve.wait_ge(L.item_ready[1], at(b, 2, 0))
                            nc.vector.tensor_tensor(gates[:, :, 0:E], scores, picked, ALU.mult).then_inc(gates_ready, 1)
                            nc.vector.tensor_tensor(gates[:, :, LO:LO + E], scores, picked, ALU.mult).then_inc(gates_ready, 1)
                            assert steps[0] == STEPS

                        def chunks(b):
                            for i, c in enumerate(order):
                                s = i % 2
                                if i == NC - NX:
                                    wait_item(dve, L, b, 3)
                                    nc.vector.tensor_copy(wT[0:LO + E], L.J[1][0:LO + E]).then_inc(wT_step, 1)
                                    dve.wait_ge(wT_step, b + 1)
                                    low = wT[LO:LO + E]
                                    nc.vector.tensor_tensor(low, L.J[1][LO:LO + E], low.bitcast(F32), ALU.subtract).then_inc(L.item_copied[1], 1)
                                dve.wait_ge(silu_done, at(b, NC, i + 1))
                                dve.wait_ge(yw_ready, at(b, NC, i + 1))
                                if c >= NX:
                                    nc.vector.tensor_tensor(L.acts[:, c, :], Y[s], silu[:, s, :], ALU.mult).then_inc(chunk_done, 1)
                                    continue
                                nc.vector.tensor_tensor(scaled[:, s, :], Y[s], silu[:, s, :], ALU.mult).then_inc(scaled_done, 1)
                                dve.wait_ge(scaled_done, at(b, NX, i - (NC - NX) + 1))
                                nc.vector.tensor_tensor(L.acts[:, c, :], WB[s], scaled[:, s, :], ALU.mult).then_inc(chunk_done, 1)

                        split_weights()
                        dve.wait_ge(weights_high, 6)
                        head(0)
                        with nc.Fori(0, NB - 1, engines=[ET.DVE]) as b:
                            chunks(b)
                            head(b + 1)
                            dve_add(nc, dve, L, b)
                            dve_norm(nc, dve, L, b)
                        chunks(NB - 1)
                        dve_add(nc, dve, L, NB - 1)
                        dve_norm(nc, dve, L, NB - 1)

                    @block.gpsimd
                    def _(pool):
                        nc.gpsimd.memset(scaled, 0.0).then_inc(zeroed, 1)
                        nc.gpsimd.memset(gates, 0.0).then_inc(zeroed, 1)
                        with nc.Fori(0, NB, engines=[ET.Pool]) as b:
                            pool_rstd(nc, pool, L, b)

        def mixture_attention(l):
            w = W[l]
            E, d = 16, 64
            with nc.cleanup_on_exit():
                L = common(l, [3, 2], None)
                sem = L.sem
                take = carve(nc.alloc_sbuf_tensor(f"arena_{l}", [P, 12000], F32))
                take_part = carve(nc.alloc_sbuf_tensor("arena_2_parts", [P, 14336], FP32R))
                wh, wl, xh, xl = take_part(3 * KT, 1024), take_part(3 * KT, 1024), take_part(KT, T), take_part(KT, T)
                whole = w["l0f_wqkv"]
                take_whole = carve(whole.rearrange("p a b -> p (a b)"))
                L.qT, L.kT, qkv = take(T), take(T), take(3 * QT, d)
                product = [take_whole(E, d), take_whole(E, d), take(E, d)]
                mixed, L.zT = take_whole(QT, E * d), take(1, T)
                attention_of(L, take, 1, 1, d, d, True)
                L.mixT = L.probsT.rearrange("p a b c -> p (a b) c")
                weights_high, weights_low, xh_ready, xl_ready = sem("weights_high"), sem("weights_low"), sem("xh_ready"), sem("xl_ready")
                halved = sem("halved")
                ones, sim_square, sim_unit, sim_norm, sim_inverse, sigmoid = take(P), take(KT, E), take(KT, E), take(E), take(E), take(E)
                halves, square = take(E), take(D)
                raw, logits, active, gated, shifted, exps, masked, weights_ = (take(QT, E) for _ in range(8))
                fallback, fallback2 = take(QT, E), take(QT, E)
                top, index_f, index = take(QT, 8), take(QT, 8), take(QT, 8).bitcast(U32)
                length2, length, inv_length, peak, idle, total, inverse = (take(QT) for _ in range(7))
                L.query = lambda h, qt: L.qT[:, qt * P:(qt + 1) * P]
                L.keys = lambda h: L.kT
                L.value = lambda h, k: qkv[:, 2 * QT + k, :]
                setup_step, squared, norm2_ready, norm_done, sim_ready = sem("setup_step"), sem("squared"), sem("norm2_ready"), sem("norm_done"), sem("sim_ready")
                exp_gates_done = sem("exp_gates_done")
                lengths_done, length_ready, route_step, shifted_ready, exps_ready = (
                    sem("lengths_done"), sem("length_ready"), sem("route_step"), sem("shifted_ready"), sem("exps_ready"))
                moe_ready, moe_copied = sem("moe_ready"), sem("moe_copied")
                reduced = [sem("reduced_pool"), sem("reduced_dve")]
                zt_ready, mixed_done = sem("zt_ready"), sem("mixed_done")
                mix_ready = [sem("mix_ready_act"), sem("mix_ready_dve")]
                mix_copied = [sem("mix_copied_act"), sem("mix_copied_dve")]
                L.extra_tokens_reader, L.extra_tokens_per = lengths_done, QT
                STEPS, NM, RING = 28, 24, 6

                def wait_reduced(eng, b, n):
                    eng.wait_ge(reduced[0], at(b, 2 * QT, n - n // 3))
                    eng.wait_ge(reduced[1], at(b, QT, n // 3))

                with nc.Block() as block:
                    @block.sync
                    def _(sp):
                        sp_stream(nc, sp, L, NB)

                    @block.tensor
                    def _(pe):
                        wait_weights(pe, l)
                        pe.wait_ge(L.pads_zeroed, 3)
                        pe.wait_ge(squared, 1)
                        for k in range(KT):
                            last = nc.tensor.matmul(L.Z[:, 0:E], ones, sim_square[:, k, :], start=(k == 0), stop=(k == KT - 1))
                        last.then_inc(norm2_ready, 1)
                        pe.wait_ge(sim_ready, 1)
                        pe.wait_ge(weights_high, 3 * KT)
                        pe.wait_ge(weights_low, 3 * KT)

                        def project(b, first):
                            pe_transpose_tokens(nc, pe, L, b, first)
                            wait_items_copied(pe, L, b, 1)
                            for t in range(QT):
                                for k in range(KT):
                                    last = nc.tensor.matmul(L.J[0][:, E * t:E * t + E], L.xT[:, k, t * P:(t + 1) * P], sim_unit[:, k, :], start=(k == 0), stop=(k == KT - 1))
                            last.then_inc(L.item_ready[0], 1)
                            pe.wait_ge(xh_ready, 2 * (b + 1))
                            pe.wait_ge(xl_ready, 2 * (b + 1))
                            for m in range(NM):
                                t, kind, half = m // 6, m // 2 % 3, m % 2
                                pe.wait_ge(moe_copied, at(b, NM, m - RING + 1))
                                if m == RING - 1 and not first:
                                    pe.wait_ge(mixed_done, QT * b)
                                rows, cols = slice(t * P, (t + 1) * P), slice(512 * half, 512 * half + 512)
                                parts = [(xa[:, k, rows], wa[:, kind * KT + k, cols]) for k in range(KT) for xa, wa in ((xh, wh), (xh, wl), (xl, wh))]
                                for n, (xa, wa) in enumerate(parts):
                                    last = nc.tensor.matmul(banks[m % RING][:], xa, wa, start=(n == 0), stop=(n == len(parts) - 1))
                                last.then_inc(moe_ready, 1)

                        def attend(b):
                            wait_reduced(pe, b, 3 * QT)
                            pe.wait_ge(L.y_added, QT * b)
                            for kind, item in ((1, 3), (0, 4)):
                                e = item % 2
                                pe.wait_ge(L.item_copied[e], at(b, L.per[e], item // 2))
                                apart(pe, L.passed["pe"])
                                for t in range(QT):
                                    last = nc.tensor.transpose(L.J[e][0:d, t * P:(t + 1) * P], qkv[:, kind * QT + t, :], L.ident)
                                last.then_inc(L.item_ready[e], 1)
                            wait_items_copied(pe, L, b, 4)
                            pe.wait_ge(L.item_copied[1], at(b, 2, 2))
                            pe_attention(nc, pe, L, b)
                            pe.wait_ge(L.z_copied, b + 1)
                            apart(pe, L.passed["pe"])
                            for t in range(QT):
                                last = nc.tensor.transpose(L.Z[:, d * t:d * t + d], L.zT[0:d, 0, t * P:(t + 1) * P], L.ident[0:d, 0:d])
                            last.then_inc(zt_ready, 1)

                        def output(b, more):
                            pe.wait_ge(mixed_done, QT * (b + 1))
                            pe.wait_ge(L.item_copied[0], 3 * (b + 1) + 2 * more)
                            pe.wait_ge(L.item_copied[1], 2 * (b + 1) + more)
                            for c in range(8):
                                pe.wait_ge(mix_copied[c % 2], at(b, 4, c // 2))
                                for t in range(QT):
                                    last = nc.tensor.transpose(L.J[c % 2][:, t * P:(t + 1) * P], mixed[:, t, c * P:(c + 1) * P], L.ident)
                                last.then_inc(mix_ready[c % 2], 1)
                            for e in range(2):
                                pe.wait_ge(mix_copied[e], at(b, 4, 4))
                            pe_output(nc, pe, L, b, L.mixT, [w["l0f_wo"][:, c, :] for c in range(8)])

                        project(0, True)
                        with nc.Fori(0, NB - 1, engines=[ET.PE]) as b:
                            attend(b)
                            project(b + 1, False)
                            output(b, 1)
                        attend(NB - 1)
                        output(NB - 1, 0)

                    def copy_mixed(eng, e, b):
                        for c in range(e, 8, 2):
                            eng.wait_ge(mix_ready[e], at(b, 4, c // 2 + 1))
                            scale_copy(nc, e, L.mixT[:, c, :], L.J[e], 1.0).then_inc(mix_copied[e], 1)

                    @block.scalar
                    def _(act):
                        wait_weights(act, l)
                        nc.scalar.activation(sigmoid, w["l0f_gates"], ACT.Exp, scale=-1.0).then_inc(exp_gates_done, 1)
                        for i in range(3 * KT):
                            nc.scalar.activation(wh[:, i, :], whole[:, i, :], ACT.Copy).then_inc(weights_high, 1)

                        def project(b):
                            act.wait_ge(L.tokens_loaded, 16 * (b + 1))
                            act.wait_ge(length_ready, b)
                            for t in range(QT):
                                act.wait_ge(lengths_done, at(b, QT, t))
                                nc.scalar.activation(square, L.tokens[:, t, :], ACT.Square, accum_out=length2[:, t:t + 1]).then_inc(lengths_done, 1)
                            copy_transposed(nc, act, L, b, 0)
                            for k in range(KT):
                                act.wait_ge(L.item_copied[k], at(b, L.per[k], 1))
                                nc.scalar.activation(xh[:, k, :], L.xT[:, k, :], ACT.Copy).then_inc(xh_ready, 1)
                            wait_item(act, L, b, 2)
                            nc.scalar.activation(raw, L.J[0][:, 0:QT * E].rearrange("p (t e) -> p t e", t=QT), ACT.Copy).then_inc(L.item_copied[0], 1)
                            act.wait_ge(shifted_ready, b + 1)
                            nc.scalar.activation(exps, shifted, ACT.Exp).then_inc(exps_ready, 1)

                        def attend(b):
                            wait_item(act, L, b, 4)
                            scale_copy(nc, 0, L.qT[0:d], L.J[0][0:d], d ** -0.5).then_inc(L.item_copied[0], 1)
                            act_attention(nc, act, L, b)

                        project(0)
                        with nc.Fori(0, NB - 1, engines=[ET.Activation]) as b:
                            attend(b)
                            project(b + 1)
                            copy_mixed(act, 0, b)
                        attend(NB - 1)
                        copy_mixed(act, 0, NB - 1)

                    @block.vector
                    def _(dve):
                        dve.wait_ge(consts_loaded, 32)
                        wait_weights(dve, l)
                        setup = [0]

                        def setup_do(ins):
                            setup[0] += 1
                            ins.then_inc(setup_step, 1)
                            dve.wait_ge(setup_step, setup[0])

                        dve.wait_ge(exp_gates_done, 1)
                        setup_do(nc.vector.tensor_scalar(sigmoid, sigmoid, 1.0, None, ALU.add))
                        setup_do(nc.vector.reciprocal(sigmoid, sigmoid))
                        dve.wait_ge(norm2_ready, 1)
                        nc.vector.tensor_copy(sim_norm, L.Z[:, 0:E]).then_inc(norm2_ready, 1)
                        dve.wait_ge(norm_done, 1)
                        setup_do(nc.vector.tensor_scalar(sim_norm, sim_norm, 1e-12, None, ALU.max))
                        setup_do(nc.vector.reciprocal(sim_inverse, sim_norm))
                        nc.vector.tensor_tensor(sim_unit, w["l0f_sim"], sim_inverse.unsqueeze(1).broadcast_to([P, KT, E]), ALU.mult).then_inc(sim_ready, 1)

                        def project(b):
                            copy_transposed(nc, dve, L, b, 1)
                            for k in range(KT):
                                dve.wait_ge(xh_ready, at(b, KT, k + 1))
                                nc.vector.tensor_tensor(xl[:, k, :], L.xT[:, k, :], xh[:, k, :].bitcast(F32), ALU.subtract).then_inc(xl_ready, 1)
                            steps = [0]

                            def step(ins):
                                steps[0] += 1
                                ins.then_inc(route_step, 1)
                                dve.wait_ge(route_step, at(b, STEPS, steps[0]))
                                apart(dve, L.passed["dve"])

                            dve.wait_ge(length_ready, b + 1)
                            step(nc.vector.tensor_scalar(length, length, 1e-12, None, ALU.max))
                            step(nc.vector.reciprocal(inv_length, length))
                            dve.wait_ge(L.item_copied[0], at(b, 3, 2))
                            for t in range(QT):
                                step(nc.vector.scalar_tensor_tensor(logits[:, t, :], raw[:, t, :], inv_length[:, t:t + 1], sigmoid, ALU.mult, ALU.subtract))
                            for t in range(QT):
                                step(nc.vector.max(top[:, t, :], logits[:, t, :]))
                            for t in range(QT):
                                step(nc.vector.max_index(index[:, t, :], top[:, t, :], logits[:, t, :]))
                            step(nc.vector.tensor_scalar(active, logits, 0.0, None, ALU.is_gt))
                            step(nc.vector.tensor_scalar(gated, logits, 0.0, None, ALU.max))
                            step(nc.vector.tensor_scalar(peak, top[:, :, 0], 0.0, None, ALU.max))
                            nc.vector.tensor_tensor(shifted, gated, peak.unsqueeze(2).broadcast_to([P, QT, E]), ALU.subtract).then_inc(shifted_ready, 1)
                            step(nc.vector.tensor_scalar(idle, top[:, :, 0], 0.0, None, ALU.is_le))
                            step(nc.vector.tensor_copy(index_f, index))
                            ids = iota[:, 0:E].unsqueeze(1).broadcast_to([P, QT, E])
                            step(nc.vector.tensor_tensor(fallback, ids, index_f[:, :, 0:1].broadcast_to([P, QT, E]), ALU.is_equal))
                            step(nc.vector.tensor_tensor(fallback2, ids, index_f[:, :, 1:2].broadcast_to([P, QT, E]), ALU.is_equal))
                            step(nc.vector.tensor_tensor(fallback, fallback, fallback2, ALU.add))
                            step(nc.vector.tensor_tensor(fallback, fallback, idle.unsqueeze(2).broadcast_to([P, QT, E]), ALU.mult))
                            step(nc.vector.tensor_tensor(active, active, fallback, ALU.add))
                            dve.wait_ge(exps_ready, b + 1)
                            step(nc.vector.tensor_tensor(masked, exps, active, ALU.mult))
                            step(nc.vector.tensor_reduce(total, masked, AX, ALU.add))
                            step(nc.vector.reciprocal(inverse, total))
                            step(nc.vector.tensor_tensor(weights_, masked, inverse.unsqueeze(2).broadcast_to([P, QT, E]), ALU.mult))
                            assert steps[0] == STEPS, steps[0]
                            for m in range(NM):
                                t, kind, half = m // 6, m // 2 % 3, m % 2
                                dve.wait_ge(moe_ready, at(b, NM, m + 1))
                                wait_reduced(dve, b, max(m // 2 - 2, 0))
                                part = product[m // 2 % 3][:, 8 * half:8 * half + 8, :]
                                nc.vector.tensor_tensor(part, banks[m % RING][:].rearrange("p (e d) -> p e d", e=8),
                                                        weights_[:, t, 8 * half:8 * half + 8].unsqueeze(2).broadcast_to([P, 8, d]), ALU.mult).then_inc(moe_copied, 1)
                                if kind == 2 and half == 1:
                                    dve.wait_ge(moe_copied, at(b, NM, m + 1))
                                    nc.vector.tensor_reduce(qkv[:, kind * QT + t, :], product[m // 2 % 3].rearrange("p e d -> p d e"), AX, ALU.add).then_inc(reduced[1], 1)

                        def attend(b):
                            wait_item(dve, L, b, 3)
                            scale_copy(nc, 1, L.kT[0:d], L.J[1][0:d], 1.0).then_inc(L.item_copied[1], 1)
                            dve_attention(nc, dve, L, b)
                            dve.wait_ge(zt_ready, b + 1)
                            for t in range(QT):
                                nc.vector.tensor_tensor(mixed[:, t, :].rearrange("p (e d) -> p e d", e=E),
                                                        L.Z[:, d * t:d * t + d].unsqueeze(1).broadcast_to([P, E, d]),
                                                        weights_[:, t, :].unsqueeze(2).broadcast_to([P, E, d]), ALU.mult).then_inc(mixed_done, 1)

                        for i in range(3 * KT):
                            dve.wait_ge(weights_high, i + 1)
                            nc.vector.tensor_tensor(wl[:, i, :], whole[:, i, :], wh[:, i, :].bitcast(F32), ALU.subtract).then_inc(weights_low, 1)
                        project(0)
                        with nc.Fori(0, NB - 1, engines=[ET.DVE]) as b:
                            attend(b)
                            project(b + 1)
                            copy_mixed(dve, 1, b)
                            dve_add(nc, dve, L, b)
                            dve_norm(nc, dve, L, b)
                        attend(NB - 1)
                        copy_mixed(dve, 1, NB - 1)
                        dve_add(nc, dve, L, NB - 1)
                        dve_norm(nc, dve, L, NB - 1)

                    @block.gpsimd
                    def _(pool):
                        nc.gpsimd.memset(ones, 1.0).then_inc(L.pads_zeroed, 1)
                        nc.gpsimd.memset(L.qT, 0.0).then_inc(L.pads_zeroed, 1)
                        nc.gpsimd.memset(L.kT, 0.0).then_inc(L.pads_zeroed, 1)
                        nc.gpsimd.memset(halves, 0.5).then_inc(L.pads_zeroed, 1)
                        wait_weights(pool, l)
                        nc.gpsimd.tensor_tensor(sim_square, w["l0f_sim"], w["l0f_sim"], ALU.mult).then_inc(squared, 1)
                        pool.wait_ge(L.pads_zeroed, 4)
                        pool.wait_ge(norm2_ready, 2)
                        nc.gpsimd.tensor_tensor(sim_norm, sim_norm, halves, ALU.pow).then_inc(norm_done, 1)

                        def lengths(b):
                            pool.wait_ge(lengths_done, QT * (b + 1))
                            nc.gpsimd.tensor_tensor(length, length2, halves[:, 0:QT], ALU.pow).then_inc(length_ready, 1)

                        def reduces(b):
                            for t, kind in ((t, kind) for t in range(QT) for kind in range(2)):
                                n = 3 * t + kind
                                pool.wait_ge(moe_copied, at(b, NM, 2 * n + 2))
                                part, half = product[n % 3], E // 2
                                while half > 1:
                                    nc.gpsimd.tensor_tensor(part[:, 0:half, :], part[:, 0:half, :], part[:, half:2 * half, :], ALU.add).then_inc(halved, 1)
                                    half //= 2
                                    pool.wait_ge(halved, at(b, 6 * QT, 3 * (2 * t + kind) + {4: 1, 2: 2, 1: 3}[half]))
                                nc.gpsimd.tensor_tensor(qkv[:, kind * QT + t, :], part[:, 0, :], part[:, 1, :], ALU.add).then_inc(reduced[0], 1)

                        lengths(0)
                        reduces(0)
                        with nc.Fori(0, NB - 1, engines=[ET.Pool]) as b:
                            pool_attention(nc, pool, L, b)
                            lengths(b + 1)
                            reduces(b + 1)
                            pool_rstd(nc, pool, L, b)
                        pool_attention(nc, pool, L, NB - 1)
                        pool_rstd(nc, pool, L, NB - 1)

        def windowed_attention(l):
            w = W[l]
            H, d, NA, NT, NP = 16, 16, 14, 8, 6
            FIT = QT
            DOT_LAG, CORR_LAG, EXP_LAG = 4, 5, 12
            TURN_LAG, COPY_LAG, VALUE_LAG = EXP_LAG + 3, EXP_LAG + 5, EXP_LAG + 7
            
            U = QT * H
            with nc.cleanup_on_exit():
                L = common(l, [7, 6], w["l1a_bo"].unsqueeze(1).broadcast_to([P, QT, D]))
                sem = L.sem
                take = carve(nc.alloc_sbuf_tensor(f"arena_{l}", [P, ARENA], F32))
                L.eT, L.ez, L.v, L.zT = take(2, T), take(H, T), take(QT, 32 * H), take(4, T)
                probs, probsT, tanhs, LT = take(NP, 2 * P), take(2, QT * 2 * P), take(NT, 2 * P), take(T)
                g, unit, ones = take(QT, D), take(QT, D), take(P)
                norm2, ln_norm2, inv_norm, newton, half_ln = (take(U) for _ in range(5))
                rowsum, inv_denom, fit, sums, rinv = (take(U) for _ in range(5))
                denom_sum, denom_inv = take(FIT // QT), take(FIT // QT)
                corr = take_rest_of_odd(NA, 2 * P)
                S, LB, TB, Z, stat = [banks[0][:], banks[1][:]], [banks[2][:], banks[6][:]], [banks[3][:], banks[4][:]], banks[5][:], banks[7][:, 0:FIT]
                zeroed, squared, norm2_ready, floor_ready, ln_ready, guess_ready, half_ready, unit_ready, chain = (
                    sem(n) for n in ("zeroed", "squared", "norm2_ready", "floor_ready", "ln_ready", "guess_ready", "half_ready", "unit_ready", "chain"))
                lb_ready, dot_ready, tanh_done, tanh_masked, corr_done, corr_masked, inv_ready, stat_ready, fit_ready, stat_step = (
                    sem(n) for n in ("lb_ready", "dot_ready", "tanh_done", "tanh_masked", "corr_done", "corr_masked", "inv_ready", "stat_ready", "fit_ready", "stat_step"))
                exp_done, rinv_ready, probs_ready, probsT_ready, probsT_copied, values_done, z_copied = (
                    sem(n) for n in ("exp_done", "rinv_ready", "probs_ready", "probsT_ready", "probsT_copied", "values_done", "z_copied"))

                def first_col(u):
                    return P if u % QT == 0 else 0

                with nc.Block() as block:
                    @block.sync
                    def _(sp):
                        sp_stream(nc, sp, L, NB)

                    @block.tensor
                    def _(pe):
                        wait_weights(pe, l)
                        pe.wait_ge(zeroed, 3)

                        def project(b, first):
                            pe_transpose_tokens(nc, pe, L, b, first)
                            wait_items_copied(pe, L, b, 1)
                            for t in range(QT):
                                for j, wt in enumerate((w["l1a_wv"], w["l1a_wg"])):
                                    pe_item(nc, pe, L, b, 2 + 2 * t + j, L.J[j][:, 0:D], [(L.xT[:, k, t * P:(t + 1) * P], wt[:, k, :]) for k in range(KT)])

                        def turn(b):
                            pe.wait_ge(unit_ready, b + 1)
                            pe.wait_ge(L.y_added, QT * b)
                            for c in range(2):
                                pe.wait_ge(L.item_copied[c], at(b, L.per[c], 5))
                                for t in range(QT):
                                    last = nc.tensor.transpose(L.J[c][:, t * P:(t + 1) * P], unit[:, t, c * P:(c + 1) * P], L.ident)
                                last.then_inc(L.item_ready[c], 1)
                            pe.wait_ge(L.item_copied[0], at(b, 7, 6))
                            pe.wait_ge(half_ready, b + 1)
                            apart(pe, L.passed["pe"])
                            for t in range(QT):
                                last = nc.tensor.transpose(L.J[0][0:H, t * P:(t + 1) * P], half_ln[:, H * t:H * t + H], L.ident)
                            last.then_inc(L.item_ready[0], 1)

                        def attend(b):
                            wait_items_copied(pe, L, b, 12)

                            def log_norms(h):
                                pe.wait_ge(tanh_done, at(b, U, QT * (h - 1)))
                                nc.tensor.matmul(LB[h % 2], w["l1a_head_rows"][:, h, :], LT, start=True, stop=True).then_inc(lb_ready, 1)

                            def dots(u):
                                h, qt = divmod(u, QT)
                                c0 = first_col(u)
                                pe.wait_ge(corr_done, at(b, U, u - 1))
                                nc.tensor.matmul(S[u % 2][:, c0:2 * P], L.eT[:, h // 8, qt * P:(qt + 1) * P],
                                                 L.ez[:, h, (qt - 1) * P + c0:(qt + 1) * P], start=True, stop=True).then_inc(dot_ready, 1)

                            def transposes(u):
                                pe.wait_ge(probs_ready, at(b, U, u + 1))
                                pe.wait_ge(probsT_copied, at(b, U // 2, u // 2 - 1))
                                for c in range(first_col(u), 2 * P, P):
                                    x = u % 2 * 2 * P + c
                                    last = nc.tensor.transpose(TB[u // 2 % 2][:, x:x + P], probs[:, u % NP, c:c + P], L.ident)
                                last.then_inc(probsT_ready, 1)

                            def values(h):
                                pe.wait_ge(probsT_copied, at(b, U // 2, 2 * h + 2))
                                j = h % 4
                                if j == 0:
                                    pe.wait_ge(z_copied, at(b, 4, h // 4))
                                for k in range(QT):
                                    n = min(2 * P, T - k * P)
                                    last = nc.tensor.matmul(Z[32 * j:32 * j + 32, k * P:k * P + n], L.v[:, k, 32 * h:32 * h + 32],
                                                            probsT[:, h % 2, 2 * P * k:2 * P * k + n], start=(k == 0), stop=(k == QT - 1), skip_group_check=True)
                                last.then_inc(values_done, 1)

                            log_norms(0)
                            for s in range(U + VALUE_LAG):
                                if s % QT == 0 and s // QT + 1 < H:
                                    log_norms(s // QT + 1)
                                if 0 <= s - DOT_LAG < U:
                                    dots(s - DOT_LAG)
                                v = s - DOT_LAG - 2
                                if v % FIT == 0 and FIT <= v <= U:
                                    n = v // FIT - 1
                                    pe.wait_ge(inv_ready, at(b, U // FIT, n + 1))
                                    nc.tensor.matmul(stat, ones, inv_denom[:, FIT * n:FIT * n + FIT], start=True, stop=True).then_inc(stat_ready, 1)
                                v = s - TURN_LAG
                                if 0 <= v < U:
                                    transposes(v)
                                v = s - VALUE_LAG
                                if v >= 0 and v % QT == QT - 1 and v < U:
                                    values(v // QT)

                        def output(b, more):
                            pe.wait_ge(z_copied, at(b, 4, 4))
                            pe.wait_ge(L.item_copied[0], 7 * (b + 1) + 5 * more)
                            pe.wait_ge(L.item_copied[1], 6 * (b + 1) + 5 * more)
                            pe_output(nc, pe, L, b, L.zT, [w["l1a_wo"][:, c, :] for c in range(4)])

                        project(0, True)
                        turn(0)
                        with nc.Fori(0, NB - 1, engines=[ET.PE]) as b:
                            attend(b)
                            project(b + 1, False)
                            output(b, 1)
                            turn(b + 1)
                        attend(NB - 1)
                        output(NB - 1, 0)

                    def copy_units(eng, e, b):
                        wait_item(eng, L, b, 10 + e)
                        scale_copy(nc, e, L.eT[:, e, :], L.J[e], 1.0)
                        for j in range(8):
                            last = scale_copy(nc, e, L.ez[:, 8 * e + j, :], L.J[e], head_mask[:, j:j + 1])
                        last.then_inc(L.item_copied[e], 1)

                    @block.scalar
                    def _(act):
                        act.wait_ge(consts_loaded, 32)
                        act.wait_ge(zeroed, 3)

                        def project(b):
                            copy_transposed(nc, act, L, b, 0)
                            for t in range(QT):
                                wait_item(act, L, b, 2 + 2 * t)
                                scale_copy(nc, 0, L.v[:, t, :].rearrange("p (h c) -> p h c", c=32)[:, :, 0:d],
                                           L.J[0][:, 0:D].rearrange("p (h c) -> p h c", c=d), 1.0).then_inc(L.item_copied[0], 1)
                            act.wait_ge(floor_ready, b + 1)
                            nc.scalar.activation(ln_norm2, norm2, ACT.Ln).then_inc(ln_ready, 1)
                            act.wait_ge(ln_ready, b + 1)
                            nc.scalar.activation(inv_norm, ln_norm2, ACT.Exp, scale=-0.5).then_inc(guess_ready, 1)

                        def turn(b):
                            copy_units(act, 0, b)
                            wait_item(act, L, b, 12)
                            nc.scalar.activation(LT[0:H], L.J[0][0:H], ACT.Copy).then_inc(L.item_copied[0], 1)

                        def attend(b):
                            for s in range(U + COPY_LAG):
                                if s < U:
                                    h, qt = divmod(s, QT)
                                    c0 = first_col(s)
                                    act.wait_ge(lb_ready, at(b, H, h + 1))
                                    act.wait_ge(corr_done, at(b, U, s - NT + 1))
                                    nc.scalar.activation(tanhs[:, s % NT, c0:2 * P], LB[h % 2][:, (qt - 1) * P + c0:(qt + 1) * P], ACT.Tanh,
                                                         bias=half_ln[:, H * qt + h:H * qt + h + 1]).then_inc(tanh_done, 1)
                                v = s - EXP_LAG
                                if 0 <= v < U:
                                    c0 = first_col(v)
                                    act.wait_ge(fit_ready, at(b, U // FIT, v // FIT + 1))
                                    act.wait_ge(corr_masked, at(b, U // 2, v // 2 + 1))
                                    act.wait_ge(probsT_ready, at(b, U, v - NP + 1))
                                    nc.scalar.activation(probs[:, v % NP, c0:2 * P], corr[:, v % NA, c0:2 * P], ACT.Exp,
                                                         scale=fit[:, v:v + 1], accum_out=sums[:, v:v + 1]).then_inc(exp_done, 1)
                                v = s - COPY_LAG
                                if 0 <= v < U and v % 2 == 1:
                                    h, qt = divmod(v - 1, QT)
                                    c0 = first_col(v - 1)
                                    x0 = 2 * P * qt - P + c0
                                    act.wait_ge(probsT_ready, at(b, U, v + 1))
                                    act.wait_ge(values_done, at(b, H, h - 1))
                                    nc.scalar.activation(probsT[:, h % 2, x0:x0 + T - c0], TB[v // 2 % 2][:, c0:T], ACT.Copy).then_inc(probsT_copied, 1)

                        project(0)
                        turn(0)
                        with nc.Fori(0, NB - 1, engines=[ET.Activation]) as b:
                            attend(b)
                            project(b + 1)
                            turn(b + 1)
                        attend(NB - 1)

                    @block.vector
                    def _(dve):
                        wait_weights(dve, l)
                        dve.wait_ge(consts_loaded, 32)

                        def project(b):
                            copy_transposed(nc, dve, L, b, 1)
                            for t in range(QT):
                                wait_item(dve, L, b, 3 + 2 * t)
                                nc.vector.tensor_tensor(g[:, t, :], L.J[1][:, 0:D], w["l1a_bg"], ALU.add).then_inc(L.item_copied[1], 1)
                            dve.wait_ge(squared, b + 1)
                            nc.vector.tensor_reduce(norm2, unit.rearrange("p t (h c) -> p (t h) c", c=d), AX, ALU.add).then_inc(norm2_ready, 1)
                            dve.wait_ge(norm2_ready, b + 1)
                            nc.vector.tensor_scalar(norm2, norm2, 1e-36, None, ALU.max).then_inc(floor_ready, 1)

                        def units(b):
                            dve.wait_ge(guess_ready, b + 1)
                            nc.vector.tensor_tensor(newton, inv_norm, norm2, ALU.mult).then_inc(chain, 1)
                            dve.wait_ge(chain, at(b, 4, 1))
                            nc.vector.tensor_tensor(newton, newton, inv_norm, ALU.mult).then_inc(chain, 1)
                            dve.wait_ge(chain, at(b, 4, 2))
                            nc.vector.tensor_scalar(newton, newton, -0.5, 1.5, ALU.mult, ALU.add).then_inc(chain, 1)
                            dve.wait_ge(chain, at(b, 4, 3))
                            nc.vector.tensor_tensor(inv_norm, inv_norm, newton, ALU.mult).then_inc(chain, 1)
                            dve.wait_ge(chain, at(b, 4, 4))
                            nc.vector.tensor_tensor(unit.rearrange("p t (h c) -> p (t h) c", c=d), g.rearrange("p t (h c) -> p (t h) c", c=d),
                                                    inv_norm.unsqueeze(2).broadcast_to([P, U, d]), ALU.mult).then_inc(unit_ready, 1)
                            nc.vector.tensor_scalar(half_ln, ln_norm2, 0.25, 0.25 * math.log(1e8), ALU.mult, ALU.add).then_inc(half_ready, 1)

                        def attend(b, norm_row=None):
                            def stats(n):
                                part = inv_denom[:, FIT * n:FIT * n + FIT]
                                dve.wait_ge(corr_done, at(b, U, FIT * n + FIT))
                                nc.vector.tensor_scalar(part, rowsum[:, FIT * n:FIT * n + FIT], 1.0 / (4 * T), 1.0, ALU.mult, ALU.add).then_inc(stat_step, 1)
                                dve.wait_ge(stat_step, at(b, 3 * U // FIT, 3 * n + 1))
                                nc.vector.reciprocal(part, part).then_inc(inv_ready, 1)

                            def fitness(n):
                                dve.wait_ge(stat_ready, at(b, U // FIT, n + 1))
                                nc.vector.tensor_reduce(denom_sum, stat.rearrange("p (h q) -> p h q", q=QT), AX, ALU.add).then_inc(stat_step, 1)
                                dve.wait_ge(stat_step, at(b, 3 * U // FIT, 3 * n + 2))
                                nc.vector.reciprocal(denom_inv, denom_sum).then_inc(stat_step, 1)
                                dve.wait_ge(stat_step, at(b, 3 * U // FIT, 3 * n + 3))
                                nc.vector.scalar_tensor_tensor(fit[:, FIT * n:FIT * n + FIT].rearrange("p (h q) -> p h q", q=QT),
                                                               inv_denom[:, FIT * n:FIT * n + FIT].rearrange("p (h q) -> p h q", q=QT), 0.25,
                                                               denom_inv.unsqueeze(2).broadcast_to([P, FIT // QT, QT]), ALU.mult, ALU.mult).then_inc(fit_ready, 1)

                            for s in range(U + VALUE_LAG + 2):
                                if norm_row is not None and s == 8:
                                    dve_moments(nc, dve, L, norm_row)
                                if norm_row is not None and s == 18:
                                    dve_result(nc, dve, L, norm_row)
                                u = s - DOT_LAG
                                if 0 <= u < U:
                                    c0 = first_col(u)
                                    dve.wait_ge(dot_ready, at(b, U, u + 1))
                                    dve.wait_ge(tanh_masked, at(b, U // 2, u // 2 + 1))
                                    dve.wait_ge(exp_done, at(b, U, u - NA + 1))
                                    nc.vector.scalar_tensor_tensor(corr[:, u % NA, c0:2 * P], tanhs[:, u % NT, c0:2 * P], 1.0, S[u % 2][:, c0:2 * P],
                                                                   ALU.add, ALU.mult, accum_out=rowsum[:, u:u + 1]).then_inc(corr_done, 1)
                                    if u % FIT == FIT - 1:
                                        stats(u // FIT)
                                v = s - DOT_LAG - 2
                                if v % FIT == 0 and FIT <= v <= U:
                                    fitness(v // FIT - 1)
                                v = s - EXP_LAG - 1
                                if 0 <= v < U:
                                    c0 = first_col(v)
                                    dve.wait_ge(exp_done, at(b, U, v + 1))
                                    nc.vector.reciprocal(rinv[:, v:v + 1], sums[:, v:v + 1]).then_inc(rinv_ready, 1)
                                    dve.wait_ge(rinv_ready, at(b, U, v + 1))
                                    pr = probs[:, v % NP, c0:2 * P]
                                    nc.vector.tensor_scalar(pr, pr, rinv[:, v:v + 1], None, ALU.mult).then_inc(probs_ready, 1)
                                v = s - VALUE_LAG - 2
                                if 0 <= v < U and v % 16 == 15:
                                    n = v // 16
                                    dve.wait_ge(values_done, at(b, H, 4 * n + 4))
                                    nc.vector.tensor_scalar(L.zT[:, n, :], Z, w["l1a_bv"][:, n:n + 1], None, ALU.add).then_inc(z_copied, 1)

                        project(0)
                        units(0)
                        copy_units(dve, 1, 0)
                        attend(0)
                        with nc.Fori(0, NB - 1, engines=[ET.DVE]) as b:
                            project(b + 1)
                            dve_add(nc, dve, L, b)
                            units(b + 1)
                            copy_units(dve, 1, b + 1)
                            attend(b + 1, norm_row=b)
                        dve_add(nc, dve, L, NB - 1)
                        dve_norm(nc, dve, L, NB - 1)

                    @block.gpsimd
                    def _(pool):
                        nc.gpsimd.memset(L.v, 0.0).then_inc(zeroed, 1)
                        nc.gpsimd.memset(LT, 0.0).then_inc(zeroed, 1)
                        nc.gpsimd.memset(ones, 1.0).then_inc(zeroed, 1)
                        pool.wait_ge(zeroed, 3)
                        wait_weights(pool, l)

                        def norms(b):
                            pool.wait_ge(L.item_copied[1], at(b, 6, 5))
                            nc.gpsimd.tensor_tensor(unit, g, g, ALU.mult).then_inc(squared, 1)

                        def mask(ring, slots, u, fill):
                            i = u % slots
                            own = ring[:, i:i + 2, P:2 * P]
                            ins = nc.gpsimd.affine_select(out=own, in_=own, compare_op=ALU.is_ge, fill=fill,
                                                          base=0, pattern=[[0, 2], [-1, P]], channel_multiplier=1)
                            n = 1 if u % QT == 0 else 2
                            before = ring[:, i + 1, 0:P] if n == 1 else ring[:, i:i + 2, 0:P]
                            return nc.gpsimd.affine_select(out=before, in_=before, compare_op=ALU.is_ge, fill=fill,
                                                           base=0, pattern=[[1, P]] if n == 1 else [[0, 2], [1, P]], channel_multiplier=-1)

                        def attend(b, norm_row=None):
                            for s in range(1, U + CORR_LAG, 2):
                                if s < U:
                                    pool.wait_ge(tanh_done, at(b, U, s + 1))
                                    apart(pool, L.passed["pool"])
                                    mask(tanhs, NT, s - 1, no_tanh).then_inc(tanh_masked, 1)
                                u = s - CORR_LAG
                                if u >= 0:
                                    pool.wait_ge(corr_done, at(b, U, u + 2))
                                    apart(pool, L.passed["pool"])
                                    mask(corr, NA, u, no_prob).then_inc(corr_masked, 1)
                                if norm_row is not None and s == 15:
                                    pool_rstd(nc, pool, L, norm_row)
                                if s == U // 2 + 1:
                                    pool_bias(nc, pool, L, b)

                        no_tanh, no_prob = nc.gpsimd.to_reg(-1.0), nc.gpsimd.to_reg(-1e30)
                        norms(0)
                        attend(0)
                        with nc.Fori(0, NB - 1, engines=[ET.Pool]) as b:
                            norms(b + 1)
                            attend(b + 1, norm_row=b)
                        pool_rstd(nc, pool, L, NB - 1)

        with nc.Block() as block:
            @block.sync
            def _(sp):
                nc.sync.dma_start(consts[:, 0:a["consts"].shape[1]], a["consts"]).then_inc(consts_loaded, 16)
                nc.sync.dma_start(hbuf[:, 0, 0:P], a["future"]).then_inc(consts_loaded, 16)
                load_weights(sp, layers[0])

            @block.vector
            def _(dve):
                dve.wait_ge(consts_loaded, 32)
                nc.vector.tensor_copy(ident_bf, ident)
                nc.vector.tensor_copy(future, hbuf[:, 0, 0:P])

        for l in layers:
            if l == 0:
                wide_attention(0, 16, 8, True, False)
            if l == 1:
                wide_attention(1, 8, 8, False, True)
            if l == 2:
                mixture_attention(2)
            if l == 3:
                windowed_attention(3)
            if l == 4:
                narrow_cross_attention(4)
            if l == 5:
                before_last.close()
                gated_experts(5)
        if 5 not in layers:
            before_last.close()




def lay_out(inputs):
    import numpy as np
    i = {k: np.ascontiguousarray(v) for k, v in inputs.items()}

    def tiles(w, p=128):
        k, n = w.shape
        return np.ascontiguousarray(w.reshape(k // p, p, n).transpose(1, 0, 2).reshape(p, -1))

    def rows(v):
        return np.ascontiguousarray(np.broadcast_to(v[None, :], (128, v.shape[0])))

    order = [4 * p + r + 2 * j for p in range(4) for r in range(2) for j in range(2)]
    a = {"x": i["x"], "ctxT": np.ascontiguousarray(i["ctx_768"].transpose(0, 2, 1))}
    a["l0a_wq"] = tiles(i["L0_attn_W_Q"][:, order].reshape(256, -1))
    a["l0a_wk"] = tiles(i["L0_attn_W_K"].reshape(256, -1))
    a["l0a_wv"] = tiles(i["L0_attn_W_V"].reshape(256, -1))
    a["l0a_wo"] = tiles(np.ascontiguousarray(i["L0_attn_W_out"].transpose(1, 0, 2)[order]).reshape(1024, 256))
    a["l0a_bo"] = rows(i["L0_attn_b_out"])
    a["l0x_wq"] = tiles(i["L0_xattn_Wq"])
    a["l0x_wk"] = tiles(i["L0_xattn_Wk"], 96)
    a["l0x_wv"] = tiles(i["L0_xattn_Wv"], 96)
    a["l0x_wo"] = tiles(i["L0_xattn_Wout"])
    a["l0x_bo"] = rows(i["L0_xattn_bout"])
    pad = lambda w: np.concatenate([w.reshape(16, 16, -1), np.zeros((16, 16, w.shape[1]), w.dtype)], 1).reshape(512, -1)
    a["l1x_wq"] = tiles(i["L1_xattn_Wq"])
    a["l1x_wk"] = tiles(i["L1_xattn_Wk"], 96)
    a["l1x_wv"] = tiles(i["L1_xattn_Wv"], 96)
    a["l1x_w1"] = tiles(pad(i["L1_xattn_W1"]))
    a["l1x_w2"] = tiles(i["L1_xattn_W2"])
    places = np.zeros((128, 4, 4, 128), np.float32)
    for pair in range(4):
        for odd in range(2):
            for r in range(4):
                for j in range(16):
                    p, m = 32 * pair + 16 * odd + j, 64 * odd + 16 * r + j
                    places[p, r % 2, pair, m] = 1
                    places[p, 2 + r // 2, pair, m] = 1
    a["l1x_places"] = places.reshape(128, -1)
    a["l1x_bq"] = np.ascontiguousarray(i["L1_xattn_bq"].reshape(2, 128).T)
    a["l1x_bk"] = np.ascontiguousarray(i["L1_xattn_bk"].reshape(2, 128).T)
    padcol = lambda v: np.ascontiguousarray(np.concatenate([v.reshape(16, 16), np.zeros((16, 16), v.dtype)], 1).reshape(4, 128).T)
    a["l1x_bv"] = padcol(i["L1_xattn_bv"])
    a["l1x_b1"] = np.ascontiguousarray(i["L1_xattn_b1"].reshape(4, 128).T)
    a["l1x_b2"] = rows(i["L1_xattn_b2"])
    qkv = [i["L0_ffn_" + n].transpose(1, 0, 2).reshape(256, 1024) for n in ("q_proj", "k_proj", "v_proj")]
    a["l0f_wqkv"] = np.ascontiguousarray(np.concatenate([tiles(m) for m in qkv], 1))
    a["l0f_wo"] = tiles(i["L0_ffn_o_proj"].reshape(1024, 256))
    a["l0f_sim"] = tiles(i["L0_ffn_sim_matrix"])
    a["l0f_gates"] = rows(i["L0_ffn_gates"])
    a["l1a_wg"] = tiles(np.ascontiguousarray(i["L1_attn_Wg"].T))
    a["l1a_wv"] = tiles(np.ascontiguousarray(i["L1_attn_Wv"].T))
    a["l1a_wo"] = tiles(pad(np.ascontiguousarray(i["L1_attn_Wo"].T)))
    a["l1a_bg"] = rows(i["L1_attn_bg"])
    a["l1a_bv"] = padcol(i["L1_attn_bv"])
    a["l1a_bo"] = rows(i["L1_attn_bo"])
    sel = np.zeros((128, 16, 128), np.float32)
    for h in range(16):
        sel[h, h, :] = 1
    a["l1a_head_rows"] = sel.reshape(128, -1)
    W1, Ws1 = i["L1_ffn_W1"], i["L1_ffn_Ws1"]
    down = np.concatenate([i["L1_ffn_W2"].transpose(0, 2, 1).reshape(-1, 256), i["L1_ffn_Ws2"].T], 0)
    a["l1f_wy"] = tiles(np.ascontiguousarray(np.concatenate([W1[:, :192].reshape(-1, 256), Ws1[:384]], 0).T))
    a["l1f_wg"] = tiles(np.ascontiguousarray(np.concatenate([W1[:, 192:].reshape(-1, 256), Ws1[384:]], 0).T))
    a["l1f_w2"] = tiles(np.ascontiguousarray(down))
    a["l1f_gate"] = tiles(np.ascontiguousarray(i["L1_ffn_gate_w"].T))
    sel = np.zeros((128, 12 * 128), np.float32)
    m = np.arange(12 * 128)
    sel[m // 192, m] = 1
    sel[32 + m // 192, m] = 1
    a["l1f_expert_rows"] = sel
    c = np.zeros((128, 158), np.float32)
    r = np.arange(128)
    c[r, r] = 1
    for j in range(2):
        c[64 * j:64 * j + 64, 128 + j] = 1
    for j in range(8):
        c[16 * j:16 * j + 16, 130 + j] = 1
    c[:, 138:142] = -0.5
    c[:, 142:158] = np.arange(16)
    a["consts"] = c
    a["future"] = np.where(r[None, :] > r[:, None], -1e30, 0).astype(np.float32)
    return a




def kernel(**inputs):
    import numpy as _np
    import concourse.bacc as _bacc
    from concourse import mybir as _mybir
    from concourse.bass_utils import run_bass_kernel_spmd as _run

    nc = _bacc.Bacc("TRN2", target_bir_lowering=False, num_devices=1)
    arrays, aps = {}, {}
    for name, a in lay_out(inputs).items():
        arrays[f"in_{name}_dram"] = a
        aps[name] = nc.dram_tensor(f"in_{name}_dram", a.shape, _mybir.dt.from_np(a.dtype), kind="ExternalInput").ap()
    shape = inputs["x"].shape
    out = nc.dram_tensor("out_0_dram", shape, _mybir.dt.float32, kind="ExternalOutput").ap()
    build(nc, aps, out)
    r = _run(nc, [arrays], core_ids=[0])
    return _np.asarray(r.results[0]["out_0_dram"])
```
